# Optimizing a Trainium2 kernel written in Bass

```python
import numpy as np
import jax
import jax.numpy as jnp

def _softmax(x, axis=-1):
    return jax.nn.softmax(x, axis=axis)

def _gelu(x):
    return jax.nn.gelu(x, approximate=True)

def _silu(x):
    return jax.nn.silu(x)

def _sigmoid(x):
    return jax.nn.sigmoid(x)

def _layernorm(x, axis=-1, eps=1e-05):
    m = jnp.mean(x, axis=axis, keepdims=True)
    v = jnp.var(x, axis=axis, keepdims=True)
    return (x - m) / jnp.sqrt(v + eps)

def _scatter_add(tgt, idx, src, axis=0):
    return tgt.at[idx].add(src)

def _segment_sum(src, seg, n):
    return jax.ops.segment_sum(src, seg, n)
kernel_name = 'mk_adaln_d1_jaxref_r4_333435'

def setup_inputs(seed: int=0):
    np.random.seed(seed)
    _w = jnp.asarray

    def _L0_attn_setup():
        import math
        import jax, jax.numpy as jnp
        import numpy as np
        PI = math.pi
        PHI = (1 + math.sqrt(5)) / 2
        B, T, D, H = (4, 256, 256, 16)
        DH = D // H

        def _chamber_beta_init(n_heads, layer_depth=0.5):
            lo = layer_depth * 0.5
            hi = 0.5 + layer_depth * 0.5
            frac = np.arange(n_heads) / max(n_heads - 1, 1)
            depth = lo + frac * (hi - lo)
            return (0.5 + 0.2 * (1.0 - 2.0 * depth)).astype(np.float32)
        key = jax.random.key(seed)
        ks = jax.random.split(key, 10)
        s = 0.02
        x = jax.random.normal(ks[0], (B, T, D), dtype=jnp.float32)
        Wa = jax.random.normal(ks[1], (D, H), jnp.float32) * s
        ba = jnp.zeros((H,), jnp.float32)
        We = jax.random.normal(ks[2], (D, H), jnp.float32) * s
        be = jnp.zeros((H,), jnp.float32)
        Wi = jax.random.normal(ks[3], (D, D), jnp.float32) * s
        Wo = jax.random.normal(ks[4], (D, D), jnp.float32) * s
        Wv = jax.random.normal(ks[5], (D, D), jnp.float32) * s
        Wout = jax.random.normal(ks[6], (D, D), jnp.float32) * s
        chi = jnp.ones((H,), jnp.float32)
        beta_p = jnp.asarray(_chamber_beta_init(H))
        iv_p = jnp.full((H,), 0.5, jnp.float32)
        ov_p = jnp.full((H,), 0.5, jnp.float32)
        return {'x': x, 'Wa': Wa, 'ba': ba, 'We': We, 'be': be, 'Wi': Wi, 'Wo': Wo, 'Wv': Wv, 'Wout': Wout, 'chi': chi, 'beta_p': beta_p, 'iv_p': iv_p, 'ov_p': ov_p}
    _L0_attn_in = _L0_attn_setup()

    def _L0_ffn_setup():
        import jax, jax.numpy as jnp
        import numpy as np
        DIM = 256
        DEPTH = 2
        HEADS = 8
        DIM_HEAD = 64
        WINDOW = 128
        INNER = HEADS * DIM_HEAD
        HID = int(DIM * 4 * 2 / 3)
        B, N = (2, 2048)
        QK_SCALE = 8.0

        def shift_token(t):
            t1, t2 = jnp.split(t, 2, axis=-1)
            t2 = jnp.pad(t2, ((0, 0), (1, 0), (0, 0)))[:, :-1]
            return jnp.concatenate([t1, t2], axis=-1)

        def l2norm(t):
            return t / jnp.clip(jnp.linalg.norm(t, axis=-1, keepdims=True), 1e-12)

        def rotate_half(x):
            x1, x2 = jnp.split(x, 2, axis=-1)
            return jnp.concatenate([-x2, x1], axis=-1)

        def rotary_xpos(q, k):
            n = q.shape[-2]
            half_idx = jnp.arange(0, DIM_HEAD, 2, dtype=jnp.float32)
            inv_freq = 1.0 / 10000.0 ** (half_idx / DIM_HEAD)
            t = jnp.arange(n, dtype=jnp.float32)
            freqs = t[:, None] * inv_freq[None, :]
            freqs = jnp.concatenate([freqs, freqs], axis=-1)
            base = (half_idx + 0.4 * DIM_HEAD) / (1.4 * DIM_HEAD)
            power = (t - n // 2) / float(WINDOW // 2)
            scale = base[None, :] ** power[:, None]
            scale = jnp.concatenate([scale, scale], axis=-1)
            cos, sin = (jnp.cos(freqs), jnp.sin(freqs))
            q = q * cos * scale + rotate_half(q) * sin * scale
            k = k * cos / scale + rotate_half(k) * sin / scale
            return (q, k)

        def local_attention(q, k, v):
            b, h, n, d = q.shape
            w = n // WINDOW
            bq = q.reshape(b, h, w, WINDOW, d) * QK_SCALE
            bk = k.reshape(b, h, w, WINDOW, d)
            bv = v.reshape(b, h, w, WINDOW, d)

            def look_around(t):
                p = jnp.pad(t, ((0, 0), (0, 0), (1, 0), (0, 0), (0, 0)))
                return jnp.concatenate([p[:, :, :w], p[:, :, 1:]], axis=3)
            bk, bv = (look_around(bk), look_around(bv))
            bt = jnp.arange(n).reshape(w, WINDOW)
            btp = jnp.pad(bt, ((1, 0), (0, 0)), constant_values=-1)
            btk = jnp.concatenate([btp[:w], btp[1:]], axis=1)
            sim = jnp.einsum('bhwid,bhwjd->bhwij', bq, bk)
            i = bt[:, :, None]
            j = btk[:, None, :]
            mask = (i < j) | (i > j + WINDOW) | (j == -1)
            sim = jnp.where(mask, -jnp.finfo(sim.dtype).max, sim)
            attn = jax.nn.softmax(sim, axis=-1)
            out = jnp.einsum('bhwij,bhwjd->bhwid', attn, bv)
            return out.reshape(b, h, n, d)

        def _layer(x, wqkv, qs, ksc, wo, lg, lb, w1, b1, w2, b2):
            b, n, _ = x.shape
            h = shift_token(x)
            qkv = h @ wqkv
            q, k, v = jnp.split(qkv, 3, axis=-1)
            to_heads = lambda t: t.reshape(b, n, HEADS, DIM_HEAD).transpose(0, 2, 1, 3)
            q, k, v = (to_heads(q), to_heads(k), to_heads(v))
            q = l2norm(q) * qs
            k = l2norm(k) * ksc
            q, k = rotary_xpos(q, k)
            o = local_attention(q, k, v)
            o = o.transpose(0, 2, 1, 3).reshape(b, n, INNER)
            x = x + o @ wo
            h = shift_token(x)
            mu = h.mean(-1, keepdims=True)
            var = h.var(-1, keepdims=True)
            h = (h - mu) / jnp.sqrt(var + 1e-05) * lg + lb
            h = h @ w1 + b1
            a, g = jnp.split(h, 2, axis=-1)
            h = a * jax.nn.gelu(g, approximate=False)
            x = x + h @ w2 + b2
            return x
        key = jax.random.key(seed)
        ks = jax.random.split(key, 6)
        return {'x': jax.random.normal(ks[0], (B, N, DIM), jnp.float32), 'wqkv': jax.random.normal(ks[1], (DEPTH, DIM, 3 * INNER), jnp.float32) * 0.02, 'q_scale': jnp.ones((DEPTH, DIM_HEAD), jnp.float32), 'k_scale': jnp.ones((DEPTH, DIM_HEAD), jnp.float32), 'wo': jax.random.normal(ks[2], (DEPTH, INNER, DIM), jnp.float32) * 0.02, 'ln_g': jnp.ones((DEPTH, DIM), jnp.float32), 'ln_b': jnp.zeros((DEPTH, DIM), jnp.float32), 'w1': jax.random.normal(ks[3], (DEPTH, DIM, 2 * HID), jnp.float32) * 0.02, 'b1': jnp.zeros((DEPTH, 2 * HID), jnp.float32), 'w2': jax.random.normal(ks[4], (DEPTH, HID, DIM), jnp.float32) * 0.02, 'b2': jnp.zeros((DEPTH, DIM), jnp.float32)}
    _L0_ffn_in = _L0_ffn_setup()
    _L0_c = _w((lambda *s: np.random.randn(*s).astype(np.float32) * 0.05)(8, 256))
    _L0_wmod = _w((lambda *s: np.random.randn(*s).astype(np.float32) * 0.05)(256, 6 * 256) * 256 ** (-0.5))
    _d = {'L0_attn_x': _L0_attn_in['x'], 'L0_attn_Wa': _L0_attn_in['Wa'], 'L0_attn_ba': _L0_attn_in['ba'], 'L0_attn_We': _L0_attn_in['We'], 'L0_attn_be': _L0_attn_in['be'], 'L0_attn_Wi': _L0_attn_in['Wi'], 'L0_attn_Wo': _L0_attn_in['Wo'], 'L0_attn_Wv': _L0_attn_in['Wv'], 'L0_attn_Wout': _L0_attn_in['Wout'], 'L0_attn_chi': _L0_attn_in['chi'], 'L0_attn_beta_p': _L0_attn_in['beta_p'], 'L0_attn_iv_p': _L0_attn_in['iv_p'], 'L0_attn_ov_p': _L0_attn_in['ov_p'], 'L0_ffn_wqkv': _L0_ffn_in['wqkv'], 'L0_ffn_q_scale': _L0_ffn_in['q_scale'], 'L0_ffn_k_scale': _L0_ffn_in['k_scale'], 'L0_ffn_wo': _L0_ffn_in['wo'], 'L0_ffn_ln_g': _L0_ffn_in['ln_g'], 'L0_ffn_ln_b': _L0_ffn_in['ln_b'], 'L0_ffn_w1': _L0_ffn_in['w1'], 'L0_ffn_b1': _L0_ffn_in['b1'], 'L0_ffn_w2': _L0_ffn_in['w2'], 'L0_ffn_b2': _L0_ffn_in['b2'], 'L0_c': _L0_c, 'L0_wmod': _L0_wmod}
    _x0 = _d['L0_attn_x']
    _d['L0_attn_x'] = jax.random.normal(jax.random.fold_in(jax.random.key(seed), 1), (8, 1024, 256), dtype=_x0.dtype)
    del _x0
    return _d

def reference(L0_attn_x, L0_attn_Wa, L0_attn_ba, L0_attn_We, L0_attn_be, L0_attn_Wi, L0_attn_Wo, L0_attn_Wv, L0_attn_Wout, L0_attn_chi, L0_attn_beta_p, L0_attn_iv_p, L0_attn_ov_p, L0_ffn_wqkv, L0_ffn_q_scale, L0_ffn_k_scale, L0_ffn_wo, L0_ffn_ln_g, L0_ffn_ln_b, L0_ffn_w1, L0_ffn_b1, L0_ffn_w2, L0_ffn_b2, L0_c, L0_wmod):

    def _L0_attn_ref(x, Wa, ba, We, be, Wi, Wo, Wv, Wout, chi, beta_p, iv_p, ov_p):
        import math
        import jax, jax.numpy as jnp
        import numpy as np
        PI = math.pi
        PHI = (1 + math.sqrt(5)) / 2
        B, T, D, H = (4, 256, 256, 16)
        DH = D // H

        def _chamber_beta_init(n_heads, layer_depth=0.5):
            lo = layer_depth * 0.5
            hi = 0.5 + layer_depth * 0.5
            frac = np.arange(n_heads) / max(n_heads - 1, 1)
            depth = lo + frac * (hi - lo)
            return (0.5 + 0.2 * (1.0 - 2.0 * depth)).astype(np.float32)
        Bb, Tt, Dd = x.shape
        Hh = Wa.shape[1]
        dh = Dd // Hh
        scale = math.sqrt(dh)
        aperture = jax.nn.sigmoid(x @ Wa + ba)
        expression = jax.nn.sigmoid(x @ We + be)
        inner = (x @ Wi).reshape(Bb, Tt, Hh, dh).transpose(0, 2, 1, 3)
        outer = (x @ Wo).reshape(Bb, Tt, Hh, dh).transpose(0, 2, 1, 3)
        alignment = jnp.einsum('bhqd,bhkd->bhqk', inner, outer) / scale
        attn_align = jax.nn.softmax(alignment, axis=-1)
        attn = attn_align * aperture.transpose(0, 2, 1)[..., :, None] * expression.transpose(0, 2, 1)[..., None, :]
        attn = attn / (attn.sum(axis=-1, keepdims=True) + 1e-08)
        v = (x @ Wv).reshape(Bb, Tt, Hh, dh).transpose(0, 2, 1, 3)
        converged = jnp.einsum('bhqk,bhkd->bhqd', attn, v)
        beta = jax.nn.sigmoid(beta_p)[None, :, None, None]
        iv = jax.nn.sigmoid(iv_p)[None, :, None, None]
        ov = jax.nn.sigmoid(ov_p)[None, :, None, None]
        angle = PI * beta
        ca, sa = (jnp.cos(angle), jnp.sin(angle))
        x_in = converged * iv
        half = dh // 2
        xr, xi = (x_in[..., :half], x_in[..., half:])
        chambered = jnp.concatenate([xr * ca - xi * sa, xr * sa + xi * ca], axis=-1) * ov
        rotated = chambered * jnp.tanh(chi)[None, :, None, None]
        combined = rotated.transpose(0, 2, 1, 3).reshape(Bb, Tt, Dd)
        return combined @ Wout

    def _L0_ffn_ref(x, wqkv, q_scale, k_scale, wo, ln_g, ln_b, w1, b1, w2, b2):
        import jax, jax.numpy as jnp
        import numpy as np
        DIM = 256
        DEPTH = 2
        HEADS = 8
        DIM_HEAD = 64
        WINDOW = 128
        INNER = HEADS * DIM_HEAD
        HID = int(DIM * 4 * 2 / 3)
        B, N = (2, 2048)
        QK_SCALE = 8.0

        def shift_token(t):
            t1, t2 = jnp.split(t, 2, axis=-1)
            t2 = jnp.pad(t2, ((0, 0), (1, 0), (0, 0)))[:, :-1]
            return jnp.concatenate([t1, t2], axis=-1)

        def l2norm(t):
            return t / jnp.clip(jnp.linalg.norm(t, axis=-1, keepdims=True), 1e-12)

        def rotate_half(x):
            x1, x2 = jnp.split(x, 2, axis=-1)
            return jnp.concatenate([-x2, x1], axis=-1)

        def rotary_xpos(q, k):
            n = q.shape[-2]
            half_idx = jnp.arange(0, DIM_HEAD, 2, dtype=jnp.float32)
            inv_freq = 1.0 / 10000.0 ** (half_idx / DIM_HEAD)
            t = jnp.arange(n, dtype=jnp.float32)
            freqs = t[:, None] * inv_freq[None, :]
            freqs = jnp.concatenate([freqs, freqs], axis=-1)
            base = (half_idx + 0.4 * DIM_HEAD) / (1.4 * DIM_HEAD)
            power = (t - n // 2) / float(WINDOW // 2)
            scale = base[None, :] ** power[:, None]
            scale = jnp.concatenate([scale, scale], axis=-1)
            cos, sin = (jnp.cos(freqs), jnp.sin(freqs))
            q = q * cos * scale + rotate_half(q) * sin * scale
            k = k * cos / scale + rotate_half(k) * sin / scale
            return (q, k)

        def local_attention(q, k, v):
            b, h, n, d = q.shape
            w = n // WINDOW
            bq = q.reshape(b, h, w, WINDOW, d) * QK_SCALE
            bk = k.reshape(b, h, w, WINDOW, d)
            bv = v.reshape(b, h, w, WINDOW, d)

            def look_around(t):
                p = jnp.pad(t, ((0, 0), (0, 0), (1, 0), (0, 0), (0, 0)))
                return jnp.concatenate([p[:, :, :w], p[:, :, 1:]], axis=3)
            bk, bv = (look_around(bk), look_around(bv))
            bt = jnp.arange(n).reshape(w, WINDOW)
            btp = jnp.pad(bt, ((1, 0), (0, 0)), constant_values=-1)
            btk = jnp.concatenate([btp[:w], btp[1:]], axis=1)
            sim = jnp.einsum('bhwid,bhwjd->bhwij', bq, bk)
            i = bt[:, :, None]
            j = btk[:, None, :]
            mask = (i < j) | (i > j + WINDOW) | (j == -1)
            sim = jnp.where(mask, -jnp.finfo(sim.dtype).max, sim)
            attn = jax.nn.softmax(sim, axis=-1)
            out = jnp.einsum('bhwij,bhwjd->bhwid', attn, bv)
            return out.reshape(b, h, n, d)

        def _layer(x, wqkv, qs, ksc, wo, lg, lb, w1, b1, w2, b2):
            b, n, _ = x.shape
            h = shift_token(x)
            qkv = h @ wqkv
            q, k, v = jnp.split(qkv, 3, axis=-1)
            to_heads = lambda t: t.reshape(b, n, HEADS, DIM_HEAD).transpose(0, 2, 1, 3)
            q, k, v = (to_heads(q), to_heads(k), to_heads(v))
            q = l2norm(q) * qs
            k = l2norm(k) * ksc
            q, k = rotary_xpos(q, k)
            o = local_attention(q, k, v)
            o = o.transpose(0, 2, 1, 3).reshape(b, n, INNER)
            x = x + o @ wo
            h = shift_token(x)
            mu = h.mean(-1, keepdims=True)
            var = h.var(-1, keepdims=True)
            h = (h - mu) / jnp.sqrt(var + 1e-05) * lg + lb
            h = h @ w1 + b1
            a, g = jnp.split(h, 2, axis=-1)
            h = a * jax.nn.gelu(g, approximate=False)
            x = x + h @ w2 + b2
            return x
        for l in range(DEPTH):
            x = _layer(x, wqkv[l], q_scale[l], k_scale[l], wo[l], ln_g[l], ln_b[l], w1[l], b1[l], w2[l], b2[l])
        return x
    x = L0_attn_x
    mod = (_silu(L0_c) @ L0_wmod).reshape(L0_c.shape[0], 6, 1, -1)
    sa, ca, ga, sb, cb, gb = (mod[:, 0], mod[:, 1], mod[:, 2], mod[:, 3], mod[:, 4], mod[:, 5])
    ga = (2 * (ga >= 0) - 1) * jnp.maximum(jnp.abs(ga), 0.25)
    gb = (2 * (gb >= 0) - 1) * jnp.maximum(jnp.abs(gb), 0.25)
    h = _layernorm(x, axis=-1) * (1 + ca) + sa
    x = x + ga * _L0_attn_ref(h, L0_attn_Wa, L0_attn_ba, L0_attn_We, L0_attn_be, L0_attn_Wi, L0_attn_Wo, L0_attn_Wv, L0_attn_Wout, L0_attn_chi, L0_attn_beta_p, L0_attn_iv_p, L0_attn_ov_p)
    h = _layernorm(x, axis=-1) * (1 + cb) + sb
    x = x + gb * _L0_ffn_ref(h, L0_ffn_wqkv, L0_ffn_q_scale, L0_ffn_k_scale, L0_ffn_wo, L0_ffn_ln_g, L0_ffn_ln_b, L0_ffn_w1, L0_ffn_b1, L0_ffn_w2, L0_ffn_b2)
    return x

_drawn_inputs = setup_inputs


def setup_inputs(seed=0):
    import zlib

    import numpy as np

    out = dict(_drawn_inputs(seed))
    spreads = {'L0_attn_ba': (0.0, 2.0),
     'L0_attn_be': (0.0, 0.8),
     'L0_attn_chi': (1.0, 0.6),
     'L0_attn_iv_p': (0.5, 0.6),
     'L0_attn_ov_p': (0.5, 0.6),
     'L0_ffn_q_scale': (1.0, 0.6),
     'L0_ffn_k_scale': (1.0, 0.6),
     'L0_ffn_ln_g': (1.0, 0.6),
     'L0_ffn_ln_b': (0.0, 0.8),
     'L0_ffn_b1': (0.0, 0.8),
     'L0_ffn_b2': (0.0, 0.449)}
    factors = {'L0_attn_Wa': 64.0,
     'L0_attn_We': 8.0,
     'L0_attn_Wi': 8.0,
     'L0_attn_Wo': 8.0,
     'L0_attn_Wv': 8.0,
     'L0_attn_Wout': 8.0,
     'L0_attn_beta_p': 8.0,
     'L0_ffn_wqkv': 6.941,
     'L0_ffn_wo': 6.823,
     'L0_ffn_w1': 4.768,
     'L0_ffn_w2': 4.748}
    for name, (base, spread) in spreads.items():
        noise = np.random.default_rng([zlib.crc32(name.encode()), seed]).standard_normal(out[name].shape)
        drawn = base * np.exp(spread * noise) if base else spread * noise
        out[name] = jnp.asarray(drawn.astype(out[name].dtype))
    for name, factor in factors.items():
        out[name] = (out[name] * factor).astype(out[name].dtype)
    return out
```

```python
from contextlib import ExitStack

import numpy as np

import concourse.bass as bass
from concourse import mybir

F32 = mybir.dt.float32
BF16 = mybir.dt.bfloat16
ALU = mybir.AluOpType
ACT = mybir.ActivationFunctionType
AX = mybir.AxisListType

P = 128
B, T, D = 8, 1024, 256
NT = T // P
DC = D // P
HALF = 512
NH = T // HALF
H, DH = 16, 16
G = 4
NG = H // G
PART = 3
PAIRS_Q = (0, 0, 0, 1, 1, 2)
PAIRS_K = (0, 1, 2, 0, 1, 0)
KS = DH * len(PAIRS_Q)
VW = 32
NEA = 2 * H
LAYERS, LH, LD = 2, 8, 64
INNER = LH * LD
HID = 682
FC = -(-HID // P)
FR = HID - (FC - 1) * P
LN_EPS = 1e-5
MASKED = -1e25
FREE = 1
SET_SILU, SET_ANGLE, SET_MOD, SET_ALL, ID_ALL = 3, 7, 23, 37, 4


def build(nc, x, Wa, ba, We, be, Wi, Wo, Wv, Wout, Wout_sw, head_vec, sgn, wqkv, q_scale, k_scale,
          wo, ln_g, ln_b, w1, b1, w2, b2, c, wmod, rope, mask, out):
    mod_d = nc.dram_tensor("mod_d", (B, 6 * D), F32, kind="Internal").ap()
    tab_d = nc.dram_tensor("tab_d", (NT, P, LAYERS * 4 * LD), F32, kind="Internal").ap()
    parts_d = nc.dram_tensor("parts_d", (2, PART, D, T), BF16, kind="Internal").ap()

    ctx = ExitStack()
    with ctx:
        def sem(name):
            return ctx.enter_context(nc.semaphore(name))

        def res(name, shape, dt=F32):
            return ctx.enter_context(nc.sbuf_tensor(name, shape, dt))

        ident = res("ident", [P, P])
        identb = res("identb", [P, P], BF16)
        wi_sb = res("wi_sb", [P, 2, DC, D])
        wvea = res("wvea", [P, DC, D + NEA])
        wfold = res("wfold", [P, DC, D])
        wga = res("wga", [P, DC, D])
        bias_ea = res("bias_ea", [P, NEA])
        wqkv_sb = res("wqkv_sb", [P, LAYERS, DC, 3 * INNER])
        wo_sb = res("wo_sb", [P, LAYERS, INNER // P, D])
        w1_sb = res("w1_sb", [P, LAYERS, DC, 2 * HID])
        w2_sb = res("w2_sb", [P, LAYERS, FC, D])
        b1_sb = res("b1_sb", [P, LAYERS, 2, FC])
        b2_sb = res("b2_sb", [P, LAYERS, D])
        lnv = res("lnv", [P, LAYERS, 2, DC])
        neghalf = res("neghalf", [P, 2 * LH])
        xs = res("xs", [P, 2, NT, D])
        modA = res("modA", [P, 3, D])
        modF = res("modF", [P, 2, 3, D])

        with ExitStack() as scope:
            def tmp(name, shape, dt=F32):
                return scope.enter_context(nc.sbuf_tensor(name, shape, dt))
            wmod_sb = tmp("wmod_sb", [P, DC, 6 * D])
            cT = tmp("cT", [P, DC, B])
            ce = tmp("ce", [P, DC, B])
            modsb = tmp("modsb", [B, 6 * D])
            sg = tmp("sg", [B, 2, D])
            hv = tmp("hv", [P, 4, DC])
            he = tmp("he", [P, 4, DC])
            hc = tmp("hc", [P, 6, DC])
            sgnc = tmp("sgnc", [P, DC])
            wout_sb = tmp("wout_sb", [P, 2, DC, D])
            rope_sb = tmp("rope_sb", [P, NT, 4, LD])
            scl = tmp("scl", [P, LAYERS, 4, LD])
            tabs = tmp("tabs", [P, NT, LAYERS, 4, LD])

        with ExitStack() as scope:
            hn = tmp("hn", [P, NT, D])
            hT = tmp("hT", [P, DC, T])
            parts = tmp("parts", [P, 4, PART, HALF], BF16)
            rest = tmp("rest", [P, 2, HALF])
            o_sb = tmp("o_sb", [P, T])
            cvT = tmp("cvT", [P, DC, T])
            stack = tmp("stack", [P, 2, 2, G, T], BF16)
            vg = tmp("vg", [P, 2, NT, G, VW])
            pr = tmp("pr", [P, 2, G, HALF])
            st1 = tmp("st1", [P, NT, 6])
            mv1 = tmp("mv1", [P, NT, 2])
            rs1 = tmp("rs1", [P, NT])
            zt = tmp("zt", [P, NT, NEA])
            mx = tmp("mx", [P, G * NT, NH])
            m2 = tmp("m2", [P, G * NT])
            mr = tmp("mr", [P, G * NT])
            m3 = tmp("m3", [P, PART, G * NT], BF16)
            mrow = tmp("mrow", [PART * G * NT, 2, P], BF16)
            den = tmp("den", [P, NT, G])
        vt, cv = hn, hT[:].rearrange("p c t -> p (c t)").rearrange("p (t d) -> p t d", t=NT)

        with ExitStack() as scope:
            tab = tmp("tab", [P, LAYERS, 4, LD])
            maskt = tmp("maskt", [P, 2 * P])
            S = [dict(
                u=tmp(f"u_s{s}", [P, D]),
                uT=tmp(f"uT_s{s}", [P, LAYERS, 2 * P + 4]),
                big=tmp(f"big_s{s}", [P, LH, 2 * P]),
                pT=tmp(f"pT_s{s}", [P, LH, 2, P]),
                qz=tmp(f"qz_s{s}", [P, LH, P]),
                kT=tmp(f"kT_s{s}", [P, LAYERS, LH // 2, 2 * P]),
                v=tmp(f"v_s{s}", [P, LAYERS, 2, INNER]),
                oT=tmp(f"oT_s{s}", [P, INNER // P, P]),
                ush=tmp(f"ush_s{s}", [P, P]),
                crow=tmp(f"crow_s{s}", [1, LAYERS, P]),
                hl=tmp(f"hl_s{s}", [P, D]),
                hlT=tmp(f"hlT_s{s}", [P, DC, P]),
                st=tmp(f"st_s{s}", [P, 2, 6]),
                mv=tmp(f"mv_s{s}", [P, 2]),
                rs=tmp(f"rs_s{s}", [P, 1]),
                ss=tmp(f"ss_s{s}", [P, 2 * LH]),
                rn=tmp(f"rn_s{s}", [P, 2 * LH]),
                mx=tmp(f"mxl_s{s}", [P, LH]),
                z=tmp(f"z_s{s}", [P, LH]),
                rz=tmp(f"rz_s{s}", [P, LH]),
                o=tmp(f"o_s{s}", [P, D]),
            ) for s in range(2)]

        psum = ctx.enter_context(nc.psum_tensor("psum", [P, 8, HALF], F32))

        def bank_bf16(k):
            return psum[:, k, :].bitcast(BF16)

        s_wts = sem("s_wts")
        s_id = sem("s_id")
        s_set_act = sem("s_set_act")
        s_set_dve = sem("s_set_dve")
        s_set_pe = sem("s_set_pe")
        s_set_out = sem("s_set_out")
        s_x_in = sem("s_x_in")
        s_stats1 = sem("s_stats1")
        s_aggr1 = sem("s_aggr1")
        s_eps1 = sem("s_eps1")
        s_rstd1 = sem("s_rstd1")
        s_norm1 = sem("s_norm1")
        s_mod1 = sem("s_mod1")
        s_wga = sem("s_wga")
        s_ones = sem("s_ones")
        s_hT_ps = sem("s_hT_ps")
        s_hT = [sem(f"s_hT_{e}") for e in ("act", "dve")]
        s_proj = sem("s_proj")
        s_hi = sem("s_hi")
        s_rest = sem("s_rest")
        s_mid = sem("s_mid")
        s_low = sem("s_low")
        s_parts_out = [sem(f"s_parts_out{k}") for k in range(4)]
        s_v_ps = sem("s_v_ps")
        s_v = sem("s_v")
        s_z = sem("s_z")
        s_z_exp = sem("s_z_exp")
        s_gate = sem("s_gate")
        s_stack_in = [sem(f"s_stack_in{k}") for k in range(2)]
        s_s_ps = sem("s_s_ps")
        s_max = sem("s_max")
        s_msplit = sem("s_msplit")
        s_mT_ps = sem("s_mT_ps")
        s_mrow = sem("s_mrow")
        s_m_in = [sem(f"s_m_in{k}") for k in range(2)]
        s_vg = sem("s_vg")
        s_st_ps = sem("s_st_ps")
        s_exp = sem("s_exp")
        s_pv = sem("s_pv")
        s_osb = sem("s_osb")
        s_oT_ps = sem("s_oT_ps")
        s_den = sem("s_den")
        s_conv = sem("s_conv")
        s_cvT_ps = sem("s_cvT_ps")
        s_cvT = [sem(f"s_cvT_{e}") for e in ("act", "dve")]
        s_att_ps = sem("s_att_ps")
        s_x1 = sem("s_x1")
        f = {n: sem("f_" + n) for n in (
            "zero tab_in ln0_st ln0_ag ln0_eps ln0_rs ln0_n ln0_m ln0 uT_ps carry uT qkv sq vev ssum "
            "clip rn ropeC ropeS rope kn qkT_ps qz kT s_ps sm neg exp rz pn pT_ps pT_a pT_d o_ps oT kvprev "
            "wo_ps u1 sh crow ub ln_st ln_ag ln_eps ln_rs hl hl_ps hlT g_ps gelu act w2_ps u2 "
            "og oo out").split()}

        block = ctx.enter_context(nc.Block())

        loads = [0]

        @block.sync
        def _(sp):
            def load(dst, src):
                loads[0] += 1
                sp.dma_start(dst, src).then_inc(s_wts, 16)

            with nc.allow_non_contiguous_dma("small set-up vectors"):
                for k in range(DC):
                    load(cT[:, k, :], c.rearrange("b (k p) -> k p b", p=P)[k])
                load(wmod_sb[:], wmod.rearrange("(k p) n -> p k n", p=P))
                load(hv[:], head_vec)
                load(sgnc[:], sgn)
                load(wout_sb[:, 0], Wout.rearrange("(k p) n -> p k n", p=P))
                load(wout_sb[:, 1], Wout_sw.rearrange("(k p) n -> p k n", p=P))
                load(rope_sb[:], rope)
                for l in range(LAYERS):
                    for n, v in ((0, q_scale), (1, k_scale)):
                        load(scl[:, l, n, :], v[l].partition_broadcast(P))
                        load(scl[:, l, 2 + n, 0:LD // 2], v[l, LD // 2:LD].partition_broadcast(P))
                        load(scl[:, l, 2 + n, LD // 2:LD], v[l, 0:LD // 2].partition_broadcast(P))
                load(wi_sb[:, 0], Wi.rearrange("(k p) n -> p k n", p=P))
                load(wi_sb[:, 1], Wo.rearrange("(k p) n -> p k n", p=P))
                load(wvea[:, :, 0:D], Wv.rearrange("(k p) n -> p k n", p=P))
                load(wvea[:, :, D:D + H], We.rearrange("(k p) n -> p k n", p=P))
                load(wvea[:, :, D + H:D + NEA], Wa.rearrange("(k p) n -> p k n", p=P))
                load(bias_ea[:, 0:H], be.partition_broadcast(P))
                load(bias_ea[:, H:NEA], ba.partition_broadcast(P))
                for l in range(LAYERS):
                    load(wqkv_sb[:, l], wqkv[l].rearrange("(k p) n -> p k n", p=P))
                    load(wo_sb[:, l], wo[l].rearrange("(k p) n -> p k n", p=P))
                    load(w1_sb[:, l], w1[l].rearrange("(k p) n -> p k n", p=P))
                    load(w2_sb[:, l, 0:FC - 1], w2[l, 0:(FC - 1) * P].rearrange("(k p) n -> p k n", p=P))
                    load(w2_sb[0:FR, l, FC - 1], w2[l, (FC - 1) * P:HID])
                    for n in range(2):
                        o = n * HID
                        load(b1_sb[:, l, n, 0:FC - 1], b1[l, o:o + (FC - 1) * P].rearrange("(k p) -> p k", p=P))
                        load(b1_sb[0:FR, l, n, FC - 1:FC], b1[l, o + (FC - 1) * P:o + HID].unsqueeze(1))
                    load(b2_sb[:, l], b2[l].partition_broadcast(P))
                    load(lnv[:, l, 0], ln_g[l].rearrange("(k p) -> p k", p=P))
                    load(lnv[:, l, 1], ln_b[l].rearrange("(k p) -> p k", p=P))
            sp.wait_ge(s_set_dve, SET_MOD)
            sp.nop(nofuse=True)
            sp.dma_start(mod_d, modsb[:]).then_inc(s_set_out, 16)
            sp.wait_ge(s_set_dve, SET_ALL)
            sp.nop(nofuse=True)
            for l in range(LAYERS):
                sp.dma_start(tab_d.rearrange("t p (l n) -> l p t n", l=LAYERS)[l],
                             tabs[:, :, l].rearrange("p t a d -> p t (a d)")).then_inc(s_set_out, 16)
            sp.wait_ge(s_set_out, 16 * (1 + LAYERS))
            sp.nop(nofuse=True)

            with sp.Fori(0, B // 2) as i:
                with sp.Fori(0, 2) as j:
                    b = i * 2 + j
                    sp.wait_ge(s_x1, FREE + b * NT)
                    sp.nop(nofuse=True)
                    sp.wait_ge(f["out"], FREE + i * (32 * NT))
                    sp.nop(nofuse=True)
                    sp.dma_start(xs[:, bass.ds(j, 1)], x.rearrange("b (t p) d -> p b t d", p=P)[:, bass.ds(b, 1)]) \
                        .then_inc(s_x_in, 16)
                    md = mod_d.rearrange("b n -> (b n)")
                    sp.dma_start(modA[:].rearrange("p a d -> p (a d)"),
                                 md[bass.ds(b * (6 * D), 3 * D)].partition_broadcast(P)).then_inc(s_x_in, 16)
                    sp.dma_start(modF[:].rearrange("p j a d -> p (j a d)")[:, bass.ds(j * (3 * D), 3 * D)],
                                 md[bass.ds(b * (6 * D) + 3 * D, 3 * D)].partition_broadcast(P)).then_inc(s_x_in, 16)
                    for n in range(8):
                        sp.wait_ge(s_low, b * 8 + n + 1)
                        sp.nop(nofuse=True)
                        qk, m, h = n // 4, (n // 2) % 2, n % 2
                        sp.dma_start(parts_d[qk, :, m * P:(m + 1) * P, h * HALF:(h + 1) * HALF]
                                     .rearrange("a p t -> p a t"), parts[:, n % 4]).then_inc(s_parts_out[n % 4], 16)
                    for k in range(4):
                        sp.wait_ge(s_parts_out[k], FREE + b * 32 + 32)
                        sp.nop(nofuse=True)

                    def stacks(g):
                        for qk, order in ((0, PAIRS_Q), (1, PAIRS_K)):
                            for s, part in enumerate(order):
                                sp.dma_start(
                                    stack[s * DH:(s + 1) * DH, g % 2, qk],
                                    parts_d[qk, part, g * G * DH:(g + 1) * G * DH, :].rearrange("(h i) t -> i h t", i=DH)
                                ).then_inc(s_stack_in[g % 2], 16)

                    def maxima(g):
                        sp.wait_ge(s_mrow, b * NG + g + 1)
                        sp.nop(nofuse=True)
                        for s in range(PART):
                            sp.dma_start(
                                stack[KS + s:KS + s + 1, g % 2, 0].rearrange("o h (a q) -> o (h a) q", q=P),
                                mrow[s * G * NT:(s + 1) * G * NT, g % 2, :]
                            ).then_inc(s_m_in[g % 2], 16)
                    stacks(0)
                    stacks(1)
                    maxima(0)
                    for g in range(1, NG):
                        maxima(g)
                        if g + 1 < NG:
                            sp.wait_ge(s_pv, b * (NG * 16) + g * 16)
                            sp.nop(nofuse=True)
                            stacks(g + 1)
                sp.wait_ge(f["zero"], i * 10 + 10)
                sp.nop(nofuse=True)
                with sp.Fori(0, NT) as t:
                    it = i * NT + t
                    sp.wait_ge(f["sm"], FREE + it * 4)
                    sp.nop(nofuse=True)
                    sp.wait_ge(s_x1, FREE + i * (2 * NT) + 2 * NT)
                    sp.nop(nofuse=True)
                    sp.dma_start(tab[:].rearrange("p l a d -> p (l a d)"),
                                 tab_d[bass.ds(t, 1)].rearrange("o p n -> p (o n)")).then_inc(f["tab_in"], 16)
                    sp.dma_start(maskt[:], mask[bass.ds(t, 1)].rearrange("o p n -> p (o n)")).then_inc(f["tab_in"], 16)
                    for l in range(LAYERS):
                        for s in range(2):
                            n = it * 4 + (2 * l + s)
                            u, ush, crow = S[s]["u"], S[s]["ush"], S[s]["crow"]
                            sp.wait_ge(f["u1"], n + 1)
                            sp.nop(nofuse=True)
                            sp.dma_start(ush[1:P, :], u[0:P - 1, P:D]).then_inc(f["sh"], 16)
                            sp.dma_start(ush[0:1, :], crow[:, l]).then_inc(f["sh"], 16)
                            sp.wait_ge(f["sh"], n * 32 + 32)
                            sp.nop(nofuse=True)
                            sp.dma_start(crow[:, l], u[P - 1:P, P:D]).then_inc(f["crow"], 16)
                            sp.wait_ge(f["crow"], n * 16 + 16)
                            sp.nop(nofuse=True)
                    for s in range(2):
                        sp.wait_ge(f["oo"], it * 2 + s + 1)
                        sp.nop(nofuse=True)
                        sp.dma_start(out.rearrange("(i j) (t p) d -> i j t p d", j=2, p=P)[bass.ds(i, 1), s, bass.ds(t, 1)]
                                     .rearrange("o q p d -> p (o q d)"), S[s]["o"][:]).then_inc(f["out"], 16)
            sp.wait_ge(f["out"], FREE + 16 * B * NT)
            sp.nop(nofuse=True)

        @block.tensor
        def _(pe):
            pe.wait_ge(s_wts, 16 * loads[0])
            pe.wait_ge(s_id, ID_ALL)
            pe.wait_ge(s_set_dve, SET_SILU)
            for n in range(3):
                for k in range(DC):
                    mm = pe.matmul(psum[0:B, n, :], cT[:, k, :], wmod_sb[:, k, n * HALF:(n + 1) * HALF],
                                   start=(k == 0), stop=(k == DC - 1))
            mm.then_inc(s_set_pe, 1)
            pe.wait_ge(s_set_dve, SET_ALL)

            def phase_a(b):
                pe.wait_ge(s_mod1, b * 2 + 2)
                for k in range(DC):
                    for t in range(NT):
                        mm = pe.transpose(psum[:, 2 * k + t // 4, (t % 4) * P:(t % 4 + 1) * P],
                                          hn[:, t, k * P:(k + 1) * P], ident[:])
                        if t % 4 == 3:
                            mm.then_inc(s_hT_ps, 1)
                for e in range(2):
                    pe.wait_ge(s_hT[e], b * 2 + 2)
                for n in range(8):
                    qk, m, h = n // 4, (n // 2) % 2, n % 2
                    if n >= 4:
                        pe.wait_ge(s_rest, b * 8 + n - 3)
                    for k in range(DC):
                        mm = pe.matmul(psum[:, n % 4, :], wi_sb[:, qk, k, m * P:(m + 1) * P],
                                       hT[:, k, h * HALF:(h + 1) * HALF], start=(k == 0), stop=(k == DC - 1))
                    mm.then_inc(s_proj, 1)
                for t in range(NT):
                    if t >= 4:
                        pe.wait_ge(s_v, b * NT + t - 3)
                        pe.wait_ge(s_z, b * NT + t - 3)
                    for k in range(DC):
                        mm = pe.matmul(psum[:, 4 + t % 4, 0:D + NEA], hT[:, k, t * P:(t + 1) * P], wvea[:, k, :],
                                       start=(k == 0), stop=(k == DC - 1))
                    mm.then_inc(s_v_ps, 1)
                pe.wait_ge(s_rest, b * 8 + 8)
                pe.wait_ge(s_v, b * NT + NT)
                pe.wait_ge(s_z, b * NT + NT)
                pe.wait_ge(s_ones, b * 3 + 3)

                def score_tile(g, m):
                    h, a = m // NT, m % NT
                    for kh in range(NH):
                        n = 2 * m + kh
                        if n >= 2 or g > 0:
                            pe.wait_ge(s_max, b * (NG * 64) + (g * 64 + n - 1))
                        pe.matmul(psum[:, 6 + kh, :], stack[0:KS, g % 2, 0, h, a * P:(a + 1) * P],
                                  stack[0:KS, g % 2, 1, h, kh * HALF:(kh + 1) * HALF], start=True, stop=True) \
                            .then_inc(s_s_ps, 1)

                def maxima(g):
                    pe.wait_ge(s_msplit, b * (NG * 5) + (g * 5 + 5))
                    pe.transpose(bank_bf16(6)[0:PART * G * NT, 0:P], m3[:].rearrange("p a m -> p (a m)"), identb[:]) \
                        .then_inc(s_mT_ps, 1)

                def attend(g):
                    pe.wait_ge(s_m_in[g % 2], FREE + b * (48 * 2) + 48 * (g // 2 + 1))
                    pe.wait_ge(s_vg, b * (NG * 2) + (g * 2 + 2))

                    def st(s):
                        qh, kc = s // NT, s % NT
                        for pair in range(2):
                            e = 2 * s + pair
                            if e >= 2 or g > 0:
                                pe.wait_ge(s_exp, b * (NG * 32) + (g * 32 + e - 1))
                            for h in (2 * pair, 2 * pair + 1):
                                mm = pe.matmul(psum[:, h, :], stack[0:KS + PART, g % 2, 1, h, kc * P:(kc + 1) * P],
                                               stack[0:KS + PART, g % 2, 0, h, qh * HALF:(qh + 1) * HALF],
                                               start=True, stop=True)
                            mm.then_inc(s_st_ps, 1)
                    st(0)
                    for s in range(16):
                        qh, kc = s // NT, s % NT
                        if s + 1 < 16:
                            st(s + 1)
                        if g + 1 < NG:
                            if s == 0:
                                pe.wait_ge(s_stack_in[(g + 1) % 2], b * (192 * 2) + 192 * ((g + 1) // 2 + 1))
                                pe.wait_ge(s_mrow, b * NG + g + 1)
                            score_tile(g + 1, 2 * s)
                            score_tile(g + 1, 2 * s + 1)
                        pe.wait_ge(s_exp, b * (NG * 32) + (g * 32 + 2 * s + 2))
                        if s == 0 and g > 0:
                            pe.wait_ge(s_conv, b * NG + g)
                        for h in range(G):
                            mm = pe.matmul(psum[h * VW:(h + 1) * VW, 4 + qh, :], vg[:, g % 2, kc, h, :],
                                           pr[:, s % 2, h, :], start=(kc == 0), stop=(kc == NT - 1))
                        mm.then_inc(s_pv, 1)
                    if g + 1 < NG:
                        maxima(g + 1)
                    pe.wait_ge(s_osb, b * NG + g + 1)
                    for t in range(NT):
                        mm = pe.transpose(psum[:, 4 + t // 4, (t % 4) * P:(t % 4 + 1) * P],
                                          o_sb[:, t * P:(t + 1) * P], ident[:])
                    mm.then_inc(s_oT_ps, 1)

                pe.wait_ge(s_stack_in[0], b * (192 * 2) + 192)
                for m in range(G * NT):
                    score_tile(0, m)
                maxima(0)
                for g in range(NG):
                    attend(g)
                pe.wait_ge(s_conv, b * NG + NG)
                for k in range(DC):
                    for t in range(NT):
                        mm = pe.transpose(psum[:, 2 * k + t // 4, (t % 4) * P:(t % 4 + 1) * P],
                                          cv[:, t, k * P:(k + 1) * P], ident[:])
                        if t % 4 == 3:
                            mm.then_inc(s_cvT_ps, 1)
                for e in range(2):
                    pe.wait_ge(s_cvT[e], b * 2 + 2)
                pe.wait_ge(s_wga, b + 1)
                for t in range(NT):
                    if t >= 4:
                        pe.wait_ge(s_x1, FREE + b * NT + t - 3)
                    for k in range(DC):
                        mm = pe.matmul(psum[:, 4 + t % 4, 0:D], cvT[:, k, t * P:(t + 1) * P], wga[:, k, :],
                                       start=(k == 0), stop=(k == DC - 1))
                    mm.then_inc(s_att_ps, 1)

            def window(it):
                for l in range(LAYERS):
                    N = [it * 4 + (2 * l + s) for s in range(2)]
                    for s in range(2):
                        w, n, bk = S[s], N[s], 4 * s
                        if l == 0:
                            pe.wait_ge(f["ln0"], it * 2 + s + 1)
                        else:
                            pe.wait_ge(f["u2"], n - 1)
                        for k in range(DC):
                            mm = pe.transpose(psum[:, bk, k * P:(k + 1) * P], w["u"][:, k * P:(k + 1) * P], ident[:])
                        mm.then_inc(f["uT_ps"], 1)
                    for s in range(2):
                        w, n, bk = S[s], N[s], 4 * s
                        pe.wait_ge(f["uT"], n + 1)
                        for m in range(3):
                            for k in range(DC):
                                mm = pe.matmul(psum[:, bk + m, :], w["uT"][:, l, k * (P + 1):k * (P + 1) + P],
                                               wqkv_sb[:, l, k, m * INNER:(m + 1) * INNER],
                                               start=(k == 0), stop=(k == DC - 1))
                        mm.then_inc(f["qkv"], 1)
                    for s in range(2):
                        w, n, bk = S[s], N[s], 4 * s
                        qk = w["big"][:].rearrange("p h n -> p (h n)")
                        pe.wait_ge(f["kn"], n + 1)
                        for m in range(2 * INNER // P):
                            mm = pe.transpose(psum[:, bk + m // 4, (m % 4) * P:(m % 4 + 1) * P],
                                              qk[:, m * P:(m + 1) * P], ident[:])
                        mm.then_inc(f["qkT_ps"], 1)
                    for s in range(2):
                        w, n, bk = S[s], N[s], 4 * s
                        pe.wait_ge(f["qz"], n + 1)
                        pe.wait_ge(f["kT"], n + 1)
                        pe.wait_ge(f["vev"], n + 1)
                        for h in range(LH):
                            mm = pe.matmul(psum[:, bk + h // 2, (h % 2) * 2 * P:(h % 2 + 1) * 2 * P], w["qz"][:, h, :],
                                           w["kT"][:, l, h // 2, :], start=True, stop=True)
                            if h % 2:
                                mm.then_inc(f["s_ps"], 1)
                    for s in range(2):
                        w, n, bk = S[s], N[s], 4 * s
                        pe.wait_ge(f["pn"], n + 1)
                        for h in range(LH):
                            for kb in range(2):
                                mm = pe.transpose(psum[:, bk + h // 2, (2 * (h % 2) + kb) * P:(2 * (h % 2) + kb + 1) * P],
                                                  w["big"][:, h, kb * P:(kb + 1) * P], ident[:])
                            if h % 2:
                                mm.then_inc(f["pT_ps"], 1)
                    for s in range(2):
                        w, n, bk = S[s], N[s], 4 * s
                        pe.wait_ge(f["pT_a"], n * 2 + 2)
                        pe.wait_ge(f["pT_d"], n * 2 + 2)
                        for m in range(LH // 2):
                            for kb in range(2):
                                for h in (2 * m, 2 * m + 1):
                                    mm = pe.matmul(psum[(h % 2) * LD:(h % 2 + 1) * LD, bk, m * P:(m + 1) * P],
                                                   w["v"][:, l, kb, h * LD:(h + 1) * LD], w["pT"][:, h, kb, :],
                                                   start=(kb == 0), stop=(kb == 1))
                        mm.then_inc(f["o_ps"], 1)
                    for s in range(2):
                        w, n, bk = S[s], N[s], 4 * s
                        pe.wait_ge(f["oT"], n + 1)
                        for k in range(INNER // P):
                            mm = pe.matmul(psum[:, bk + 1, 0:D], w["oT"][:, k, :], wo_sb[:, l, k, :],
                                           start=(k == 0), stop=(k == INNER // P - 1))
                        mm.then_inc(f["wo_ps"], 1)
                    for s in range(2):
                        w, n, bk = S[s], N[s], 4 * s
                        pe.wait_ge(f["hl"], n * 2 + 2)
                        for k in range(DC):
                            mm = pe.transpose(psum[:, bk, k * P:(k + 1) * P], w["hl"][:, k * P:(k + 1) * P], ident[:])
                        mm.then_inc(f["hl_ps"], 1)
                    for s in range(2):
                        w, n, bk = S[s], N[s], 4 * s
                        pe.wait_ge(f["hlT"], n * 2 + 2)
                        for m in range(2 * FC):
                            cc, rows = m % FC, P if m % FC < FC - 1 else FR
                            col = (HID if m < FC else 0) + cc * P
                            for k in range(DC):
                                mm = pe.matmul(psum[0:rows, bk + 1 + m // 4, (m % 4) * P:(m % 4 + 1) * P],
                                               w1_sb[:, l, k, col:col + rows], w["hlT"][:, k, :],
                                               start=(k == 0), stop=(k == DC - 1))
                        mm.then_inc(f["g_ps"], 1)
                    for s in range(2):
                        w, n, bk = S[s], N[s], 4 * s
                        act = w["pT"][:].rearrange("p h k n -> p (h k) n")
                        pe.wait_ge(f["act"], n * FC + FC)
                        for cc in range(FC):
                            rows = P if cc < FC - 1 else FR
                            mm = pe.matmul(psum[:, bk, 0:D], act[0:rows, cc, :], w2_sb[0:rows, l, cc, :],
                                           start=(cc == 0), stop=(cc == FC - 1))
                        mm.then_inc(f["w2_ps"], 1)

            with pe.Fori(0, B // 2) as i:
                with pe.Fori(0, 2) as j:
                    phase_a(i * 2 + j)
                with pe.Fori(0, NT) as t:
                    window(i * NT + t)

        @block.scalar
        def _(act):
            act.wait_ge(s_wts, 16 * loads[0])
            act.activation(ce[:], cT[:], ACT.Exp, scale=-1.0).then_inc(s_set_act, 1)
            act.activation(he[:, 0:3], hv[:, 0:3], ACT.Exp, scale=-1.0).then_inc(s_set_act, 1)
            act.activation(he[:, 3], hv[:, 3], ACT.Tanh).then_inc(s_set_act, 1)
            act.wait_ge(s_set_dve, SET_ANGLE)
            act.activation(hc[:, 4], hc[:, 2], ACT.Sin).then_inc(s_set_act, 1)
            act.activation(hc[:, 5], hc[:, 3], ACT.Sin).then_inc(s_set_act, 1)

            def phase_a(b):
                for k in range(DC):
                    act.wait_ge(s_hT_ps, b * 4 + 2 * k + 1)
                    act.activation(hT[:, k, 0:HALF], psum[:, 2 * k, :], ACT.Copy).then_inc(s_hT[0], 1)

                def hi(n):
                    act.wait_ge(s_proj, b * 8 + n + 1)
                    act.wait_ge(s_parts_out[n % 4], FREE + b * 32 + 16 * (n // 4))
                    act.activation(parts[:, n % 4, 0], psum[:, n % 4, :], ACT.Copy).then_inc(s_hi, 1)
                hi(0)
                for n in range(8):
                    if n < 7:
                        hi(n + 1)
                    act.wait_ge(s_rest, b * 8 + n + 1)
                    act.activation(parts[:, n % 4, 1], rest[:, n % 2], ACT.Copy).then_inc(s_mid, 1)
                for t in range(NT):
                    act.wait_ge(s_v_ps, b * NT + t + 1)
                    act.activation(vt[:, t, :], psum[:, 4 + t % 4, 0:D], ACT.Copy).then_inc(s_v, 1)
                act.wait_ge(s_z, b * NT + NT)
                act.activation(zt[:], zt[:], ACT.Exp, scale=-1.0).then_inc(s_z_exp, 1)
                for g in range(NG):
                    for s in range(16):
                        for pair in range(2):
                            act.wait_ge(s_st_ps, b * (NG * 32) + (g * 32 + 2 * s + pair + 1))
                            if s >= 2 or g > 0:
                                act.wait_ge(s_pv, b * (NG * 16) + (g * 16 + s - 1))
                            act.activation(pr[:, s % 2, 2 * pair:2 * pair + 2, :], psum[:, 2 * pair:2 * pair + 2, :],
                                           ACT.Exp, scale=DH ** -0.5).then_inc(s_exp, 1)
                    act.wait_ge(s_pv, b * (NG * 16) + (g * 16 + 16))
                    if g > 0:
                        act.wait_ge(s_oT_ps, b * NG + g)
                    act.activation(o_sb[:].rearrange("p (a n) -> p a n", a=2), psum[:, 4:6, :], ACT.Copy).then_inc(s_osb, 1)
                for k in range(DC):
                    act.wait_ge(s_cvT_ps, b * 4 + 2 * k + 1)
                    act.activation(cvT[:, k, 0:HALF], psum[:, 2 * k, :], ACT.Copy).then_inc(s_cvT[0], 1)

            def window(it):
                for l in range(LAYERS):
                    N = [it * 4 + (2 * l + s) for s in range(2)]
                    for s in range(2):
                        w, n, bk = S[s], N[s], 4 * s
                        act.wait_ge(f["qkv"], n + 1)
                        act.activation(w["pT"][:].rearrange("p h k n -> p (h k n)")[:, 0:2 * INNER]
                                       .rearrange("p (a n) -> p a n", a=2), psum[:, bk:bk + 2, :], ACT.Square) \
                            .then_inc(f["sq"], 1)
                        act.wait_ge(f["kvprev"], FREE + it * 8)
                        act.activation(w["v"][:, l, 1, :], psum[:, bk + 2, :], ACT.Copy).then_inc(f["vev"], 1)
                    for s in range(2):
                        w, n, bk = S[s], N[s], 4 * s
                        act.wait_ge(f["qkT_ps"], n + 1)
                        for hh in range(2):
                            ins = act.activation(w["qz"][hh * LD:(hh + 1) * LD, hh:LH:2, :],
                                                 psum[hh * LD:(hh + 1) * LD, bk, :].rearrange("p (m q) -> p m q", q=P),
                                                 ACT.Copy)
                        ins.then_inc(f["qz"], 1)
                    for s in range(2):
                        w, n, bk = S[s], N[s], 4 * s
                        act.wait_ge(f["neg"], n + 1)
                        for h in range(LH):
                            ins = act.activation(w["big"][:, h, :], w["big"][:, h, :], ACT.Exp, bias=w["mx"][:, h:h + 1],
                                                 accum_out=w["z"][:, h:h + 1])
                        ins.then_inc(f["exp"], 1)
                    for s in range(2):
                        w, n, bk = S[s], N[s], 4 * s
                        for m in (0, 2):
                            act.wait_ge(f["pT_ps"], n * 4 + m + 1)
                            act.activation(w["pT"][:, 2 * m:2 * m + 2], psum[:, bk + m, :]
                                           .rearrange("p (h k n) -> p h k n", h=2, k=2), ACT.Copy).then_inc(f["pT_a"], 1)
                    for s in range(2):
                        w, n, bk = S[s], N[s], 4 * s
                        act.wait_ge(f["o_ps"], n + 1)
                        act.activation(w["oT"][:].rearrange("p a n -> p (a n)"), psum[:, bk, :], ACT.Copy) \
                            .then_inc(f["oT"], 1)
                    for s in range(2):
                        w, n, bk = S[s], N[s], 4 * s
                        gl = w["pT"][:].rearrange("p h k n -> p (h k) n")
                        act.wait_ge(f["g_ps"], n + 1)
                        for cc in range(FC):
                            rows = P if cc < FC - 1 else FR
                            act.activation(gl[0:rows, cc, :], psum[0:rows, bk + 1 + cc // 4, (cc % 4) * P:(cc % 4 + 1) * P],
                                           ACT.Gelu, bias=b1_sb[0:rows, l, 1, cc:cc + 1]).then_inc(f["gelu"], 1)

            with act.Fori(0, B // 2) as i:
                with act.Fori(0, 2) as j:
                    phase_a(i * 2 + j)
                act.wait_ge(f["zero"], i * 10 + 10)
                with act.Fori(0, NT) as t:
                    window(i * NT + t)

        @block.vector
        def _(dve):
            chain = [0]

            def link(ins):
                chain[0] += 1
                ins.then_inc(s_set_dve, 1)
                dve.wait_ge(s_set_dve, chain[0])

            dve.wait_ge(s_wts, 16 * loads[0])
            dve.wait_ge(s_set_act, 1)
            link(dve.tensor_scalar(ce[:], ce[:], 1.0, None, ALU.add))
            link(dve.reciprocal(ce[:], ce[:]))
            link(dve.tensor_tensor(cT[:], cT[:], ce[:], ALU.mult))
            assert chain[0] == SET_SILU
            dve.wait_ge(s_set_act, 3)
            link(dve.tensor_scalar(he[:, 0:3], he[:, 0:3], 1.0, None, ALU.add))
            link(dve.reciprocal(he[:, 0:3], he[:, 0:3]))
            link(dve.tensor_scalar(hc[:, 2], he[:, 0], float(np.pi), None, ALU.mult))
            link(dve.tensor_scalar(hc[:, 3], hc[:, 2], -1.0, float(np.pi / 2), ALU.mult, ALU.add))
            assert chain[0] == SET_ANGLE
            link(dve.tensor_tensor(hc[:, 0], he[:, 1], he[:, 2], ALU.mult))
            link(dve.tensor_tensor(hc[:, 0], hc[:, 0], he[:, 3], ALU.mult))
            link(dve.tensor_tensor(sgnc[:], sgnc[:], hc[:, 0], ALU.mult))
            dve.wait_ge(s_set_pe, 1)
            link(dve.tensor_copy(modsb[:].rearrange("p (a n) -> p a n", a=3), psum[0:B, 0:3, :]))
            for n in (1, 4):
                link(dve.tensor_scalar(modsb[:, n * D:(n + 1) * D], modsb[:, n * D:(n + 1) * D], 1.0, None, ALU.add))
            for k, n in enumerate((2, 5)):
                g = modsb[:, n * D:(n + 1) * D]
                link(dve.tensor_scalar(sg[:, k], g, 0.0, 2.0, ALU.is_ge, ALU.mult))
                link(dve.tensor_scalar(sg[:, k], sg[:, k], -1.0, None, ALU.add))
                link(dve.tensor_tensor(g, g, sg[:, k], ALU.mult))
                link(dve.tensor_scalar(g, g, 0.25, None, ALU.max))
                link(dve.tensor_tensor(g, g, sg[:, k], ALU.mult))
            assert chain[0] == SET_MOD
            dve.wait_ge(s_set_act, 5)
            link(dve.tensor_tensor(hc[:, 4], hc[:, 4], sgnc[:], ALU.mult))
            link(dve.tensor_tensor(hc[:, 5], hc[:, 5], hc[:, 0], ALU.mult))
            for k in range(DC):
                link(dve.tensor_scalar(wout_sb[:, 0, k], wout_sb[:, 0, k], hc[:, 5, k:k + 1], None, ALU.mult))
                link(dve.scalar_tensor_tensor(out=wfold[:, k], in0=wout_sb[:, 1, k], scalar=hc[:, 4, k:k + 1],
                                              in1=wout_sb[:, 0, k], op0=ALU.mult, op1=ALU.add))
            for l in range(LAYERS):
                for a in range(4):
                    link(dve.tensor_tensor(tabs[:, :, l, a], rope_sb[:, :, a],
                                           scl[:, l, a].unsqueeze(1).broadcast_to([P, NT, LD]), ALU.mult))
            assert chain[0] == SET_ALL, chain[0]

            def phase_a(b, j):
                xb = xs[:, bass.ds(j, 1)].rearrange("p o t d -> p (o t) d")
                dve.wait_ge(s_x_in, b * 48 + 48)
                for t in range(NT):
                    dve.bn_stats(st1[:, t, :], xb[:, t, :]).then_inc(s_stats1, 1)
                dve.wait_ge(s_stats1, b * NT + NT)
                dve.nop(nofuse=True)
                for t in range(NT):
                    dve.bn_aggr(mv1[:, t, :], st1[:, t, :]).then_inc(s_aggr1, 1)
                dve.wait_ge(s_rstd1, b + 1)
                for t in range(NT):
                    dve.tensor_scalar(hn[:, t, :], xb[:, t, :], mv1[:, t, 0:1], rs1[:, t:t + 1], ALU.subtract, ALU.mult) \
                        .then_inc(s_norm1, 1)
                dve.wait_ge(s_norm1, b * NT + NT)
                dve.tensor_tensor(hn[:], hn[:], modA[:, 1].unsqueeze(1).broadcast_to([P, NT, D]), ALU.mult).then_inc(s_mod1, 1)
                dve.wait_ge(s_mod1, b * 2 + 1)
                dve.tensor_tensor(hn[:], hn[:], modA[:, 0].unsqueeze(1).broadcast_to([P, NT, D]), ALU.add).then_inc(s_mod1, 1)
                for k in range(DC):
                    dve.wait_ge(s_hT_ps, b * 4 + 2 * k + 2)
                    dve.tensor_copy(hT[:, k, HALF:T], psum[:, 2 * k + 1, :]).then_inc(s_hT[1], 1)

                def take_hi(n):
                    dve.wait_ge(s_hi, b * 8 + n + 1)
                    if n >= 2:
                        dve.wait_ge(s_low, b * 8 + n - 1)
                    dve.tensor_tensor(rest[:, n % 2], psum[:, n % 4, :], parts[:, n % 4, 0], ALU.subtract).then_inc(s_rest, 1)
                take_hi(0)
                for n in range(8):
                    if n < 7:
                        take_hi(n + 1)
                    dve.wait_ge(s_mid, b * 8 + n + 1)
                    dve.wait_ge(s_rest, b * 8 + n + 1)
                    dve.tensor_tensor(parts[:, n % 4, 2], rest[:, n % 2], parts[:, n % 4, 1], ALU.subtract).then_inc(s_low, 1)
                for t in range(NT):
                    dve.wait_ge(s_v_ps, b * NT + t + 1)
                    dve.wait_ge(s_v, b * NT + t + 1)
                    dve.tensor_tensor(zt[:, t, :], psum[:, 4 + t % 4, D:D + NEA], bias_ea[:], ALU.add).then_inc(s_z, 1)
                dve.wait_ge(s_z_exp, b + 1)
                dve.tensor_scalar(zt[:], zt[:], 1.0, None, ALU.add).then_inc(s_gate, 1)
                dve.wait_ge(s_gate, b * 3 + 1)
                dve.reciprocal(zt[:, :, 0:H], zt[:, :, 0:H]).then_inc(s_gate, 1)
                dve.tensor_scalar(zt[:, :, H:NEA], zt[:, :, H:NEA], 1e-8, None, ALU.mult).then_inc(s_gate, 1)

                def maximum(g, n):
                    dve.wait_ge(s_s_ps, b * (NG * 64) + (g * 64 + n + 1))
                    dve.tensor_reduce(mx[:, n // 2, n % 2:n % 2 + 1], psum[:, 6 + n % 2, :], AX.X, ALU.max).then_inc(s_max, 1)

                def maxima(g):
                    c0 = g * 5
                    dve.wait_ge(s_max, b * (NG * 64) + (g * 64 + 64))
                    dve.tensor_tensor(m2[:], mx[:, :, 0], mx[:, :, 1], ALU.max).then_inc(s_msplit, 1)
                    dve.wait_ge(s_msplit, b * (NG * 5) + c0 + 1)
                    dve.tensor_copy(m3[:, 0], m2[:]).then_inc(s_msplit, 1)
                    dve.wait_ge(s_msplit, b * (NG * 5) + c0 + 2)
                    dve.tensor_tensor(mr[:], m2[:], m3[:, 0], ALU.subtract).then_inc(s_msplit, 1)
                    dve.wait_ge(s_msplit, b * (NG * 5) + c0 + 3)
                    dve.tensor_copy(m3[:, 1], mr[:]).then_inc(s_msplit, 1)
                    dve.wait_ge(s_msplit, b * (NG * 5) + c0 + 4)
                    dve.tensor_tensor(m3[:, 2], mr[:], m3[:, 1], ALU.subtract).then_inc(s_msplit, 1)
                    dve.wait_ge(s_mT_ps, b * NG + g + 1)
                    dve.wait_ge(s_m_in[g % 2], FREE + b * (48 * 2) + 48 * (g // 2))
                    dve.tensor_copy(mrow[:, g % 2, :], bank_bf16(6)[0:PART * G * NT, 0:P]).then_inc(s_mrow, 1)

                def normalise(g):
                    dve.wait_ge(s_oT_ps, b * NG + g + 1)
                    ov = psum[:, 4:6, :].rearrange("p a (t h w) -> p (a t) h w", h=G, w=VW)
                    c0 = b * (NG * 3) + g * 3
                    dve.tensor_tensor(den[:], ov[:, :, :, DH + 1], zt[:, :, H + G * g:H + G * (g + 1)], ALU.mult).then_inc(s_den, 1)
                    dve.wait_ge(s_den, c0 + 1)
                    dve.tensor_tensor(den[:], ov[:, :, :, DH], den[:], ALU.add).then_inc(s_den, 1)
                    dve.wait_ge(s_den, c0 + 2)
                    dve.reciprocal(den[:], den[:]).then_inc(s_den, 1)
                    dve.wait_ge(s_den, c0 + 3)
                    dve.tensor_tensor(cv[:, :, G * DH * g:G * DH * (g + 1)].rearrange("p t (h i) -> p t h i", i=DH),
                                      ov[:, :, :, 0:DH], den[:].unsqueeze(3).broadcast_to([P, NT, G, DH]), ALU.mult) \
                        .then_inc(s_conv, 1)

                for n in range(2 * G * NT):
                    maximum(0, n)
                maxima(0)
                for g in range(NG):
                    if g + 1 < NG:
                        for n in range(2 * G * NT):
                            maximum(g + 1, n)
                        maxima(g + 1)
                    normalise(g)
                for k in range(DC):
                    dve.wait_ge(s_cvT_ps, b * 4 + 2 * k + 2)
                    dve.tensor_copy(cvT[:, k, HALF:T], psum[:, 2 * k + 1, :]).then_inc(s_cvT[1], 1)
                for t in range(NT):
                    dve.wait_ge(s_att_ps, b * NT + t + 1)
                    dve.tensor_tensor(xb[:, t, :], psum[:, 4 + t % 4, 0:D], xb[:, t, :], ALU.add).then_inc(s_x1, 1)

            def window(i, it, t):
                dve.wait_ge(s_x1, FREE + i * (2 * NT) + 2 * NT)
                for s in range(2):
                    w, n = S[s], it * 2 + s
                    x1 = xs[:, s, bass.ds(t, 1), :].rearrange("p o d -> p (o d)")
                    dve.bn_stats(w["st"][:, 0, :], x1).then_inc(f["ln0_st"], 1)
                    dve.wait_ge(f["ln0_st"], n + 1)
                    dve.nop(nofuse=True)
                    dve.bn_aggr(w["mv"][:], w["st"][:, 0, :]).then_inc(f["ln0_ag"], 1)
                for s in range(2):
                    w, n = S[s], it * 2 + s
                    x1 = xs[:, s, bass.ds(t, 1), :].rearrange("p o d -> p (o d)")
                    dve.wait_ge(f["ln0_rs"], n + 1)
                    dve.tensor_scalar(w["u"][:], x1, w["mv"][:, 0:1], w["rs"][:], ALU.subtract, ALU.mult).then_inc(f["ln0_n"], 1)
                    dve.wait_ge(f["ln0_n"], n + 1)
                    dve.tensor_tensor(w["u"][:], w["u"][:], modF[:, s, 1], ALU.mult).then_inc(f["ln0_m"], 1)
                    dve.wait_ge(f["ln0_m"], n + 1)
                    dve.tensor_tensor(w["u"][:], w["u"][:], modF[:, s, 0], ALU.add).then_inc(f["ln0"], 1)
                for l in range(LAYERS):
                    N = [it * 4 + (2 * l + s) for s in range(2)]
                    for s in range(2):
                        w, n, bk = S[s], N[s], 4 * s
                        uT = w["uT"][:, l]
                        dve.wait_ge(f["uT_ps"], n + 1)
                        dve.tensor_copy(uT[:, P + 1:P + 2], uT[:, 2 * P + 1:2 * P + 2]).then_inc(f["carry"], 1)
                        dve.wait_ge(f["carry"], n + 1)
                        dve.tensor_copy(uT[:, 0:2 * (P + 2)].rearrange("p (a n) -> p a n", a=2)[:, :, 0:P],
                                        psum[:, bk, 0:D].rearrange("p (a n) -> p a n", a=2)).then_inc(f["uT"], 1)
                    for s in range(2):
                        w, n, bk = S[s], N[s], 4 * s
                        sq = w["pT"][:].rearrange("p h k n -> p (h k n)")[:, 0:2 * INNER].rearrange("p (h d) -> p h d", d=LD)
                        qk = psum[:, bk:bk + 2, :].rearrange("p a (h d) -> p a h d", d=LD)
                        flat = w["big"][:].rearrange("p h n -> p (h n)")
                        rot = flat[:, 0:2 * INNER].rearrange("p (a h d) -> p a h d", a=2, d=LD)
                        rs = flat[:, 2 * INNER:4 * INNER].rearrange("p (a h d) -> p a h d", a=2, d=LD)
                        dve.wait_ge(f["tab_in"], it * 32 + 32)
                        dve.wait_ge(f["sq"], n + 1)
                        dve.tensor_reduce(w["ss"][:], sq, AX.X, ALU.add).then_inc(f["ssum"], 1)
                        dve.tensor_tensor(rot, qk, tab[:, l, 0:2].unsqueeze(2).broadcast_to([P, 2, LH, LD]), ALU.mult) \
                            .then_inc(f["ropeC"], 1)
                        hd = LD // 2
                        for lo, hi in ((0, hd), (hd, 0)):
                            ins = dve.tensor_tensor(rs[:, :, :, lo:lo + hd], qk[:, :, :, hi:hi + hd],
                                                    tab[:, l, 2:4, lo:lo + hd].unsqueeze(2).broadcast_to([P, 2, LH, hd]), ALU.mult)
                            if lo:
                                ins.then_inc(f["ropeS"], 1)
                            else:
                                ins.then_inc(f["rope"], 1)
                        dve.wait_ge(f["ropeC"], n + 1)
                        dve.wait_ge(f["ropeS"], n + 1)
                        dve.wait_ge(f["rope"], n * 2 + 1)
                        dve.tensor_tensor(flat[:, 0:2 * INNER], flat[:, 0:2 * INNER], flat[:, 2 * INNER:4 * INNER], ALU.add) \
                            .then_inc(f["rope"], 1)
                        dve.wait_ge(f["rope"], n * 2 + 2)
                        dve.wait_ge(f["rn"], n + 1)
                        dve.tensor_tensor(rot[:, 1], rot[:, 1], w["rn"][:, LH:2 * LH].unsqueeze(2).broadcast_to([P, LH, LD]), ALU.mult) \
                            .then_inc(f["kn"], 1)
                    for s in range(2):
                        w, n, bk = S[s], N[s], 4 * s
                        dve.wait_ge(f["qkT_ps"], n + 1)
                        dve.wait_ge(f["kvprev"], FREE + it * 8)
                        dve.tensor_copy(w["kT"][:, l, :, P:2 * P], psum[:, bk + 1, :].rearrange("p (m q) -> p m q", q=P)) \
                            .then_inc(f["kT"], 1)
                    for s in range(2):
                        w, n, bk = S[s], N[s], 4 * s
                        for h in range(LH):
                            if h % 2 == 0:
                                dve.wait_ge(f["s_ps"], n * (LH // 2) + h // 2 + 1)
                                dve.nop(nofuse=True)
                            ins = dve.tensor_tensor_reduce(out=w["big"][:, h, :],
                                                           in0=psum[:, bk + h // 2, (h % 2) * 2 * P:(h % 2 + 1) * 2 * P],
                                                           in1=maskt[:], scale=w["rn"][:, h:h + 1], scalar=-3.4e38,
                                                           op0=ALU.add, op1=ALU.max, accum_out=w["mx"][:, h:h + 1])
                        ins.then_inc(f["sm"], 1)
                        dve.wait_ge(f["sm"], FREE + n + 1)
                        dve.tensor_scalar(w["mx"][:], w["mx"][:], -1.0, None, ALU.mult).then_inc(f["neg"], 1)
                    for s in range(2):
                        w, n, bk = S[s], N[s], 4 * s
                        dve.wait_ge(f["exp"], n + 1)
                        dve.reciprocal(w["rz"][:], w["z"][:]).then_inc(f["rz"], 1)
                        dve.wait_ge(f["rz"], n + 1)
                        for h in range(LH):
                            ins = dve.tensor_scalar(w["big"][:, h, :], w["big"][:, h, :], w["rz"][:, h:h + 1], None, ALU.mult)
                        ins.then_inc(f["pn"], 1)
                    for s in range(2):
                        w, n, bk = S[s], N[s], 4 * s
                        for m in (1, 3):
                            dve.wait_ge(f["pT_ps"], n * 4 + m + 1)
                            dve.tensor_copy(w["pT"][:, 2 * m:2 * m + 2], psum[:, bk + m, :]
                                            .rearrange("p (h k n) -> p h k n", h=2, k=2)).then_inc(f["pT_d"], 1)
                    for s in range(2):
                        w, n, bk = S[s], N[s], 4 * s
                        dve.wait_ge(f["wo_ps"], n + 1)
                        dve.tensor_tensor(w["u"][:], psum[:, bk + 1, 0:D], w["u"][:], ALU.add).then_inc(f["u1"], 1)
                    for s in range(2):
                        w, n, bk = S[s], N[s], 4 * s
                        dve.wait_ge(f["u1"], n + 1)
                        dve.bn_stats(w["st"][:, 0, :], w["u"][:, 0:P]).then_inc(f["ln_st"], 1)
                        dve.wait_ge(f["sh"], n * 32 + 32)
                        dve.bn_stats(w["st"][:, 1, :], w["ush"][:]).then_inc(f["ln_st"], 1)
                        dve.wait_ge(f["ln_st"], n * 2 + 2)
                        dve.nop(nofuse=True)
                        dve.bn_aggr(w["mv"][:], w["st"][:].rearrange("p a n -> p (a n)")).then_inc(f["ln_ag"], 1)
                    for s in range(2):
                        w, n, bk = S[s], N[s], 4 * s
                        dve.wait_ge(f["ln_rs"], n + 1)
                        for k, src in ((0, w["u"][:, 0:P]), (1, w["ush"][:])):
                            dve.tensor_scalar(w["hl"][:, k * P:(k + 1) * P], src, w["mv"][:, 0:1], w["rs"][:], ALU.subtract, ALU.mult) \
                                .then_inc(f["hl"], 1)
                        dve.wait_ge(f["crow"], n * 16 + 16)
                        dve.wait_ge(f["hl"], n * 2 + 2)
                        dve.tensor_tensor(w["u"][:], w["u"][:], b2_sb[:, l], ALU.add).then_inc(f["ub"], 1)
                    for s in range(2):
                        w, n, bk = S[s], N[s], 4 * s
                        dve.wait_ge(f["hl_ps"], n + 1)
                        for k in range(DC):
                            dve.tensor_scalar(w["hlT"][:, k, :], psum[:, bk, k * P:(k + 1) * P], lnv[:, l, 0, k:k + 1],
                                              lnv[:, l, 1, k:k + 1], ALU.mult, ALU.add).then_inc(f["hlT"], 1)
                    for s in range(2):
                        w, n, bk = S[s], N[s], 4 * s
                        gl = w["pT"][:].rearrange("p h k n -> p (h k) n")
                        dve.wait_ge(f["gelu"], n * FC + FC)
                        for cc in range(FC):
                            rows, m = (P if cc < FC - 1 else FR), FC + cc
                            dve.scalar_tensor_tensor(out=gl[0:rows, cc, :],
                                                     in0=psum[0:rows, bk + 1 + m // 4, (m % 4) * P:(m % 4 + 1) * P],
                                                     scalar=b1_sb[0:rows, l, 0, cc:cc + 1], in1=gl[0:rows, cc, :],
                                                     op0=ALU.add, op1=ALU.mult).then_inc(f["act"], 1)
                    for s in range(2):
                        w, n, bk = S[s], N[s], 4 * s
                        dve.wait_ge(f["w2_ps"], n + 1)
                        dve.wait_ge(f["ub"], n + 1)
                        dve.tensor_tensor(w["u"][:], psum[:, bk, 0:D], w["u"][:], ALU.add).then_inc(f["u2"], 1)
                for s in range(2):
                    w, n = S[s], it * 2 + s
                    x1 = xs[:, s, bass.ds(t, 1), :].rearrange("p o d -> p (o d)")
                    dve.wait_ge(f["u2"], it * 4 + 2 + s + 1)
                    dve.wait_ge(f["out"], FREE + it * 32)
                    dve.tensor_tensor(w["o"][:], w["u"][:], modF[:, s, 2], ALU.mult).then_inc(f["og"], 1)
                    dve.wait_ge(f["og"], n + 1)
                    dve.tensor_tensor(w["o"][:], w["o"][:], x1, ALU.add).then_inc(f["oo"], 1)

            with dve.Fori(0, B // 2) as i:
                with dve.Fori(0, 2) as j:
                    phase_a(i * 2 + j, j)
                dve.wait_ge(f["zero"], i * 10 + 10)
                dve.nop(nofuse=True)
                with dve.Fori(0, NT) as t:
                    window(i, i * NT + t, t)

        @block.gpsimd
        def _(gp):
            for s in (s_x1, f["out"], f["sm"], f["kvprev"], *s_parts_out, *s_m_in):
                gp.sem_inc(s, FREE)
            gp.memset(ident[:], 0.0).then_inc(s_id, 1)
            gp.wait_ge(s_id, 1)
            gp.nop(nofuse=True)
            gp.affine_select(out=ident[:], in_=ident[:], compare_op=ALU.not_equal, fill=1.0, base=0,
                             pattern=[[-1, P]], channel_multiplier=1).then_inc(s_id, 1)
            gp.wait_ge(s_id, 2)
            gp.nop(nofuse=True)
            gp.tensor_copy(identb[:], ident[:]).then_inc(s_id, 1)
            gp.memset(neghalf[:], -0.5).then_inc(s_id, 1)
            gp.wait_ge(s_id, ID_ALL)
            gp.wait_ge(s_set_dve, SET_ALL)
            gp.wait_ge(s_set_out, 16 * (1 + LAYERS))
            gp.nop(nofuse=True)

            def phase_a(b):
                gp.wait_ge(s_aggr1, b * NT + NT)
                gp.nop(nofuse=True)
                gp.tensor_scalar(rs1[:], mv1[:, :, 1], LN_EPS, 1.0, ALU.add, ALU.mult).then_inc(s_eps1, 1)
                gp.wait_ge(s_eps1, b + 1)
                gp.nop(nofuse=True)
                gp.tensor_tensor(rs1[:], rs1[:], neghalf[:, 0:NT], ALU.pow).then_inc(s_rstd1, 1)
                gp.tensor_tensor(wga[:], wfold[:], modA[:, 2].unsqueeze(1).broadcast_to([P, DC, D]), ALU.mult).then_inc(s_wga, 1)
                gp.wait_ge(s_wga, b + 1)
                gp.nop(nofuse=True)
                gp.memset(stack[KS:KS + PART, :, 1], -1.0).then_inc(s_ones, 1)
                gp.wait_ge(s_ones, b * 3 + 1)
                gp.nop(nofuse=True)
                gp.memset(vg[:, :, :, :, DH:VW], 0.0).then_inc(s_ones, 1)
                gp.wait_ge(s_ones, b * 3 + 2)
                gp.nop(nofuse=True)
                gp.memset(vg[:, :, :, :, DH + 1:DH + 2], 1.0).then_inc(s_ones, 1)
                gp.wait_ge(s_ones, b * 3 + 3)
                gp.wait_ge(s_gate, b * 3 + 3)
                gp.wait_ge(s_v, b * NT + NT)
                gp.nop(nofuse=True)
                for g in range(NG):
                    if g > 1:
                        gp.wait_ge(s_pv, b * (NG * 16) + (g - 1) * 16)
                        gp.nop(nofuse=True)
                    e = zt[:, :, G * g:G * (g + 1)]
                    gp.tensor_tensor(vg[:, g % 2, :, :, 0:DH], vt[:, :, G * DH * g:G * DH * (g + 1)].rearrange("p t (h i) -> p t h i", i=DH),
                                     e.unsqueeze(3).broadcast_to([P, NT, G, DH]), ALU.mult).then_inc(s_vg, 1)
                    gp.tensor_copy(vg[:, g % 2, :, :, DH], e).then_inc(s_vg, 1)

            def window(it):
                for s in range(2):
                    w, n = S[s], it * 2 + s
                    gp.wait_ge(f["ln0_ag"], n + 1)
                    gp.nop(nofuse=True)
                    gp.tensor_scalar(w["rs"][:], w["mv"][:, 1:2], LN_EPS, 1.0, ALU.add, ALU.mult).then_inc(f["ln0_eps"], 1)
                    gp.wait_ge(f["ln0_eps"], n + 1)
                    gp.nop(nofuse=True)
                    gp.tensor_tensor(w["rs"][:], w["rs"][:], neghalf[:, 0:1], ALU.pow).then_inc(f["ln0_rs"], 1)
                for l in range(LAYERS):
                    N = [it * 4 + (2 * l + s) for s in range(2)]
                    for s in range(2):
                        w, n = S[s], N[s]
                        gp.wait_ge(f["ssum"], n + 1)
                        gp.nop(nofuse=True)
                        gp.tensor_scalar(w["ss"][:], w["ss"][:], 1e-24, None, ALU.max).then_inc(f["clip"], 1)
                        gp.wait_ge(f["clip"], n * 2 + 1)
                        gp.nop(nofuse=True)
                        gp.tensor_tensor(w["rn"][:], w["ss"][:], neghalf[:], ALU.pow).then_inc(f["clip"], 1)
                        gp.wait_ge(f["clip"], n * 2 + 2)
                        gp.nop(nofuse=True)
                        gp.tensor_scalar(w["rn"][:, 0:LH], w["rn"][:, 0:LH], 8.0, 1.0, ALU.mult, ALU.mult).then_inc(f["rn"], 1)
                    for s in range(2):
                        w, n = S[s], N[s]
                        gp.wait_ge(f["o_ps"], n + 1)
                        gp.nop(nofuse=True)
                        gp.tensor_copy(w["v"][:, l, 0, :], w["v"][:, l, 1, :]).then_inc(f["kvprev"], 1)
                        gp.tensor_copy(w["kT"][:, l, :, 0:P], w["kT"][:, l, :, P:2 * P]).then_inc(f["kvprev"], 1)
                    for s in range(2):
                        w, n = S[s], N[s]
                        gp.wait_ge(f["ln_ag"], n + 1)
                        gp.nop(nofuse=True)
                        gp.tensor_scalar(w["rs"][:], w["mv"][:, 1:2], LN_EPS, 1.0, ALU.add, ALU.mult).then_inc(f["ln_eps"], 1)
                        gp.wait_ge(f["ln_eps"], n + 1)
                        gp.nop(nofuse=True)
                        gp.tensor_tensor(w["rs"][:], w["rs"][:], neghalf[:, 0:1], ALU.pow).then_inc(f["ln_rs"], 1)

            with gp.Fori(0, B // 2) as i:
                with gp.Fori(0, 2) as j:
                    phase_a(i * 2 + j)
                gp.wait_ge(s_x1, FREE + i * (2 * NT) + 2 * NT)
                gp.nop(nofuse=True)
                for s in range(2):
                    w = S[s]
                    for k, buf in enumerate((w["uT"], w["kT"], w["v"], w["qz"], w["crow"])):
                        gp.memset(buf[:], 0.0).then_inc(f["zero"], 1)
                        gp.wait_ge(f["zero"], i * 10 + (5 * s + k + 1))
                        gp.nop(nofuse=True)
                with gp.Fori(0, NT) as t:
                    window(i * NT + t)


def _constants():
    n = np.float32
    half = np.arange(0, LD, 2, dtype=n)
    inv = (n(1.0) / n(10000.0) ** (half / n(LD))).astype(n)
    t = np.arange(T, dtype=n)
    fr = t[:, None] * inv[None, :]
    fr = np.concatenate([fr, fr], -1)
    base = (half + n(0.4 * LD)) / n(1.4 * LD)
    scale = base[None, :] ** ((t - T // 2) / n(P // 2))[:, None]
    scale = np.concatenate([scale, scale], -1).astype(n)
    cos, sin = np.cos(fr.astype(np.float64)), np.sin(fr.astype(np.float64))
    sign = np.concatenate([-np.ones(LD // 2), np.ones(LD // 2)])
    rope = np.stack([cos * scale, cos / scale, sign * sin * scale, sign * sin / scale], 1).astype(n)
    rope = np.ascontiguousarray(rope.reshape(NT, P, 4, LD).transpose(1, 0, 2, 3))
    q, k = np.arange(P)[:, None], np.arange(2 * P)[None, :] - P
    keep = (k <= q) & (k >= q - P)
    mask = np.stack([keep & ((k >= 0) | (w > 0)) for w in range(NT)])
    return rope, np.where(mask, 0.0, MASKED).astype(n)


def kernel(**inputs):
    import concourse.bacc as _bacc
    from concourse.bass_utils import run_bass_kernel_spmd as _run

    a = {k: np.ascontiguousarray(v) for k, v in inputs.items()}
    rope, mask = _constants()
    wout = a["L0_attn_Wout"]
    heads = np.stack([a["L0_attn_" + k] for k in ("beta_p", "iv_p", "ov_p", "chi")])
    heads = np.repeat(heads, DH, axis=1).reshape(4, DC, P).transpose(2, 0, 1)
    sgn = np.where(np.arange(D) % DH < DH // 2, 1.0, -1.0).astype(np.float32).reshape(DC, P).T
    swapped = wout.reshape(H, 2, DH // 2, D)[:, ::-1].reshape(D, D)
    arrays = {
        "x": a["L0_attn_x"], "Wa": a["L0_attn_Wa"], "ba": a["L0_attn_ba"], "We": a["L0_attn_We"], "be": a["L0_attn_be"],
        "Wi": a["L0_attn_Wi"], "Wo": a["L0_attn_Wo"], "Wv": a["L0_attn_Wv"], "Wout": wout, "Wout_sw": swapped,
        "head_vec": heads, "sgn": sgn, "wqkv": a["L0_ffn_wqkv"], "q_scale": a["L0_ffn_q_scale"],
        "k_scale": a["L0_ffn_k_scale"], "wo": a["L0_ffn_wo"], "ln_g": a["L0_ffn_ln_g"], "ln_b": a["L0_ffn_ln_b"],
        "w1": a["L0_ffn_w1"], "b1": a["L0_ffn_b1"], "w2": a["L0_ffn_w2"], "b2": a["L0_ffn_b2"], "c": a["L0_c"],
        "wmod": a["L0_wmod"], "rope": rope, "mask": mask,
    }
    arrays = {k: np.ascontiguousarray(v) for k, v in arrays.items()}
    nc = _bacc.Bacc("TRN2", target_bir_lowering=False, num_devices=1)
    aps = {k: nc.dram_tensor("in_" + k, v.shape, mybir.dt.from_np(v.dtype), kind="ExternalInput").ap()
           for k, v in arrays.items()}
    aps["out"] = nc.dram_tensor("out_x", (B, T, D), F32, kind="ExternalOutput").ap()
    build(nc, **aps)
    r = _run(nc, [{"in_" + k: v for k, v in arrays.items()}], core_ids=[0])
    return r.results[0]["out_x"]
```

```python
from contextlib import ExitStack

import numpy as np

import concourse.bass as bass
from concourse import mybir

F32 = mybir.dt.float32
BF16 = mybir.dt.bfloat16
ALU = mybir.AluOpType
ACT = mybir.ActivationFunctionType
AX = mybir.AxisListType

P = 128
B, T, D = 8, 1024, 256
NT = T // P
DC = D // P
HALF = 512
NH = T // HALF
H, DH = 16, 16
G = 4
NG = H // G
PART = 3
PAIRS_Q = (0, 0, 0, 1, 1, 2)
PAIRS_K = (0, 1, 2, 0, 1, 0)
KS = DH * len(PAIRS_Q)
NU = NG * NH
TU = G * NT // NH
MU = TU * NH
BLOCKS = 8
LN1_ALL = 2 + NT
AHEAD = MU + 12
NEXT = -(-(NU * MU - AHEAD) // 4)
CV_BANKS = (4, 5, 0, 1)
STATS = 4 * NT + 6
STACK_IN = 16 * 2 * len(PAIRS_Q)
VW = 32
NEA = 2 * H
LAYERS, LH, LD = 2, 8, 64
INNER = LH * LD
HID = 682
FC = -(-HID // P)
FR = HID - (FC - 1) * P
LN_EPS = 1e-5
MASKED = -1e25
FREE = 1
SET_SILU, SET_ANGLE, SET_MOD, SET_ALL, ID_ALL = 3, 7, 23, 37, 7


def build(nc, x, Wa, ba, We, be, Wi, Wo, Wv, Wout, Wout_sw, head_vec, sgn, wqkv, q_scale, k_scale,
          wo, ln_g, ln_b, w1, b1, w2, b2, c, wmod, rope, mask, out):
    mod_d = nc.dram_tensor("mod_d", (B, 6 * D), F32, kind="Internal").ap()
    tab_d = nc.dram_tensor("tab_d", (NT, P, LAYERS * 4 * LD), F32, kind="Internal").ap()
    x1_d = nc.dram_tensor("x1_d", (B, T, D), F32, kind="Internal").ap()
    parts_d = nc.dram_tensor("parts_d", (2, PART, D, T), BF16, kind="Internal").ap()

    ctx = ExitStack()
    with ctx:
        def sem(name):
            return ctx.enter_context(nc.semaphore(name))

        def res(name, shape, dt=F32):
            return ctx.enter_context(nc.sbuf_tensor(name, shape, dt))

        ident = res("ident", [P, P])
        turned = res("turned", [P, P])
        identb = res("identb", [P, P], BF16)
        wi_sb = res("wi_sb", [P, 2, DC, D])
        wvea = res("wvea", [P, DC, D + NEA])
        wfold = res("wfold", [P, DC, D])
        wga = res("wga", [P, DC, D])
        bias_ea = res("bias_ea", [P, NEA])
        wqkv_sb = res("wqkv_sb", [P, LAYERS, DC, 3 * INNER])
        wo_sb = res("wo_sb", [P, LAYERS, INNER // P, D])
        w1_sb = res("w1_sb", [P, LAYERS, DC, 2 * HID])
        w2_sb = res("w2_sb", [P, LAYERS, FC, D])
        b1_sb = res("b1_sb", [P, LAYERS, 2, FC])
        b2_sb = res("b2_sb", [P, LAYERS, D])
        lnv = res("lnv", [P, LAYERS, 2, DC])
        neghalf = res("neghalf", [P, 2 * LH])

        def nested(stack):
            return lambda name, shape, dt=F32: stack.enter_context(nc.sbuf_tensor(name, shape, dt))

        with ExitStack() as scope_a:
            tmp = nested(scope_a)
            modA = tmp("modA", [P, 3, D])
            hn = tmp("hn", [P, NT, D])
            xr = tmp("xr", [P, NT, D])
            st1 = tmp("st1", [P, NT, 6])
            mv1 = tmp("mv1", [P, NT, 2])
            rs1 = tmp("rs1", [P, NT])

            with ExitStack() as scope:
                tmp = nested(scope)
                wmod_sb = tmp("wmod_sb", [P, DC, 6 * D])
                cT = tmp("cT", [P, DC, B])
                ce = tmp("ce", [P, DC, B])
                modsb = tmp("modsb", [B, 6 * D])
                sg = tmp("sg", [B, 2, D])
                hv = tmp("hv", [P, 4, DC])
                he = tmp("he", [P, 4, DC])
                hc = tmp("hc", [P, 6, DC])
                sgnc = tmp("sgnc", [P, DC])
                wout_sb = tmp("wout_sb", [P, 2, DC, D])
                rope_sb = tmp("rope_sb", [P, NT, 4, LD])
                scl = tmp("scl", [P, LAYERS, 4, LD])
                tabs = tmp("tabs", [P, NT, LAYERS, 4, LD])

            tmp = nested(scope_a)
            hT = tmp("hT", [P, DC, T])
            cv = tmp("cv", [P, NT, D])
            parts = tmp("parts", [P, 4, PART, HALF], BF16)
            rest = tmp("rest", [P, 2, HALF])
            o_sb = tmp("o_sb", [P, HALF])
            stack = tmp("stack", [P, 2, 2, NH, G, HALF], BF16)
            vg = tmp("vg", [P, 2, NT, G, VW])
            pr = tmp("pr", [P, 2, G, HALF])
            zt = tmp("zt", [P, NT, NEA])
            mx = tmp("mx", [P, 2, TU, NH])
            m2 = tmp("m2", [P, TU])
            mr = tmp("mr", [P, TU])
            m3 = tmp("m3", [P, PART, TU], BF16)
            mrow = tmp("mrow", [PART * TU, 2, P], BF16)
            den = tmp("den", [P, NT // NH, G])
        vt, cvT = hn, hT

        with ExitStack() as scope:
            tmp = nested(scope)
            tab = tmp("tab", [P, LAYERS, 4, LD])
            xs = tmp("xs", [P, 2, NT, D])
            modF = tmp("modF", [P, 2, 3, D])
            S = [dict(
                u0=tmp(f"u0_s{s}", [P, D]),
                u=tmp(f"u_s{s}", [P, D]),
                mask=tmp(f"mask_s{s}", [P, 2 * P]),
                x1n=tmp(f"x1n_s{s}", [P, 6]),
                uT=tmp(f"uT_s{s}", [P, LAYERS, 2 * P + 4]),
                big=tmp(f"big_s{s}", [P, LH, 2 * P]),
                pT=tmp(f"pT_s{s}", [P, LH, 2, P]),
                qz=tmp(f"qz_s{s}", [P, LH, P]),
                kT=tmp(f"kT_s{s}", [P, LAYERS, LH // 2, 2 * P]),
                v=tmp(f"v_s{s}", [P, LAYERS, 2, INNER]),
                oT=tmp(f"oT_s{s}", [P, INNER // P, P]),
                ush=tmp(f"ush_s{s}", [P, P]),
                crow=tmp(f"crow_s{s}", [1, LAYERS, P]),
                hl=tmp(f"hl_s{s}", [P, D]),
                hlT=tmp(f"hlT_s{s}", [P, DC, P]),
                st=tmp(f"st_s{s}", [P, 2, 6]),
                mv=tmp(f"mv_s{s}", [P, 2]),
                mv0=tmp(f"mv0_s{s}", [P, 2]),
                rs0=tmp(f"rs0_s{s}", [P, 1]),
                rs=tmp(f"rs_s{s}", [P, 1]),
                ss=tmp(f"ss_s{s}", [P, 2 * LH]),
                rn=tmp(f"rn_s{s}", [P, 2 * LH]),
                mx=tmp(f"mxl_s{s}", [P, LH]),
                z=tmp(f"z_s{s}", [P, LH]),
                rz=tmp(f"rz_s{s}", [P, LH]),
                o=tmp(f"o_s{s}", [P, D]),
            ) | {"bk": 4 * s} for s in range(2)]

        psum = ctx.enter_context(nc.psum_tensor("psum", [P, 8, HALF], F32))

        def bank_bf16(k):
            return psum[:, k, :].bitcast(BF16)

        s_wts = sem("s_wts")
        s_wf = sem("s_wf")
        s_id = sem("s_id")
        s_set_act = sem("s_set_act")
        s_set_dve = sem("s_set_dve")
        s_set_pe = sem("s_set_pe")
        s_set_out = sem("s_set_out")
        s_x_in = sem("s_x_in")
        s_mod_in = sem("s_mod_in")
        s_stats1 = sem("s_stats1")
        s_ln1 = sem("s_ln1")
        s_hn = sem("s_hn")
        s_wga = sem("s_wga")
        s_ones = sem("s_ones")
        s_hT_ps = sem("s_hT_ps")
        s_hT = sem("s_hT")
        s_proj = sem("s_proj")
        s_part = sem("s_part")
        s_parts_out = [sem(f"s_parts_out{k}") for k in range(4)]
        s_v_ps = sem("s_v_ps")
        s_v = sem("s_v")
        s_z = sem("s_z")
        s_z_exp = sem("s_z_exp")
        s_gate = sem("s_gate")
        s_stack_in = [sem(f"s_stack_in{k}") for k in range(2)]
        s_s_ps = sem("s_s_ps")
        s_max = sem("s_max")
        s_msplit = sem("s_msplit")
        s_mT_ps = sem("s_mT_ps")
        s_mrow = sem("s_mrow")
        s_m_in = [sem(f"s_m_in{k}") for k in range(2)]
        s_vg = sem("s_vg")
        s_st_ps = sem("s_st_ps")
        s_exp = sem("s_exp")
        s_pv = sem("s_pv")
        s_osb = sem("s_osb")
        s_oT_ps = sem("s_oT_ps")
        s_den = sem("s_den")
        s_conv = sem("s_conv")
        s_cvT_ps = sem("s_cvT_ps")
        s_cvT = [sem(f"s_cvT_{e}") for e in ("act", "dve")]
        s_att_ps = sem("s_att_ps")
        s_x1 = sem("s_x1")
        s_xr_in = sem("s_xr_in")
        s_x1_out = sem("s_x1_out")
        s_xs0_in = sem("s_xs0_in")
        s_xs_in = sem("s_xs_in")
        s_tab_in = sem("s_tab_in")
        s_zero = sem("s_zero")
        for s in range(2):
            S[s].update({"s_" + n: sem(f"s{s}_{n}") for n in (
                "mask_in ln0_ag ln0_rs ln0 uT_ps carry uT qkv sq vev ssum "
                "rn rope kn qkT_ps qz kT s_ps sm exp rz pn pT_ps pT o_ps oT kvprev "
                "wo_ps u1 sh_ps sh ub ln_ag ln_rs hl hl_ps hlT g_ps gelu act w2_ps u2 "
                "oo out").split()})
        X, Y = S

        def half(l, it, do, prev=True):
            before = (1 - l, it - 1 if l == 0 else it)
            for step in ("Xw2 Ys2 XuT Ys3 Xq01 Yp Xq2a Ywoa Ywob Xt Ysh Xq2b Xs0 Xs1 Xs2 Yh Xs3 Yw1a Yw1b "
                         "Xp | Yw2 Xwoa YuT Xwob Yq0a Xsh Yq0b Yq2a Xh Yq2b Xw1a Yt Xw1b Ys0 Ys1").split():
                if step == "|":
                    prev, before = True, (l, it)
                elif step[0] == "X":
                    do(step[1:], X, l, it)
                elif prev:
                    do(step[1:], Y, *before)

        def interleave(score, tile, rows, behind=0):
            tiles = iter(range(NT))
            for _ in range(5):
                tile(next(tiles))
            for q in range(AHEAD):
                if q == MU + 4:
                    rows()
                score(q)
                if q - behind in (5, 11, 17):
                    tile(next(tiles))

        block = ctx.enter_context(nc.Block())

        loads = [0, 0]

        @block.sync
        def _(sp):
            def load(dst, src):
                loads[0] += 1
                sp.dma_start(dst, src).then_inc(s_wts, 16)

            def load_f(dst, src):
                loads[1] += 1
                sp.dma_start(dst, src).then_inc(s_wf, 16)

            def x_load(dst, b):
                return sp.dma_start(dst[:].unsqueeze(1), x.rearrange("b (t p) d -> p b t d", p=P)[:, bass.ds(b, 1)])

            x_load(hn, 0).then_inc(s_x_in, 16)
            with nc.allow_non_contiguous_dma("small set-up vectors"):
                for k in range(DC):
                    load(cT[:, k, :], c.rearrange("b (k p) -> k p b", p=P)[k])
                load(wmod_sb[:], wmod.rearrange("(k p) n -> p k n", p=P))
                load(hv[:], head_vec)
                load(sgnc[:], sgn)
                load(wout_sb[:, 0], Wout.rearrange("(k p) n -> p k n", p=P))
                load(wout_sb[:, 1], Wout_sw.rearrange("(k p) n -> p k n", p=P))
                load(rope_sb[:], rope)
                for l in range(LAYERS):
                    for n, v in ((0, q_scale), (1, k_scale)):
                        load(scl[:, l, n, :], v[l].partition_broadcast(P))
                        load(scl[:, l, 2 + n, 0:LD // 2], v[l, LD // 2:LD].partition_broadcast(P))
                        load(scl[:, l, 2 + n, LD // 2:LD], v[l, 0:LD // 2].partition_broadcast(P))
                load(wi_sb[:, 0], Wi.rearrange("(k p) n -> p k n", p=P))
                load(wi_sb[:, 1], Wo.rearrange("(k p) n -> p k n", p=P))
                load(wvea[:, :, 0:D], Wv.rearrange("(k p) n -> p k n", p=P))
                load(wvea[:, :, D:D + H], We.rearrange("(k p) n -> p k n", p=P))
                load(wvea[:, :, D + H:D + NEA], Wa.rearrange("(k p) n -> p k n", p=P))
                load(bias_ea[:, 0:H], be.partition_broadcast(P))
                load(bias_ea[:, H:NEA], ba.partition_broadcast(P))
            sp.wait_ge(s_set_dve, SET_MOD)
            sp.nop(nofuse=True)
            sp.dma_start(mod_d, modsb[:]).then_inc(s_set_out, 16)
            sp.wait_ge(s_set_dve, SET_ALL)
            sp.nop(nofuse=True)
            for l in range(LAYERS):
                sp.dma_start(tab_d.rearrange("t p (l n) -> l p t n", l=LAYERS)[l],
                             tabs[:, :, l].rearrange("p t a d -> p t (a d)")).then_inc(s_set_out, 16)
            sp.wait_ge(s_set_out, 16 * (1 + LAYERS))
            sp.nop(nofuse=True)

            md = mod_d.rearrange("b n -> (b n)")

            def modulation(b):
                sp.dma_start(modA[:].rearrange("p a d -> p (a d)"),
                             md[bass.ds(b * (6 * D), 3 * D)].partition_broadcast(P)).then_inc(s_mod_in, 16)

            def next_x(b):
                sp.wait_ge(s_wga, b)
                sp.nop(nofuse=True)
                modulation(b)
                sp.wait_ge(s_vg, b * (2 * NG))
                sp.nop(nofuse=True)
                x_load(hn, b).then_inc(s_x_in, 16)

            def split_out(b):
                for n in range(BLOCKS):
                    sp.wait_ge(s_part, b * (4 * BLOCKS) + (4 * n + 4))
                    sp.nop(nofuse=True)
                    qk, m, h = n // 4, (n // 2) % 2, n % 2
                    sp.dma_start(parts_d[qk, :, m * P:(m + 1) * P, h * HALF:(h + 1) * HALF]
                                 .rearrange("a p t -> p a t"), parts[:, n % 4]).then_inc(s_parts_out[n % 4], 16)
                for k in range(4):
                    sp.wait_ge(s_parts_out[k], FREE + b * 32 + 32)
                    sp.nop(nofuse=True)

            def stacks(b, g, prev=True):
                if g > 1:
                    sp.wait_ge(s_st_ps, b * (NU * 16) + 32 * (g - 1))
                    sp.nop(nofuse=True)
                elif prev:
                    sp.wait_ge(s_st_ps, b * (NU * 16) + 32 * (g - 1))
                    sp.nop(nofuse=True)
                for qk, order in ((0, PAIRS_Q), (1, PAIRS_K)):
                    for s, part in enumerate(order):
                        sp.dma_start(
                            stack[s * DH:(s + 1) * DH, g % 2, qk],
                            parts_d[qk, part, g * G * DH:(g + 1) * G * DH, :].rearrange("(h i) (a t) -> i a h t", i=DH, a=NH)
                        ).then_inc(s_stack_in[g % 2], 16)

            def maxima_in(b, u):
                sp.wait_ge(s_mrow, b * NU + u + 1)
                sp.nop(nofuse=True)
                for s in range(PART):
                    sp.dma_start(
                        stack[KS + s:KS + s + 1, (u // 2) % 2, 0, u % 2].rearrange("o h (a q) -> o (h a) q", q=P),
                        mrow[s * TU:(s + 1) * TU, u % 2, :]
                    ).then_inc(s_m_in[u % 2], 16)

            def x_in(b, prev=True):
                if prev:
                    sp.wait_ge(s_x1_out, b * 16)
                    sp.nop(nofuse=True)
                x_load(xr, b).then_inc(s_xr_in, 16)

            def x1_out(b):
                sp.wait_ge(s_x1, FREE + b * NT + NT)
                sp.nop(nofuse=True)
                sp.dma_start(x1_d.rearrange("b (t p) d -> p b t d", p=P)[:, bass.ds(b, 1)], xr[:].unsqueeze(1)).then_inc(s_x1_out, 16)

            def batch(b, more):
                for u in range(1, NU):
                    maxima_in(b, u)
                    if u % 2 == 0 and u < NU - 2:
                        stacks(b, u // 2 + 1)
                    if u == NU - 4 and more:
                        next_x(b + 1)
                if more:
                    split_out(b + 1)
                    stacks(b + 1, 0)
                    stacks(b + 1, 1)
                    maxima_in(b + 1, 0)
                x1_out(b)
                if more:
                    x_in(b + 1)
            modulation(0)
            x_in(0, prev=False)
            split_out(0)
            for g in range(2):
                stacks(0, g, prev=False)
            maxima_in(0, 0)
            with nc.allow_non_contiguous_dma("small set-up vectors"):
                for l in range(LAYERS):
                    load_f(wqkv_sb[:, l], wqkv[l].rearrange("(k p) n -> p k n", p=P))
                    load_f(wo_sb[:, l], wo[l].rearrange("(k p) n -> p k n", p=P))
                    load_f(w1_sb[:, l], w1[l].rearrange("(k p) n -> p k n", p=P))
                    load_f(w2_sb[:, l, 0:FC - 1], w2[l, 0:(FC - 1) * P].rearrange("(k p) n -> p k n", p=P))
                    load_f(w2_sb[0:FR, l, FC - 1], w2[l, (FC - 1) * P:HID])
                    for n in range(2):
                        o = n * HID
                        load_f(b1_sb[:, l, n, 0:FC - 1], b1[l, o:o + (FC - 1) * P].rearrange("(k p) -> p k", p=P))
                        load_f(b1_sb[0:FR, l, n, FC - 1:FC], b1[l, o + (FC - 1) * P:o + HID].unsqueeze(1))
                    load_f(b2_sb[:, l], b2[l].partition_broadcast(P))
                    load_f(lnv[:, l, 0], ln_g[l].rearrange("(k p) -> p k", p=P))
                    load_f(lnv[:, l, 1], ln_b[l].rearrange("(k p) -> p k", p=P))
            with sp.Fori(0, B - 1) as b:
                batch(b, True)
            batch(B - 1, False)
            sp.wait_ge(s_x1_out, B * 16)
            sp.nop(nofuse=True)

            with sp.Fori(0, B // 2) as i:
                for w in S:
                    sp.wait_ge(w["s_out"], FREE + i * (16 * NT))
                    sp.nop(nofuse=True)
                for s in range(2):
                    sp.dma_start(modF[:, s].rearrange("p a d -> p (a d)"),
                                 md[bass.ds(i * (12 * D) + (6 * s + 3) * D, 3 * D)].partition_broadcast(P)).then_inc(s_xs0_in, 16)
                for lo, hi, done in ((0, 1, s_xs0_in), (1, NT, s_xs_in)):
                    for s in range(2):
                        sp.dma_start(xs[:, s, lo:hi].unsqueeze(1),
                                     x1_d.rearrange("b (t p) d -> p b t d", p=P)[:, bass.ds(i * 2 + s, 1), lo:hi]).then_inc(done, 16)
                sp.wait_ge(s_zero, i * 8 + 10)
                sp.nop(nofuse=True)

                def tables(t, it, wait):
                    if wait:
                        for w in S:
                            sp.wait_ge(w["s_kn"], it * 2)
                            sp.nop(nofuse=True)
                    sp.dma_start(tab[:].rearrange("p l a d -> p (l a d)"),
                                 tab_d[bass.ds(t, 1)].rearrange("o p n -> p (o n)")).then_inc(s_tab_in, 16)

                def masks(w, t, it, wait):
                    if wait:
                        sp.wait_ge(w["s_sm"], it * 8)
                        sp.nop(nofuse=True)
                    sp.dma_start(w["mask"][:], mask[bass.ds(t, 1)].rearrange("o p n -> p (o n)")).then_inc(w["s_mask_in"], 16)

                def store(w, s, t, it):
                    sp.wait_ge(w["s_oo"], it * 2 + 2)
                    sp.nop(nofuse=True)
                    sp.dma_start(out.rearrange("(i j) (t p) d -> i j t p d", j=2, p=P)[bass.ds(i, 1), s, bass.ds(t, 1)]
                                 .rearrange("o q p d -> p (o q d)"), w["o"][:]).then_inc(w["s_out"], 16)

                def window(t, it, prev):
                    tables(t, it, prev)
                    masks(X, t, it, prev)
                    if prev:
                        store(X, 0, t - 1, it - 1)
                    masks(Y, t, it, prev)
                    if prev:
                        store(Y, 1, t - 1, it - 1)
                window(0, i * NT, False)
                with sp.Fori(1, NT) as t:
                    window(t, i * NT + t, True)
                last = i * NT + (NT - 1)
                store(X, 0, NT - 1, last)
                store(Y, 1, NT - 1, last)
            for w in S:
                sp.wait_ge(w["s_out"], FREE + 16 * (B // 2) * NT)
                sp.nop(nofuse=True)

        @block.tensor
        def _(pe):
            pe.wait_ge(s_wts, 16 * loads[0])
            pe.wait_ge(s_id, ID_ALL)
            pe.wait_ge(s_set_dve, SET_SILU)
            for n in range(3):
                for k in range(DC):
                    mm = pe.matmul(psum[0:B, n, :], cT[:, k, :], wmod_sb[:, k, n * HALF:(n + 1) * HALF],
                                   start=(k == 0), stop=(k == DC - 1))
            mm.then_inc(s_set_pe, 1)
            pe.wait_ge(s_set_dve, SET_ALL)

            pe.wait_ge(s_ones, 3)

            def hT_group(b, c, prev):
                k, hf = c // 2, c % 2
                if c == 0:
                    pe.wait_ge(s_hn, b * 2 + 2)
                if c >= 2:
                    pe.wait_ge(s_hT, b * 4 + c - 1)
                elif prev:
                    pe.wait_ge(s_max, b * (NU * MU) + (c - 1))
                for t in range(4):
                    mm = pe.transpose(psum[:, 6 + c % 2, t * P:(t + 1) * P], hn[:, 4 * hf + t, k * P:(k + 1) * P], ident[:])
                mm.then_inc(s_hT_ps, 1)

            def project(b, n, k):
                qk, m, h = n // 4, (n // 2) % 2, n % 2
                if n == 0 and k == 0:
                    pe.wait_ge(s_hT, b * 4 + 4)
                if n >= 2 and k == 0:
                    pe.wait_ge(s_part, b * (4 * BLOCKS) + (4 * (n - 2) + 2))
                mm = pe.matmul(psum[:, 6 + n % 2, :], wi_sb[:, qk, k, m * P:(m + 1) * P],
                               hT[:, k, h * HALF:(h + 1) * HALF], start=(k == 0), stop=(k == DC - 1))
                if k == DC - 1:
                    mm.then_inc(s_proj, 1)

            def v_tile(b, t, prev):
                if t == 0 and prev:
                    pe.wait_ge(s_exp, b * (NU * 16))
                if t >= 4:
                    pe.wait_ge(s_v, b * NT + t - 3)
                    pe.wait_ge(s_z, b * NT + t - 3)
                for k in range(DC):
                    mm = pe.matmul(psum[:, t % 4, 0:D + NEA], hT[:, k, t * P:(t + 1) * P], wvea[:, k, :],
                                   start=(k == 0), stop=(k == DC - 1))
                mm.then_inc(s_v_ps, 1)

            def v_done(b):
                pe.wait_ge(s_v, b * NT + NT)
                pe.wait_ge(s_z, b * NT + NT)

            def score_job(b, q):
                u, m, kh = q // MU, (q % MU) // NH, q % NH
                g, h, a = u // 2, m // (NT // NH), m % (NT // NH)
                if q % (2 * MU) == 0:
                    pe.wait_ge(s_stack_in[g % 2], b * (STACK_IN * 2) + STACK_IN * (g // 2 + 1))
                if q >= 2:
                    pe.wait_ge(s_max, b * (NU * MU) + (q - 1))
                else:
                    pe.wait_ge(s_part, b * (4 * BLOCKS) + (4 * (6 + q) + 2))
                pe.matmul(psum[:, 6 + kh, :], stack[0:KS, g % 2, 0, u % 2, h, a * P:(a + 1) * P],
                          stack[0:KS, g % 2, 1, kh, h, :], start=True, stop=True).then_inc(s_s_ps, 1)

            def maxima(b, u):
                pe.wait_ge(s_msplit, b * (NU * 5) + (u * 5 + 5))
                if u > 1:
                    pe.wait_ge(s_conv, b * NU + u - 1)
                pe.nop(nofuse=True)
                pe.transpose(bank_bf16(4 + u % 2)[0:PART * TU, 0:P], m3[:].rearrange("p a m -> p (a m)"), identb[:]) \
                    .then_inc(s_mT_ps, 1)

            def st(b, e, pair):
                u, kc = e // NT, e % NT
                if kc == 0 and pair == 0:
                    pe.wait_ge(s_m_in[u % 2], FREE + b * (48 * NG) + 48 * (u // 2 + 1))
                if 2 * e + pair >= 2:
                    pe.wait_ge(s_exp, b * (NU * 16) + (2 * e + pair - 1))
                for h in (2 * pair, 2 * pair + 1):
                    mm = pe.matmul(psum[:, h, :], stack[0:KS + PART, (u // 2) % 2, 1, kc // 4, h, (kc % 4) * P:(kc % 4 + 1) * P],
                                   stack[0:KS + PART, (u // 2) % 2, 0, u % 2, h, :], start=True, stop=True)
                mm.then_inc(s_st_ps, 1)

            def pv(b, e, pair):
                u, kc = e // NT, e % NT
                if pair == 0:
                    pe.wait_ge(s_exp, b * (NU * 16) + (2 * e + 2))
                    if kc == 0:
                        pe.wait_ge(s_vg, b * (NG * 2) + (u // 2 * 2 + 2))
                for h in (2 * pair, 2 * pair + 1):
                    mm = pe.matmul(psum[h * VW:(h + 1) * VW, 4 + u % 2, :], vg[:, (u // 2) % 2, kc, h, :],
                                   pr[:, e % 2, h, :], start=(kc == 0), stop=(kc == NT - 1))
                if pair == 1:
                    mm.then_inc(s_pv, 1)

            def result(b, u):
                pe.wait_ge(s_osb, b * NU + u + 1)
                for t in range(NT // NH):
                    mm = pe.transpose(psum[:, 4 + u % 2, t * P:(t + 1) * P], o_sb[:, t * P:(t + 1) * P], ident[:])
                mm.then_inc(s_oT_ps, 1)

            def cv_group(b, c):
                hf, k = c // 2, c % 2
                if c == 0:
                    pe.wait_ge(s_conv, b * NU + NU)
                for t in range(4):
                    mm = pe.transpose(psum[:, CV_BANKS[c], t * P:(t + 1) * P], cv[:, 4 * hf + t, k * P:(k + 1) * P], ident[:])
                mm.then_inc(s_cvT_ps, 1)

            def out_tile(b, t):
                if t == 0:
                    for e in range(2):
                        pe.wait_ge(s_cvT[e], b * 2 + 2)
                    pe.wait_ge(s_wga, b + 1)
                if t >= 2:
                    pe.wait_ge(s_x1, FREE + b * NT + t - 1)
                for k in range(DC):
                    mm = pe.matmul(psum[:, 2 + t % 2, 0:D], cvT[:, k, t * P:(t + 1) * P], wga[:, k, :],
                                   start=(k == 0), stop=(k == DC - 1))
                mm.then_inc(s_att_ps, 1)

            def start(b, last=None):
                interleave(lambda q: score_job(b, q), lambda t: last is not None and out_tile(last, t),
                           lambda: maxima(b, 0))
                if last is not None:
                    pe.wait_ge(s_x1, FREE + last * NT + NT)
                st(b, 0, 0)
                st(b, 0, 1)

            def batch(b, more):
                for e in range(NU * NT):
                    u, kc = e // NT, e % NT
                    jobs = range(min(AHEAD + 4 * e, NU * MU), min(AHEAD + 4 * e + 4, NU * MU))
                    ahead = e - NEXT
                    for k in range(4):
                        if k < 2:
                            if e + 1 < NU * NT:
                                st(b, e + 1, k)
                        else:
                            pv(b, e, k - 2)
                        if k < len(jobs):
                            score_job(b, jobs[k])
                        if k < 2 and more and 0 <= ahead < 2:
                            hT_group(b + 1, 2 * ahead + k, True)
                        if k < 2 and more and 2 <= ahead < 2 + BLOCKS:
                            project(b + 1, ahead - 2, k)
                        if k == 1 and kc == 2 and u > 0:
                            result(b, u - 1)
                        if k == 1 and kc == 5 and u + 1 < NU:
                            maxima(b, u + 1)
                if more:
                    for t in range(2):
                        v_tile(b + 1, t, True)
                result(b, NU - 1)
                if more:
                    for t in range(2, NT):
                        v_tile(b + 1, t, True)
                for c in range(2):
                    cv_group(b, c)
                if more:
                    v_done(b + 1)
                else:
                    pe.wait_ge(s_exp, b * (NU * 16) + NU * 16)
                for c in range(2, 4):
                    cv_group(b, c)
                if more:
                    start(b + 1, last=b)
                else:
                    for t in range(NT):
                        out_tile(b, t)

            for c in range(4):
                hT_group(0, c, False)
            for n in range(BLOCKS):
                for k in range(DC):
                    project(0, n, k)
            for t in range(NT):
                v_tile(0, t, False)
            v_done(0)
            start(0)
            with pe.Fori(0, B - 1) as b:
                batch(b, True)
            batch(B - 1, False)

            def w2_block(w, l, n):
                bk = w["bk"]
                hid = w["pT"][:].rearrange("p h k n -> p (h k) n")
                pe.wait_ge(w["s_act"], n * FC + FC)
                for cc in range(FC):
                    rows = P if cc < FC - 1 else FR
                    mm = pe.matmul(psum[:, bk, 0:D], hid[0:rows, cc, :], w2_sb[0:rows, l, cc, :],
                                   start=(cc == 0), stop=(cc == FC - 1))
                mm.then_inc(w["s_w2_ps"], 1)

            def blk(name, w, l, it, prev=True):
                n, bk = it * 2 + l, w["bk"]
                if name == "w2":
                    if prev:
                        w2_block(w, 1 - l, n - 1)
                elif name == "uT":
                    src = w["u0"] if l == 0 else w["u"]
                    if l == 0:
                        pe.wait_ge(w["s_ln0"], it * 3 + 3)
                    if l == 1 or prev:
                        pe.wait_ge(w["s_u2"], n)
                    for k in range(DC):
                        mm = pe.transpose(psum[:, bk, k * P:(k + 1) * P], src[:, k * P:(k + 1) * P], ident[:])
                    mm.then_inc(w["s_uT_ps"], 1)
                elif name in ("q01", "q0a", "q0b", "q2a", "q2b"):
                    if name in ("q01", "q0a"):
                        pe.wait_ge(w["s_uT"], n + 1)
                    steps = [(m, k) for m in range(3) for k in range(DC)]
                    steps = {"q01": steps[:2 * DC], "q0a": steps[:1], "q0b": steps[1:2 * DC],
                             "q2a": steps[2 * DC:-1], "q2b": steps[-1:]}[name]
                    for m, k in steps:
                        mm = pe.matmul(psum[:, bk + m, :], w["uT"][:, l, k * (P + 1):k * (P + 1) + P],
                                       wqkv_sb[:, l, k, m * INNER:(m + 1) * INNER],
                                       start=(k == 0), stop=(k == DC - 1))
                    if name not in ("q0a", "q2a"):
                        mm.then_inc(w["s_qkv"], 1)
                elif name == "t":
                    qk = w["big"][:].rearrange("p h n -> p (h n)")
                    pe.wait_ge(w["s_kn"], n + 1)
                    for m in range(2 * INNER // P):
                        mm = pe.transpose(psum[:, bk + m // 4, (m % 4) * P:(m % 4 + 1) * P],
                                          qk[:, m * P:(m + 1) * P], ident[:])
                        if m % 4 == 3:
                            mm.then_inc(w["s_qkT_ps"], 1)
                elif name in ("s0", "s1", "s2", "s3"):
                    if name == "s0":
                        pe.wait_ge(w["s_qz"], n + 1)
                        pe.wait_ge(w["s_kT"], n + 1)
                    if name == "s2":
                        pe.wait_ge(w["s_vev"], n + 1)
                    for h in (2 * int(name[1]), 2 * int(name[1]) + 1):
                        mm = pe.matmul(psum[:, bk + h // 2, (h % 2) * 2 * P:(h % 2 + 1) * 2 * P], w["qz"][:, h, :],
                                       w["kT"][:, l, h // 2, :], start=True, stop=True)
                    mm.then_inc(w["s_s_ps"], 1)
                elif name == "p":
                    for h in range(LH):
                        if h % 2 == 0:
                            pe.wait_ge(w["s_pn"], n * 4 + (h // 2 + 1))
                        for kb in range(2):
                            mm = pe.transpose(psum[:, bk + h // 2, (2 * (h % 2) + kb) * P:(2 * (h % 2) + kb + 1) * P],
                                              w["big"][:, h, kb * P:(kb + 1) * P], ident[:])
                        if h % 2:
                            mm.then_inc(w["s_pT_ps"], 1)
                    for m in range(LH // 2):
                        pe.wait_ge(w["s_pT"], n * 4 + (m + 1))
                        for kb in range(2):
                            for h in (2 * m, 2 * m + 1):
                                mm = pe.matmul(psum[(h % 2) * LD:(h % 2 + 1) * LD, bk, m * P:(m + 1) * P],
                                               w["v"][:, l, kb, h * LD:(h + 1) * LD], w["pT"][:, h, kb, :],
                                               start=(kb == 0), stop=(kb == 1))
                    mm.then_inc(w["s_o_ps"], 1)
                elif name in ("woa", "wob"):
                    if name == "woa":
                        pe.wait_ge(w["s_oT"], n + 1)
                    half_k = INNER // P // 2
                    for k in range(half_k) if name == "woa" else range(half_k, 2 * half_k):
                        mm = pe.matmul(psum[:, bk + 1, 0:D], w["oT"][:, k, :], wo_sb[:, l, k, :],
                                       start=(k == 0), stop=(k == INNER // P - 1))
                    if name == "wob":
                        mm.then_inc(w["s_wo_ps"], 1)
                elif name == "sh":
                    pe.wait_ge(w["s_u1"], n + 1)
                    pe.matmul(psum[:, bk + 2, 0:P], turned[:], w["u"][:, P:D], start=True, stop=True) \
                        .then_inc(w["s_sh_ps"], 1)
                elif name == "h":
                    pe.wait_ge(w["s_hl"], n * 2 + 2)
                    for k in range(DC):
                        mm = pe.transpose(psum[:, bk, k * P:(k + 1) * P], w["hl"][:, k * P:(k + 1) * P], ident[:])
                    mm.then_inc(w["s_hl_ps"], 1)
                elif name in ("w1a", "w1b"):
                    if name == "w1a":
                        pe.wait_ge(w["s_hlT"], n * 2 + 2)
                    for m in range(2 * FC - 2) if name == "w1a" else range(2 * FC - 2, 2 * FC):
                        cc, rows = m % FC, P if m % FC < FC - 1 else FR
                        col = (HID if m < FC else 0) + cc * P
                        for k in range(DC):
                            mm = pe.matmul(psum[0:rows, bk + 1 + m // 4, (m % 4) * P:(m % 4 + 1) * P],
                                           w1_sb[:, l, k, col:col + rows], w["hlT"][:, k, :],
                                           start=(k == 0), stop=(k == DC - 1))
                        if m % 4 == 3:
                            mm.then_inc(w["s_g_ps"], 1)
                else:
                    raise ValueError(name)

            def first(name, w, l, it):
                blk(name, w, l, it, prev=l == 1)

            pe.wait_ge(s_wf, 16 * loads[1])
            with pe.Fori(0, B // 2) as i:
                half(0, i * NT, first, prev=False)
                half(1, i * NT, first)
                with pe.Fori(1, NT) as t:
                    for l in range(LAYERS):
                        half(l, i * NT + t, blk)
                last = i * NT + (NT - 1)
                w2_block(X, 1, last * 2 + 1)
                for name in ("s2", "s3", "p", "woa", "wob", "sh", "h", "w1a", "w1b"):
                    blk(name, Y, 1, last)
                w2_block(Y, 1, last * 2 + 1)

        @block.scalar
        def _(act):
            act.wait_ge(s_wts, 16 * loads[0])
            act.activation(ce[:], cT[:], ACT.Exp, scale=-1.0).then_inc(s_set_act, 1)
            act.activation(he[:, 0:3], hv[:, 0:3], ACT.Exp, scale=-1.0).then_inc(s_set_act, 1)
            act.activation(he[:, 3], hv[:, 3], ACT.Tanh).then_inc(s_set_act, 1)
            act.wait_ge(s_set_dve, SET_ANGLE)
            act.activation(hc[:, 4], hc[:, 2], ACT.Sin).then_inc(s_set_act, 1)
            act.activation(hc[:, 5], hc[:, 3], ACT.Sin).then_inc(s_set_act, 1)

            def values(b):
                for t in range(NT):
                    act.wait_ge(s_v_ps, b * NT + t + 1)
                    act.activation(vt[:, t, :], psum[:, t % 4, 0:D], ACT.Copy).then_inc(s_v, 1)

            def gates(b):
                act.wait_ge(s_z, b * NT + NT)
                act.activation(zt[:], zt[:], ACT.Exp, scale=-1.0).then_inc(s_z_exp, 1)

            def take_result(b, u):
                act.wait_ge(s_pv, b * (NU * NT) + (u * NT + NT))
                if u > 0:
                    act.wait_ge(s_oT_ps, b * NU + u)
                act.activation(o_sb[:], psum[:, 4 + u % 2, :], ACT.Copy).then_inc(s_osb, 1)

            def batch(b, more):
                for e in range(NU * NT):
                    for pair in range(2):
                        act.wait_ge(s_st_ps, b * (NU * 16) + (2 * e + pair + 1))
                        if e >= 2:
                            act.wait_ge(s_pv, b * (NU * NT) + (e - 1))
                        act.activation(pr[:, e % 2, 2 * pair:2 * pair + 2, :], psum[:, 2 * pair:2 * pair + 2, :],
                                       ACT.Exp, scale=DH ** -0.5).then_inc(s_exp, 1)
                    if e % NT == 1 and e > NT:
                        take_result(b, e // NT - 1)
                take_result(b, NU - 1)
                if more:
                    values(b + 1)
                for n, c in enumerate((0, 2)):
                    act.wait_ge(s_cvT_ps, b * 4 + c + 1)
                    act.activation(cvT[:, c % 2, (c // 2) * HALF:(c // 2 + 1) * HALF], psum[:, CV_BANKS[c], :], ACT.Copy) \
                        .then_inc(s_cvT[0], 1)
                if more:
                    gates(b + 1)
            values(0)
            gates(0)
            with act.Fori(0, B - 1) as b:
                batch(b, True)
            batch(B - 1, False)

            def blk(name, w, l, it):
                n, bk = it * 2 + l, w["bk"]
                if name == "A":
                    act.wait_ge(w["s_qkv"], n * 2 + 1)
                    act.activation(w["pT"][:].rearrange("p h k n -> p (h k n)")[:, 0:2 * INNER]
                                   .rearrange("p (a n) -> p a n", a=2), psum[:, bk:bk + 2, :], ACT.Square) \
                        .then_inc(w["s_sq"], 1)
                elif name == "V":
                    act.wait_ge(w["s_qkv"], n * 2 + 2)
                    act.wait_ge(w["s_kvprev"], FREE + it * 4)
                    act.activation(w["v"][:, l, 1, :], psum[:, bk + 2, :], ACT.Copy).then_inc(w["s_vev"], 1)
                elif name == "B":
                    act.wait_ge(w["s_qkT_ps"], n * 2 + 1)
                    for hh in range(2):
                        ins = act.activation(w["qz"][hh * LD:(hh + 1) * LD, hh:LH:2, :],
                                             psum[hh * LD:(hh + 1) * LD, bk, :].rearrange("p (m q) -> p m q", q=P),
                                             ACT.Copy)
                    ins.then_inc(w["s_qz"], 1)
                elif name == "E":
                    for h in range(LH):
                        if h % 4 == 0:
                            act.wait_ge(w["s_sm"], n * 4 + (h // 4 * 2 + 2))
                        ins = act.activation(w["big"][:, h, :], w["big"][:, h, :], ACT.Exp, bias=w["mx"][:, h:h + 1],
                                             accum_out=w["z"][:, h:h + 1])
                        if h % 2:
                            ins.then_inc(w["s_exp"], 1)
                elif name == "C":
                    for m in range(4):
                        act.wait_ge(w["s_pT_ps"], n * 4 + m + 1)
                        act.activation(w["pT"][:, 2 * m:2 * m + 2], psum[:, bk + m, :]
                                       .rearrange("p (h k n) -> p h k n", h=2, k=2), ACT.Copy).then_inc(w["s_pT"], 1)
                    act.wait_ge(w["s_o_ps"], n + 1)
                    act.activation(w["oT"][:].rearrange("p a n -> p (a n)"), psum[:, bk, :], ACT.Copy) \
                        .then_inc(w["s_oT"], 1)
                elif name == "H":
                    act.wait_ge(w["s_hl_ps"], n + 1)
                    for k in range(DC):
                        act.activation(w["hlT"][:, k, :], psum[:, bk, k * P:(k + 1) * P], ACT.Identity,
                                       scale=lnv[:, l, 0, k:k + 1], bias=lnv[:, l, 1, k:k + 1]).then_inc(w["s_hlT"], 1)
                elif name == "D":
                    gl = w["pT"][:].rearrange("p h k n -> p (h k) n")
                    for cc in range(FC):
                        rows = P if cc < FC - 1 else FR
                        if cc % 4 == 0:
                            act.wait_ge(w["s_g_ps"], n * 3 + (cc // 4 + 1))
                        act.activation(gl[0:rows, cc, :], psum[0:rows, bk + 1 + cc // 4, (cc % 4) * P:(cc % 4 + 1) * P],
                                       ACT.Gelu, bias=b1_sb[0:rows, l, 1, cc:cc + 1]).then_inc(w["s_gelu"], 1)

            def turn(l, it, prev=True):
                before = (1 - l, it - 1 if l == 0 else it)
                if prev:
                    blk("E", Y, *before)
                blk("A", X, l, it)
                if prev:
                    blk("C", Y, *before)
                blk("B", X, l, it)
                blk("V", X, l, it)
                blk("E", X, l, it)
                if prev:
                    blk("D", Y, *before)
                blk("C", X, l, it)
                blk("A", Y, l, it)
                blk("H", X, l, it)
                blk("V", Y, l, it)
                blk("D", X, l, it)
                blk("B", Y, l, it)

            act.wait_ge(s_wf, 16 * loads[1])
            with act.Fori(0, B // 2) as i:
                act.wait_ge(s_zero, i * 8 + 10)
                turn(0, i * NT, prev=False)
                turn(1, i * NT)
                with act.Fori(1, NT) as t:
                    for l in range(LAYERS):
                        turn(l, i * NT + t)
                last = i * NT + (NT - 1)
                for name in "ECD":
                    blk(name, Y, 1, last)

        @block.vector
        def _(dve):
            chain = [0]

            def link(ins):
                chain[0] += 1
                ins.then_inc(s_set_dve, 1)
                dve.wait_ge(s_set_dve, chain[0])

            def statistics(b, t):
                if t == 0:
                    dve.wait_ge(s_x_in, b * 16 + 16)
                dve.bn_stats(st1[:, t, :], hn[:, t, :]).then_inc(s_stats1, 1)

            def moments(b):
                dve.wait_ge(s_stats1, b * (2 * NT) + NT)
                dve.nop(nofuse=True)
                for t in range(NT):
                    dve.bn_aggr(mv1[:, t, :], st1[:, t, :]).then_inc(s_stats1, 1)

            for t in range(NT):
                statistics(0, t)
            moments(0)
            dve.wait_ge(s_wts, 16 * loads[0])
            dve.wait_ge(s_set_act, 1)
            link(dve.tensor_scalar(ce[:], ce[:], 1.0, None, ALU.add))
            link(dve.reciprocal(ce[:], ce[:]))
            link(dve.tensor_tensor(cT[:], cT[:], ce[:], ALU.mult))
            assert chain[0] == SET_SILU
            dve.wait_ge(s_set_act, 3)
            link(dve.tensor_scalar(he[:, 0:3], he[:, 0:3], 1.0, None, ALU.add))
            link(dve.reciprocal(he[:, 0:3], he[:, 0:3]))
            link(dve.tensor_scalar(hc[:, 2], he[:, 0], float(np.pi), None, ALU.mult))
            link(dve.tensor_scalar(hc[:, 3], hc[:, 2], -1.0, float(np.pi / 2), ALU.mult, ALU.add))
            assert chain[0] == SET_ANGLE
            link(dve.tensor_tensor(hc[:, 0], he[:, 1], he[:, 2], ALU.mult))
            link(dve.tensor_tensor(hc[:, 0], hc[:, 0], he[:, 3], ALU.mult))
            link(dve.tensor_tensor(sgnc[:], sgnc[:], hc[:, 0], ALU.mult))
            dve.wait_ge(s_set_pe, 1)
            link(dve.tensor_copy(modsb[:].rearrange("p (a n) -> p a n", a=3), psum[0:B, 0:3, :]))
            for n in (1, 4):
                link(dve.tensor_scalar(modsb[:, n * D:(n + 1) * D], modsb[:, n * D:(n + 1) * D], 1.0, None, ALU.add))
            for k, n in enumerate((2, 5)):
                g = modsb[:, n * D:(n + 1) * D]
                link(dve.tensor_scalar(sg[:, k], g, 0.0, 2.0, ALU.is_ge, ALU.mult))
                link(dve.tensor_scalar(sg[:, k], sg[:, k], -1.0, None, ALU.add))
                link(dve.tensor_tensor(g, g, sg[:, k], ALU.mult))
                link(dve.tensor_scalar(g, g, 0.25, None, ALU.max))
                link(dve.tensor_tensor(g, g, sg[:, k], ALU.mult))
            assert chain[0] == SET_MOD
            dve.wait_ge(s_set_act, 5)
            link(dve.tensor_tensor(hc[:, 4], hc[:, 4], sgnc[:], ALU.mult))
            link(dve.tensor_tensor(hc[:, 5], hc[:, 5], hc[:, 0], ALU.mult))
            for k in range(DC):
                link(dve.tensor_scalar(wout_sb[:, 0, k], wout_sb[:, 0, k], hc[:, 5, k:k + 1], None, ALU.mult))
                link(dve.scalar_tensor_tensor(out=wfold[:, k], in0=wout_sb[:, 1, k], scalar=hc[:, 4, k:k + 1],
                                              in1=wout_sb[:, 0, k], op0=ALU.mult, op1=ALU.add))
            for l in range(LAYERS):
                for a in range(4):
                    link(dve.tensor_tensor(tabs[:, :, l, a], rope_sb[:, :, a],
                                           scl[:, l, a].unsqueeze(1).broadcast_to([P, NT, LD]), ALU.mult))
            assert chain[0] == SET_ALL, chain[0]

            def take_hT(b, c):
                k, hf = c // 2, c % 2
                dve.wait_ge(s_hT_ps, b * 4 + c + 1)
                dve.tensor_copy(hT[:, k, hf * HALF:(hf + 1) * HALF], psum[:, 6 + c % 2, :]).then_inc(s_hT, 1)

            def split_block(b, n):
                c0, ps = b * (4 * BLOCKS), psum[:, 6 + n % 2, :]
                dve.wait_ge(s_proj, b * BLOCKS + n + 1)
                dve.wait_ge(s_parts_out[n % 4], FREE + b * 32 + 16 * (n // 4))
                dve.tensor_copy(parts[:, n % 4, 0], ps).then_inc(s_part, 1)
                dve.wait_ge(s_part, c0 + (4 * n + 1))
                dve.tensor_tensor(rest[:, n % 2], ps, parts[:, n % 4, 0], ALU.subtract).then_inc(s_part, 1)
                dve.wait_ge(s_part, c0 + (4 * n + 2))
                dve.tensor_copy(parts[:, n % 4, 1], rest[:, n % 2]).then_inc(s_part, 1)
                dve.wait_ge(s_part, c0 + (4 * n + 3))
                dve.tensor_tensor(parts[:, n % 4, 2], rest[:, n % 2], parts[:, n % 4, 1], ALU.subtract).then_inc(s_part, 1)

            def logits(b, prev):
                if prev:
                    dve.wait_ge(s_conv, b * NU)
                    dve.wait_ge(s_vg, b * (2 * NG))
                for t in range(NT):
                    dve.wait_ge(s_v_ps, b * NT + t + 1)
                    dve.wait_ge(s_v, b * NT + t + 1)
                    dve.tensor_tensor(zt[:, t, :], psum[:, t % 4, D:D + NEA], bias_ea[:], ALU.add).then_inc(s_z, 1)

            def gates(b):
                dve.wait_ge(s_z_exp, b + 1)
                dve.tensor_scalar(zt[:], zt[:], 1.0, None, ALU.add).then_inc(s_gate, 1)
                dve.wait_ge(s_gate, b * 3 + 1)
                dve.reciprocal(zt[:, :, 0:H], zt[:, :, 0:H]).then_inc(s_gate, 1)
                dve.tensor_scalar(zt[:, :, H:NEA], zt[:, :, H:NEA], 1e-8, None, ALU.mult).then_inc(s_gate, 1)

            def maximum(b, q):
                u, m, kh = q // MU, (q % MU) // NH, q % NH
                dve.wait_ge(s_s_ps, b * (NU * MU) + (q + 1))
                dve.tensor_reduce(mx[:, u % 2, m, kh:kh + 1], psum[:, 6 + kh, :], AX.X, ALU.max).then_inc(s_max, 1)

            def split(b, u):
                c0 = b * (NU * 5)
                dve.wait_ge(s_max, b * (NU * MU) + (u * MU + MU))
                if u > 0:
                    dve.wait_ge(s_mT_ps, b * NU + u)
                dve.tensor_tensor(m2[:], mx[:, u % 2, :, 0], mx[:, u % 2, :, 1], ALU.max).then_inc(s_msplit, 1)
                dve.wait_ge(s_msplit, c0 + (u * 5 + 1))
                dve.tensor_copy(m3[:, 0], m2[:]).then_inc(s_msplit, 1)
                dve.wait_ge(s_msplit, c0 + (u * 5 + 2))
                dve.tensor_tensor(mr[:], m2[:], m3[:, 0], ALU.subtract).then_inc(s_msplit, 1)
                dve.wait_ge(s_msplit, c0 + (u * 5 + 3))
                dve.tensor_copy(m3[:, 1], mr[:]).then_inc(s_msplit, 1)
                dve.wait_ge(s_msplit, c0 + (u * 5 + 4))
                dve.tensor_tensor(m3[:, 2], mr[:], m3[:, 1], ALU.subtract).then_inc(s_msplit, 1)

            def rows(b, u):
                dve.wait_ge(s_mT_ps, b * NU + u + 1)
                dve.wait_ge(s_m_in[u % 2], FREE + b * (48 * NG) + 48 * (u // 2))
                dve.tensor_copy(mrow[:, u % 2, :], bank_bf16(4 + u % 2)[0:PART * TU, 0:P]).then_inc(s_mrow, 1)

            def normalise(b, u):
                g, t0, nt = u // 2, (u % 2) * (NT // NH), NT // NH
                dve.wait_ge(s_oT_ps, b * NU + u + 1)
                ov = psum[:, 4 + u % 2, :].rearrange("p (t h w) -> p t h w", h=G, w=VW)
                c0 = b * (NU * 3)
                if u > 0:
                    dve.wait_ge(s_conv, b * NU + u)
                dve.tensor_tensor(den[:], ov[:, :, :, DH + 1], zt[:, t0:t0 + nt, H + G * g:H + G * (g + 1)], ALU.mult).then_inc(s_den, 1)
                dve.wait_ge(s_den, c0 + (u * 3 + 1))
                dve.tensor_tensor(den[:], ov[:, :, :, DH], den[:], ALU.add).then_inc(s_den, 1)
                dve.wait_ge(s_den, c0 + (u * 3 + 2))
                dve.reciprocal(den[:], den[:]).then_inc(s_den, 1)
                dve.wait_ge(s_den, c0 + (u * 3 + 3))
                dve.tensor_tensor(cv[:, t0:t0 + nt, G * DH * g:G * DH * (g + 1)].rearrange("p t (h i) -> p t h i", i=DH),
                                  ov[:, :, :, 0:DH], den[:].unsqueeze(3).broadcast_to([P, nt, G, DH]), ALU.mult) \
                    .then_inc(s_conv, 1)

            def residual(b, t):
                if t == 0:
                    dve.wait_ge(s_xr_in, b * 16 + 16)
                dve.wait_ge(s_att_ps, b * NT + t + 1)
                dve.tensor_tensor(xr[:, t, :], psum[:, 2 + t % 2, 0:D], xr[:, t, :], ALU.add).then_inc(s_x1, 1)

            def start(b, last=None):
                def take(q):
                    maximum(b, q)
                    if q == MU - 1:
                        split(b, 0)
                interleave(take, lambda t: last is not None and residual(last, t), lambda: rows(b, 0), behind=2)

            def batch(b, more):
                for e in range(NU * NT):
                    u, kc = e // NT, e % NT
                    for k in range(4):
                        q = AHEAD + 4 * e + k
                        if q < NU * MU:
                            maximum(b, q)
                            if q % MU == MU - 1:
                                split(b, q // MU)
                        if k == 1 and kc == 3 and u > 0:
                            normalise(b, u - 1)
                        if k == 1 and kc == 5 and u + 1 < NU:
                            rows(b, u + 1)
                    if more:
                        if 0 <= e - STATS < NT // 2:
                            for t in range(2):
                                statistics(b + 1, 2 * (e - STATS) + t)
                        if e == STATS + NT // 2:
                            moments(b + 1)
                        if 0 <= e - NEXT < 2:
                            for c in range(2):
                                take_hT(b + 1, 2 * (e - NEXT) + c)
                        if 2 <= e - NEXT < 2 + BLOCKS:
                            split_block(b + 1, e - NEXT - 2)
                normalise(b, NU - 1)
                if more:
                    logits(b + 1, True)
                for c in (1, 3):
                    dve.wait_ge(s_cvT_ps, b * 4 + c + 1)
                    dve.tensor_copy(cvT[:, c % 2, (c // 2) * HALF:(c // 2 + 1) * HALF], psum[:, CV_BANKS[c], :]) \
                        .then_inc(s_cvT[1], 1)
                if more:
                    gates(b + 1)
                    start(b + 1, last=b)
                else:
                    for t in range(NT):
                        residual(b, t)

            dve.wait_ge(s_mod_in, 16)
            dve.wait_ge(s_ln1, LN1_ALL)
            dve.tensor_tensor(hn[:], hn[:], modA[:, 1].unsqueeze(1).broadcast_to([P, NT, D]), ALU.mult).then_inc(s_hn, 1)
            dve.wait_ge(s_hn, 1)
            dve.tensor_tensor(hn[:], hn[:], modA[:, 0].unsqueeze(1).broadcast_to([P, NT, D]), ALU.add).then_inc(s_hn, 1)
            for c in range(4):
                take_hT(0, c)
            for n in range(BLOCKS):
                split_block(0, n)
            logits(0, False)
            gates(0)
            start(0)
            with dve.Fori(0, B - 1) as b:
                batch(b, True)
            batch(B - 1, False)

            def ln0(w, s, t, it):
                x1 = xs[:, s, bass.ds(t, 1), :].rearrange("p o d -> p (o d)")
                dve.bn_stats(w["x1n"][:], x1).then_inc(w["s_ln0_ag"], 1)
                dve.wait_ge(w["s_ln0_ag"], it * 2 + 1)
                dve.nop(nofuse=True)
                dve.bn_aggr(w["mv0"][:], w["x1n"][:]).then_inc(w["s_ln0_ag"], 1)

            def ln0_end(w, s, t, it):
                x1 = xs[:, s, bass.ds(t, 1), :].rearrange("p o d -> p (o d)")
                dve.wait_ge(w["s_ln0_rs"], it * 2 + 2)
                dve.tensor_scalar(w["u0"][:], x1, w["mv0"][:, 0:1], w["rs0"][:], ALU.subtract, ALU.mult).then_inc(w["s_ln0"], 1)
                dve.wait_ge(w["s_ln0"], it * 3 + 1)
                dve.tensor_tensor(w["u0"][:], w["u0"][:], modF[:, s, 1], ALU.mult).then_inc(w["s_ln0"], 1)
                dve.wait_ge(w["s_ln0"], it * 3 + 2)
                dve.tensor_tensor(w["u0"][:], w["u0"][:], modF[:, s, 0], ALU.add).then_inc(w["s_ln0"], 1)

            def finish_layer(w, l, n):
                dve.wait_ge(w["s_w2_ps"], n + 1)
                dve.wait_ge(w["s_ub"], n + 1)
                dve.tensor_tensor(w["u"][:], psum[:, w["bk"], 0:D], w["u"][:], ALU.add).then_inc(w["s_u2"], 1)

            def finish(w, s, t, it):
                x1 = xs[:, s, bass.ds(t, 1), :].rearrange("p o d -> p (o d)")
                dve.wait_ge(w["s_u2"], it * 2 + 2)
                dve.wait_ge(w["s_out"], FREE + it * 16)
                dve.tensor_tensor(w["o"][:], w["u"][:], modF[:, s, 2], ALU.mult).then_inc(w["s_oo"], 1)
                dve.wait_ge(w["s_oo"], it * 2 + 1)
                dve.tensor_tensor(w["o"][:], w["o"][:], x1, ALU.add).then_inc(w["s_oo"], 1)

            def blk(name, w, l, it, prev=True):
                n, bk = it * 2 + l, w["bk"]
                flat = w["big"][:].rearrange("p h n -> p (h n)")
                if name == "F":
                    if prev:
                        finish_layer(w, 1 - l, n - 1)
                elif name == "U":
                    uT = w["uT"][:, l]
                    dve.wait_ge(w["s_uT_ps"], n + 1)
                    dve.tensor_copy(uT[:, P + 1:P + 2], uT[:, 2 * P + 1:2 * P + 2]).then_inc(w["s_carry"], 1)
                    dve.wait_ge(w["s_carry"], n + 1)
                    dve.tensor_copy(uT[:, 0:2 * (P + 2)].rearrange("p (a n) -> p a n", a=2)[:, :, 0:P],
                                    psum[:, bk, 0:D].rearrange("p (a n) -> p a n", a=2)).then_inc(w["s_uT"], 1)
                elif name == "A2":
                    sq = w["pT"][:].rearrange("p h k n -> p (h k n)")[:, 0:2 * INNER].rearrange("p (h d) -> p h d", d=LD)
                    qk = psum[:, bk:bk + 2, :].rearrange("p a (h d) -> p a h d", d=LD)
                    rot = flat[:, 0:2 * INNER].rearrange("p (a h d) -> p a h d", a=2, d=LD)
                    rs = flat[:, 2 * INNER:4 * INNER].rearrange("p (a h d) -> p a h d", a=2, d=LD)
                    dve.wait_ge(s_tab_in, it * 16 + 16)
                    dve.wait_ge(w["s_sq"], n + 1)
                    dve.tensor_reduce(w["ss"][:], sq, AX.X, ALU.add).then_inc(w["s_ssum"], 1)
                    dve.tensor_tensor(rot, qk, tab[:, l, 0:2].unsqueeze(2).broadcast_to([P, 2, LH, LD]), ALU.mult) \
                        .then_inc(w["s_rope"], 1)
                    hd = LD // 2
                    for lo, hi in ((0, hd), (hd, 0)):
                        ins = dve.tensor_tensor(rs[:, :, :, lo:lo + hd], qk[:, :, :, hi:hi + hd],
                                                tab[:, l, 2:4, lo:lo + hd].unsqueeze(2).broadcast_to([P, 2, LH, hd]), ALU.mult)
                    ins.then_inc(w["s_rope"], 1)
                    dve.wait_ge(w["s_rope"], n * 3 + 2)
                    dve.tensor_tensor(flat[:, 0:2 * INNER], flat[:, 0:2 * INNER], flat[:, 2 * INNER:4 * INNER], ALU.add) \
                        .then_inc(w["s_rope"], 1)
                    dve.wait_ge(w["s_rope"], n * 3 + 3)
                    dve.wait_ge(w["s_rn"], n * 4 + 2)
                    dve.tensor_tensor(rot[:, 1], rot[:, 1], w["rn"][:, LH:2 * LH].unsqueeze(2).broadcast_to([P, LH, LD]), ALU.mult) \
                        .then_inc(w["s_kn"], 1)
                elif name == "B1":
                    dve.wait_ge(w["s_qkT_ps"], n * 2 + 2)
                    dve.wait_ge(w["s_kvprev"], FREE + it * 4)
                    dve.tensor_copy(w["kT"][:, l, :, P:2 * P], psum[:, bk + 1, :].rearrange("p (m q) -> p m q", q=P)) \
                        .then_inc(w["s_kT"], 1)
                elif name in ("B2", "B2a", "B2b", "B2c"):
                    if name == "B2":
                        dve.wait_ge(w["s_mask_in"], it * 16 + 16)
                        dve.wait_ge(w["s_rn"], n * 4 + 4)
                    for h in {"B2": range(0, 2), "B2a": range(2, 4), "B2b": range(4, 6), "B2c": range(6, 8)}[name]:
                        if h % 2 == 0:
                            dve.wait_ge(w["s_s_ps"], n * (LH // 2) + h // 2 + 1)
                            dve.nop(nofuse=True)
                        ins = dve.tensor_tensor_reduce(out=w["big"][:, h, :],
                                                       in0=psum[:, bk + h // 2, (h % 2) * 2 * P:(h % 2 + 1) * 2 * P],
                                                       in1=w["mask"][:], scale=w["rn"][:, h:h + 1], scalar=-3.4e38,
                                                       op0=ALU.add, op1=ALU.max, accum_out=w["mx"][:, h:h + 1])
                    if name in ("B2a", "B2c"):
                        a = 0 if name == "B2a" else 4
                        ins.then_inc(w["s_sm"], 1)
                        dve.wait_ge(w["s_sm"], n * 4 + (a // 2 + 1))
                        dve.tensor_scalar(w["mx"][:, a:a + 4], w["mx"][:, a:a + 4], -1.0, None, ALU.mult).then_inc(w["s_sm"], 1)
                elif name == "B3":
                    for m in range(4):
                        dve.wait_ge(w["s_exp"], n * 4 + m + 1)
                        dve.reciprocal(w["rz"][:, 2 * m:2 * m + 2], w["z"][:, 2 * m:2 * m + 2]).then_inc(w["s_rz"], 1)
                        dve.wait_ge(w["s_rz"], n * 4 + m + 1)
                        for h in (2 * m, 2 * m + 1):
                            ins = dve.tensor_scalar(w["big"][:, h, :], w["big"][:, h, :], w["rz"][:, h:h + 1], None, ALU.mult)
                        ins.then_inc(w["s_pn"], 1)
                elif name == "C1":
                    dve.wait_ge(w["s_wo_ps"], n + 1)
                    dve.tensor_tensor(w["u"][:], psum[:, bk + 1, 0:D], (w["u0"] if l == 0 else w["u"])[:], ALU.add) \
                        .then_inc(w["s_u1"], 1)
                elif name == "C2":
                    dve.wait_ge(w["s_u1"], n + 1)
                    dve.bn_stats(w["st"][:, 0, :], w["u"][:, 0:P]).then_inc(w["s_ln_ag"], 1)
                    dve.wait_ge(w["s_sh_ps"], n + 1)
                    dve.tensor_copy(w["ush"][:], psum[:, bk + 2, 0:P]).then_inc(w["s_sh"], 1)
                    dve.wait_ge(w["s_sh"], n * 3 + 1)
                    dve.tensor_copy(w["ush"][0:1, :], w["crow"][:, l]).then_inc(w["s_sh"], 1)
                    dve.wait_ge(w["s_sh"], n * 3 + 2)
                    dve.tensor_copy(w["crow"][:, l], psum[0:1, bk + 2, 0:P]).then_inc(w["s_sh"], 1)
                    dve.bn_stats(w["st"][:, 1, :], w["ush"][:]).then_inc(w["s_ln_ag"], 1)
                    dve.wait_ge(w["s_ln_ag"], n * 3 + 2)
                    dve.nop(nofuse=True)
                    dve.bn_aggr(w["mv"][:], w["st"][:].rearrange("p a n -> p (a n)")).then_inc(w["s_ln_ag"], 1)
                elif name == "C3":
                    dve.wait_ge(w["s_ln_rs"], n * 2 + 2)
                    for k, src in ((0, w["u"][:, 0:P]), (1, w["ush"][:])):
                        dve.tensor_scalar(w["hl"][:, k * P:(k + 1) * P], src, w["mv"][:, 0:1], w["rs"][:], ALU.subtract, ALU.mult) \
                            .then_inc(w["s_hl"], 1)
                elif name == "D1":
                    dve.wait_ge(w["s_hl_ps"], n + 1)
                    for k in range(DC):
                        dve.tensor_scalar(w["hlT"][:, k, :], psum[:, bk, k * P:(k + 1) * P], lnv[:, l, 0, k:k + 1],
                                          lnv[:, l, 1, k:k + 1], ALU.mult, ALU.add).then_inc(w["s_hlT"], 1)
                elif name == "D2":
                    dve.wait_ge(w["s_hl"], n * 2 + 2)
                    dve.tensor_tensor(w["u"][:], w["u"][:], b2_sb[:, l], ALU.add).then_inc(w["s_ub"], 1)
                    gl = w["pT"][:].rearrange("p h k n -> p (h k) n")
                    dve.wait_ge(w["s_gelu"], n * FC + FC)
                    dve.wait_ge(w["s_g_ps"], n * 3 + 3)
                    for cc in range(FC):
                        rows, m = (P if cc < FC - 1 else FR), FC + cc
                        dve.scalar_tensor_tensor(out=gl[0:rows, cc, :],
                                                 in0=psum[0:rows, bk + 1 + m // 4, (m % 4) * P:(m % 4 + 1) * P],
                                                 scalar=b1_sb[0:rows, l, 0, cc:cc + 1], in1=gl[0:rows, cc, :],
                                                 op0=ALU.add, op1=ALU.mult).then_inc(w["s_act"], 1)

            def turn(l, t, it, prev=True, ahead=True):
                before = (1 - l, it - 1 if l == 0 else it)
                blk("F", X, l, it, prev)
                blk("U", X, l, it)
                if prev:
                    blk("B2b", Y, *before)
                    blk("B2c", Y, *before)
                    if l == 0:
                        finish(X, 0, t - 1, it - 1)
                    blk("B3", Y, *before)
                blk("A2", X, l, it)
                if prev:
                    blk("C1", Y, *before)
                blk("B1", X, l, it)
                if prev:
                    blk("C2", Y, *before)
                blk("B2", X, l, it)
                if prev:
                    blk("C3", Y, *before)
                blk("B2a", X, l, it)
                if prev:
                    blk("D1", Y, *before)
                blk("B2b", X, l, it)
                blk("B2c", X, l, it)
                blk("B3", X, l, it)
                if prev:
                    blk("D2", Y, *before)
                if l == 1 and ahead:
                    for s in range(2):
                        ln0(S[s], s, t + 1, it + 1)
                blk("F", Y, l, it, prev)
                blk("U", Y, l, it)
                blk("C1", X, l, it)
                blk("C2", X, l, it)
                blk("C3", X, l, it)
                blk("A2", Y, l, it)
                if prev and l == 0:
                    finish(Y, 1, t - 1, it - 1)
                blk("B1", Y, l, it)
                blk("D2", X, l, it)
                blk("B2", Y, l, it)
                blk("B2a", Y, l, it)
                if l == 1 and ahead:
                    for s in range(2):
                        ln0_end(S[s], s, t + 1, it + 1)

            dve.wait_ge(s_wf, 16 * loads[1])
            dve.nop(nofuse=True)
            with dve.Fori(0, B // 2) as i:
                dve.wait_ge(s_zero, i * 8 + 10)
                dve.wait_ge(s_xs0_in, i * 64 + 64)
                for s in range(2):
                    ln0(S[s], s, 0, i * NT)
                for s in range(2):
                    ln0_end(S[s], s, 0, i * NT)
                turn(0, 0, i * NT, prev=False)
                dve.wait_ge(s_xs_in, i * 32 + 32)
                turn(1, 0, i * NT)
                with dve.Fori(1, NT - 1) as t:
                    for l in range(LAYERS):
                        turn(l, t, i * NT + t)
                last = i * NT + (NT - 1)
                for l in range(LAYERS):
                    turn(l, NT - 1, last, ahead=False)
                finish_layer(X, 1, last * 2 + 1)
                for name in ("B2b", "B2c"):
                    blk(name, Y, 1, last)
                finish(X, 0, NT - 1, last)
                for name in ("B3", "C1", "C2", "C3", "D1", "D2"):
                    blk(name, Y, 1, last)
                finish_layer(Y, 1, last * 2 + 1)
                finish(Y, 1, NT - 1, last)

        @block.gpsimd
        def _(gp):
            for s in (s_x1, *s_parts_out, *s_m_in, *(w[n] for w in S for n in ("s_out", "s_kvprev"))):
                gp.sem_inc(s, FREE)
            gp.memset(ident[:], 0.0).then_inc(s_id, 1)
            gp.wait_ge(s_id, 1)
            gp.nop(nofuse=True)
            gp.affine_select(out=ident[:], in_=ident[:], compare_op=ALU.not_equal, fill=1.0, base=0,
                             pattern=[[-1, P]], channel_multiplier=1).then_inc(s_id, 1)
            gp.wait_ge(s_id, 2)
            gp.nop(nofuse=True)
            gp.tensor_copy(identb[:], ident[:]).then_inc(s_id, 1)
            gp.memset(turned[:], 0.0).then_inc(s_id, 1)
            for n, base in enumerate((1, 1 - P)):
                gp.wait_ge(s_id, 4 + n)
                gp.nop(nofuse=True)
                gp.affine_select(out=turned[:], in_=turned[:], compare_op=ALU.not_equal, fill=1.0, base=base,
                                 pattern=[[-1, P]], channel_multiplier=1).then_inc(s_id, 1)
            gp.memset(neghalf[:], -0.5).then_inc(s_id, 1)
            gp.wait_ge(s_id, ID_ALL)
            gp.nop(nofuse=True)
            def norm(b):
                c0 = b * LN1_ALL
                gp.wait_ge(s_stats1, b * (2 * NT) + 2 * NT)
                gp.nop(nofuse=True)
                gp.tensor_scalar(rs1[:], mv1[:, :, 1], LN_EPS, 1.0, ALU.add, ALU.mult).then_inc(s_ln1, 1)
                gp.wait_ge(s_ln1, c0 + 1)
                gp.nop(nofuse=True)
                gp.tensor_tensor(rs1[:], rs1[:], neghalf[:, 0:NT], ALU.pow).then_inc(s_ln1, 1)
                gp.wait_ge(s_ln1, c0 + 2)
                gp.nop(nofuse=True)
                for t in range(NT):
                    gp.tensor_scalar(hn[:, t, :], hn[:, t, :], mv1[:, t, 0:1], rs1[:, t:t + 1], ALU.subtract, ALU.mult) \
                        .then_inc(s_ln1, 1)

            norm(0)
            gp.wait_ge(s_set_dve, SET_ALL)
            gp.wait_ge(s_set_out, 16 * (1 + LAYERS))

            gp.wait_ge(s_ln1, LN1_ALL)
            gp.nop(nofuse=True)
            gp.memset(stack[KS:KS + PART, :, 1], -1.0).then_inc(s_ones, 1)
            gp.wait_ge(s_ones, 1)
            gp.nop(nofuse=True)
            gp.memset(vg[:, :, :, :, DH:VW], 0.0).then_inc(s_ones, 1)
            gp.wait_ge(s_ones, 2)
            gp.nop(nofuse=True)
            gp.memset(vg[:, :, :, :, DH + 1:DH + 2], 1.0).then_inc(s_ones, 1)
            gp.wait_ge(s_ones, 3)
            gp.nop(nofuse=True)

            def modulate(b):
                gp.wait_ge(s_mod_in, b * 16 + 16)
                gp.wait_ge(s_ln1, b * LN1_ALL + LN1_ALL)
                gp.nop(nofuse=True)
                gp.tensor_tensor(hn[:], hn[:], modA[:, 1].unsqueeze(1).broadcast_to([P, NT, D]), ALU.mult).then_inc(s_hn, 1)
                gp.wait_ge(s_hn, b * 2 + 1)
                gp.nop(nofuse=True)
                gp.tensor_tensor(hn[:], hn[:], modA[:, 0].unsqueeze(1).broadcast_to([P, NT, D]), ALU.add).then_inc(s_hn, 1)

            def values(b, g):
                if g == 0:
                    gp.wait_ge(s_gate, b * 3 + 3)
                    gp.wait_ge(s_v, b * NT + NT)
                    gp.nop(nofuse=True)
                if g > 1:
                    gp.wait_ge(s_pv, b * (NU * NT) + (g - 1) * 16)
                    gp.nop(nofuse=True)
                e = zt[:, :, G * g:G * (g + 1)]
                gp.tensor_tensor(vg[:, g % 2, :, :, 0:DH], vt[:, :, G * DH * g:G * DH * (g + 1)].rearrange("p t (h i) -> p t h i", i=DH),
                                 e.unsqueeze(3).broadcast_to([P, NT, G, DH]), ALU.mult).then_inc(s_vg, 1)
                gp.tensor_copy(vg[:, g % 2, :, :, DH], e).then_inc(s_vg, 1)

            def batch(b, more):
                values(b, 0)
                values(b, 1)
                gp.wait_ge(s_x1, FREE + b * NT)
                gp.nop(nofuse=True)
                gp.tensor_tensor(wga[:], wfold[:], modA[:, 2].unsqueeze(1).broadcast_to([P, DC, D]), ALU.mult).then_inc(s_wga, 1)
                values(b, 2)
                values(b, 3)
                if more:
                    norm(b + 1)
                    modulate(b + 1)
            with gp.Fori(0, B - 1) as b:
                batch(b, True)
            batch(B - 1, False)

            def ln0(w, it):
                gp.wait_ge(w["s_ln0_ag"], it * 2 + 2)
                gp.nop(nofuse=True)
                gp.tensor_scalar(w["rs0"][:], w["mv0"][:, 1:2], LN_EPS, 1.0, ALU.add, ALU.mult).then_inc(w["s_ln0_rs"], 1)
                gp.wait_ge(w["s_ln0_rs"], it * 2 + 1)
                gp.nop(nofuse=True)
                gp.tensor_tensor(w["rs0"][:], w["rs0"][:], neghalf[:, 0:1], ALU.pow).then_inc(w["s_ln0_rs"], 1)

            def blk(name, w, l, it):
                n = it * 2 + l
                if name == "A":
                    gp.wait_ge(w["s_ssum"], n + 1)
                    gp.nop(nofuse=True)
                    gp.tensor_scalar(w["ss"][:], w["ss"][:], 1e-24, None, ALU.max).then_inc(w["s_rn"], 1)
                    for half_h in (slice(LH, 2 * LH), slice(0, LH)):
                        gp.wait_ge(w["s_rn"], n * 4 + 1)
                        gp.nop(nofuse=True)
                        gp.tensor_tensor(w["rn"][:, half_h], w["ss"][:, half_h], neghalf[:, 0:LH], ALU.pow).then_inc(w["s_rn"], 1)
                    gp.wait_ge(w["s_rn"], n * 4 + 3)
                    gp.nop(nofuse=True)
                    gp.tensor_scalar(w["rn"][:, 0:LH], w["rn"][:, 0:LH], 8.0, 1.0, ALU.mult, ALU.mult).then_inc(w["s_rn"], 1)
                elif name == "C":
                    gp.wait_ge(w["s_o_ps"], n + 1)
                    gp.nop(nofuse=True)
                    gp.tensor_copy(w["v"][:, l, 0, :], w["v"][:, l, 1, :]).then_inc(w["s_kvprev"], 1)
                    gp.tensor_copy(w["kT"][:, l, :, 0:P], w["kT"][:, l, :, P:2 * P]).then_inc(w["s_kvprev"], 1)
                elif name == "D":
                    gp.wait_ge(w["s_ln_ag"], n * 3 + 3)
                    gp.nop(nofuse=True)
                    gp.tensor_scalar(w["rs"][:], w["mv"][:, 1:2], LN_EPS, 1.0, ALU.add, ALU.mult).then_inc(w["s_ln_rs"], 1)
                    gp.wait_ge(w["s_ln_rs"], n * 2 + 1)
                    gp.nop(nofuse=True)
                    gp.tensor_tensor(w["rs"][:], w["rs"][:], neghalf[:, 0:1], ALU.pow).then_inc(w["s_ln_rs"], 1)

            def turn(l, it, prev=True, ahead=True):
                before = (1 - l, it - 1 if l == 0 else it)
                blk("A", X, l, it)
                if prev:
                    blk("D", Y, *before)
                    blk("C", Y, *before)
                if l == 1 and ahead:
                    for w in S:
                        ln0(w, it + 1)
                blk("D", X, l, it)
                blk("A", Y, l, it)
                blk("C", X, l, it)

            gp.wait_ge(s_x1_out, B * 16)
            gp.nop(nofuse=True)
            for w in S:
                gp.memset(w["qz"][:], 0.0).then_inc(s_zero, 1)
            gp.wait_ge(s_zero, 2)
            gp.nop(nofuse=True)
            with gp.Fori(0, B // 2) as i:
                for w in S:
                    gp.wait_ge(w["s_out"], FREE + i * (16 * NT))
                    gp.nop(nofuse=True)
                for s in range(2):
                    w = S[s]
                    for k, buf in enumerate((w["uT"][:, :, 2 * P + 1:2 * P + 2], w["kT"][:, :, :, 0:P], w["v"][:, :, 0, :],
                                             w["crow"][:])):
                        gp.memset(buf, 0.0).then_inc(s_zero, 1)
                        gp.wait_ge(s_zero, i * 8 + (2 + 4 * s + k + 1))
                        gp.nop(nofuse=True)
                for w in S:
                    ln0(w, i * NT)
                turn(0, i * NT, prev=False)
                turn(1, i * NT)
                with gp.Fori(1, NT - 1) as t:
                    for l in range(LAYERS):
                        turn(l, i * NT + t)
                last = i * NT + (NT - 1)
                for l in range(LAYERS):
                    turn(l, last, ahead=False)
                for name in "DC":
                    blk(name, Y, 1, last)


def _constants():
    n = np.float32
    half = np.arange(0, LD, 2, dtype=n)
    inv = (n(1.0) / n(10000.0) ** (half / n(LD))).astype(n)
    t = np.arange(T, dtype=n)
    fr = t[:, None] * inv[None, :]
    fr = np.concatenate([fr, fr], -1)
    base = (half + n(0.4 * LD)) / n(1.4 * LD)
    scale = base[None, :] ** ((t - T // 2) / n(P // 2))[:, None]
    scale = np.concatenate([scale, scale], -1).astype(n)
    cos, sin = np.cos(fr.astype(np.float64)), np.sin(fr.astype(np.float64))
    sign = np.concatenate([-np.ones(LD // 2), np.ones(LD // 2)])
    rope = np.stack([cos * scale, cos / scale, sign * sin * scale, sign * sin / scale], 1).astype(n)
    rope = np.ascontiguousarray(rope.reshape(NT, P, 4, LD).transpose(1, 0, 2, 3))
    q, k = np.arange(P)[:, None], np.arange(2 * P)[None, :] - P
    keep = (k <= q) & (k >= q - P)
    mask = np.stack([keep & ((k >= 0) | (w > 0)) for w in range(NT)])
    return rope, np.where(mask, 0.0, MASKED).astype(n)


def kernel(**inputs):
    import concourse.bacc as _bacc
    from concourse.bass_utils import run_bass_kernel_spmd as _run

    a = {k: np.ascontiguousarray(v) for k, v in inputs.items()}
    rope, mask = _constants()
    wout = a["L0_attn_Wout"]
    heads = np.stack([a["L0_attn_" + k] for k in ("beta_p", "iv_p", "ov_p", "chi")])
    heads = np.repeat(heads, DH, axis=1).reshape(4, DC, P).transpose(2, 0, 1)
    sgn = np.where(np.arange(D) % DH < DH // 2, 1.0, -1.0).astype(np.float32).reshape(DC, P).T
    swapped = wout.reshape(H, 2, DH // 2, D)[:, ::-1].reshape(D, D)
    arrays = {
        "x": a["L0_attn_x"], "Wa": a["L0_attn_Wa"], "ba": a["L0_attn_ba"], "We": a["L0_attn_We"], "be": a["L0_attn_be"],
        "Wi": a["L0_attn_Wi"], "Wo": a["L0_attn_Wo"], "Wv": a["L0_attn_Wv"], "Wout": wout, "Wout_sw": swapped,
        "head_vec": heads, "sgn": sgn, "wqkv": a["L0_ffn_wqkv"], "q_scale": a["L0_ffn_q_scale"],
        "k_scale": a["L0_ffn_k_scale"], "wo": a["L0_ffn_wo"], "ln_g": a["L0_ffn_ln_g"], "ln_b": a["L0_ffn_ln_b"],
        "w1": a["L0_ffn_w1"], "b1": a["L0_ffn_b1"], "w2": a["L0_ffn_w2"], "b2": a["L0_ffn_b2"], "c": a["L0_c"],
        "wmod": a["L0_wmod"], "rope": rope, "mask": mask,
    }
    arrays = {k: np.ascontiguousarray(v) for k, v in arrays.items()}
    nc = _bacc.Bacc("TRN2", target_bir_lowering=False, num_devices=1)
    aps = {k: nc.dram_tensor("in_" + k, v.shape, mybir.dt.from_np(v.dtype), kind="ExternalInput").ap()
           for k, v in arrays.items()}
    aps["out"] = nc.dram_tensor("out_x", (B, T, D), F32, kind="ExternalOutput").ap()
    build(nc, **aps)
    r = _run(nc, [{"in_" + k: v for k, v in arrays.items()}], core_ids=[0])
    return r.results[0]["out_x"]
```

```python
from contextlib import ExitStack

import numpy as np

import concourse.bass as bass
from concourse import mybir

F32 = mybir.dt.float32
BF16 = mybir.dt.bfloat16
ALU = mybir.AluOpType
ACT = mybir.ActivationFunctionType
AX = mybir.AxisListType

P = 128
B, T, D = 8, 1024, 256
NT = T // P
DC = D // P
HALF = 512
NH = T // HALF
H, DH = 16, 16
G = 4
NG = H // G
PART = 3
PAIRS_Q = (0, 0, 0, 1, 1, 2)
PAIRS_K = (0, 1, 2, 0, 1, 0)
KS = DH * len(PAIRS_Q)
NU = NG * NH
TU = G * NT // NH
MU = TU * NH
BLOCKS = 8
LN1_ALL = 2 + NT
AHEAD = MU + 12
NEXT = -(-(NU * MU - AHEAD) // 4)
CV_BANKS = (4, 5, 0, 1)
STATS = 4 * NT + 6
STACK_IN = 16 * 2 * len(PAIRS_Q)
VW = 32
NEA = 2 * H
PAIRS = B // 2
LAYERS, LH, LD = 2, 8, 64
INNER = LH * LD
HID = 682
FC = -(-HID // P)
FR = HID - (FC - 1) * P
LN_EPS = 1e-5
MASKED = -1e25
FREE = 1
SET_SILU, SET_ANGLE, SET_MOD, SET_ALL, ID_ALL = 3, 7, 23, 37, 7


def build(nc, x, Wa, ba, We, be, Wi, Wo, Wv, Wout, Wout_sw, head_vec, sgn, wqkv, q_scale, k_scale,
          wo, ln_g, ln_b, w1, b1, w2, b2, c, wmod, rope, mask, out):
    mod_d = nc.dram_tensor("mod_d", (B, 6 * D), F32, kind="Internal").ap()
    tab_d = nc.dram_tensor("tab_d", (NT, P, LAYERS * 4 * LD), F32, kind="Internal").ap()
    x1_d = nc.dram_tensor("x1_d", (B, T, D), F32, kind="Internal").ap()
    parts_d = nc.dram_tensor("parts_d", (2, PART, D, T), BF16, kind="Internal").ap()

    ctx = ExitStack()
    with ctx:
        def sem(name):
            return ctx.enter_context(nc.semaphore(name))

        def res(name, shape, dt=F32):
            return ctx.enter_context(nc.sbuf_tensor(name, shape, dt))

        ident = res("ident", [P, P])
        turned = res("turned", [P, P])
        identb = res("identb", [P, P], BF16)
        wi_sb = res("wi_sb", [P, 2, DC, D])
        wvea = res("wvea", [P, DC, D + NEA])
        wfold = res("wfold", [P, DC, D])
        wga = res("wga", [P, DC, D])
        bias_ea = res("bias_ea", [P, NEA])
        wqkv_sb = res("wqkv_sb", [P, LAYERS, DC, 3 * INNER])
        wo_sb = res("wo_sb", [P, LAYERS, INNER // P, D])
        w1_sb = res("w1_sb", [P, LAYERS, DC, 2 * HID])
        w2_sb = res("w2_sb", [P, LAYERS, FC, D])
        b1_sb = res("b1_sb", [P, LAYERS, 2, FC])
        b2_sb = res("b2_sb", [P, LAYERS, D])
        lnv = res("lnv", [P, LAYERS, 2, DC])
        neghalf = res("neghalf", [P, 2 * LH])

        def nested(stack):
            return lambda name, shape, dt=F32: stack.enter_context(nc.sbuf_tensor(name, shape, dt))

        with ExitStack() as scope_a:
            tmp = nested(scope_a)
            modA = tmp("modA", [P, 3, D])
            hn = tmp("hn", [P, NT, D])
            hT = tmp("hT", [P, DC, T])
            xr = tmp("xr", [P, NT, D])
            st1 = tmp("st1", [P, NT, 6])
            mv1 = tmp("mv1", [P, NT, 2])
            rs1 = tmp("rs1", [P, NT])

            with ExitStack() as scope:
                tmp = nested(scope)
                wmod_sb = tmp("wmod_sb", [P, DC, 6 * D])
                cT = tmp("cT", [P, DC, B])
                ce = tmp("ce", [P, DC, B])
                modsb = tmp("modsb", [B, 6 * D])
                sg = tmp("sg", [B, 2, D])
                hv = tmp("hv", [P, 4, DC])
                he = tmp("he", [P, 4, DC])
                hc = tmp("hc", [P, 6, DC])
                sgnc = tmp("sgnc", [P, DC])
                wout_sb = tmp("wout_sb", [P, 2, DC, D])
                rope_sb = tmp("rope_sb", [P, NT, 4, LD])
                scl = tmp("scl", [P, LAYERS, 4, LD])
                tabs = tmp("tabs", [P, NT, LAYERS, 4, LD])

            tmp = nested(scope_a)
            cv = tmp("cv", [P, NT, D])
            parts = tmp("parts", [P, 4, PART, HALF], BF16)
            rest = tmp("rest", [P, 2, HALF])
            o_sb = tmp("o_sb", [P, HALF])
            stack = tmp("stack", [P, 2, 2, NH, G, HALF], BF16)
            vg = tmp("vg", [P, 2, NT, G, VW])
            pr = tmp("pr", [P, 2, G, HALF])
            zt = tmp("zt", [P, NT, NEA])
            mx = tmp("mx", [P, 2, TU, NH])
            m2 = tmp("m2", [P, TU])
            mr = tmp("mr", [P, TU])
            m3 = tmp("m3", [P, PART, TU], BF16)
            mrow = tmp("mrow", [PART * TU, 2, P], BF16)
            den = tmp("den", [P, NT // NH, G])
        vt, cvT = hn, hT

        with ExitStack() as scope:
            tmp = nested(scope)
            tab = tmp("tab", [P, LAYERS, 4, LD])
            xs = tmp("xs", [P, 2, NT, D])
            modF = tmp("modF", [P, 2, 2, D])
            zero = tmp("zero", [P, P])
            gateF = tmp("gateF", [P, 2, D])
            S = [dict(
                u0=tmp(f"u0_s{s}", [P, D]),
                u=tmp(f"u_s{s}", [P, D]),
                mask=tmp(f"mask_s{s}", [P, 2 * P]),
                x1n=tmp(f"x1n_s{s}", [P, 6]),
                uT=tmp(f"uT_s{s}", [P, LAYERS, 2 * P + 4]),
                big=tmp(f"big_s{s}", [P, LH, 2 * P]),
                pT=tmp(f"pT_s{s}", [P, LH, 2, P]),
                qz=tmp(f"qz_s{s}", [P, LH, P]),
                kT=tmp(f"kT_s{s}", [P, LAYERS, LH // 2, 2 * P]),
                v=tmp(f"v_s{s}", [P, LAYERS, 2, INNER]),
                oT=tmp(f"oT_s{s}", [P, INNER // P, P]),
                ush=tmp(f"ush_s{s}", [P, P]),
                crow=tmp(f"crow_s{s}", [1, LAYERS, P]),
                hl=tmp(f"hl_s{s}", [P, D]),
                hlT=tmp(f"hlT_s{s}", [P, DC, P]),
                st=tmp(f"st_s{s}", [P, 2, 6]),
                mv=tmp(f"mv_s{s}", [P, 2]),
                mv0=tmp(f"mv0_s{s}", [P, 2]),
                rs0=tmp(f"rs0_s{s}", [P, 1]),
                rs=tmp(f"rs_s{s}", [P, 1]),
                ss=tmp(f"ss_s{s}", [P, 2 * LH]),
                rn=tmp(f"rn_s{s}", [P, 2 * LH]),
                mx=tmp(f"mxl_s{s}", [P, LH]),
                z=tmp(f"z_s{s}", [P, LH]),
                rz=tmp(f"rz_s{s}", [P, LH]),
                o=tmp(f"o_s{s}", [P, D]),
            ) | {"bk": 4 * s} for s in range(2)]

        psum = ctx.enter_context(nc.psum_tensor("psum", [P, 8, HALF], F32))

        def bank_bf16(k):
            return psum[:, k, :].bitcast(BF16)

        s_wts = sem("s_wts")
        s_wf = sem("s_wf")
        s_id = sem("s_id")
        s_set_act = sem("s_set_act")
        s_set_dve = sem("s_set_dve")
        s_set_pe = sem("s_set_pe")
        s_set_out = sem("s_set_out")
        s_x_in = sem("s_x_in")
        s_mod_in = sem("s_mod_in")
        s_stats1 = sem("s_stats1")
        s_ln1 = sem("s_ln1")
        s_hn = sem("s_hn")
        s_wga = sem("s_wga")
        s_ones = sem("s_ones")
        s_hT_ps = sem("s_hT_ps")
        s_hT = sem("s_hT")
        s_proj = sem("s_proj")
        s_part = sem("s_part")
        s_parts_out = [sem(f"s_parts_out{k}") for k in range(4)]
        s_v_ps = sem("s_v_ps")
        s_v = sem("s_v")
        s_z = sem("s_z")
        s_z_exp = sem("s_z_exp")
        s_gate = sem("s_gate")
        s_stack_in = [sem(f"s_stack_in{k}") for k in range(2)]
        s_s_ps = sem("s_s_ps")
        s_max = sem("s_max")
        s_msplit = sem("s_msplit")
        s_mT_ps = sem("s_mT_ps")
        s_mrow = sem("s_mrow")
        s_m_in = [sem(f"s_m_in{k}") for k in range(2)]
        s_vg = sem("s_vg")
        s_st_ps = sem("s_st_ps")
        s_exp = sem("s_exp")
        s_pv = sem("s_pv")
        s_osb = sem("s_osb")
        s_oT_ps = sem("s_oT_ps")
        s_den = sem("s_den")
        s_conv = sem("s_conv")
        s_cvT_ps = sem("s_cvT_ps")
        s_cvT = [sem(f"s_cvT_{e}") for e in ("act", "dve")]
        s_att_ps = sem("s_att_ps")
        s_x1 = sem("s_x1")
        s_xr_in = sem("s_xr_in")
        s_x1_out = sem("s_x1_out")
        s_xs0_in = sem("s_xs0_in")
        s_xs_in = sem("s_xs_in")
        s_tab_in = sem("s_tab_in")
        s_zero = sem("s_zero")
        for s in range(2):
            S[s].update({"s_" + n: sem(f"s{s}_{n}") for n in (
                "mask_in ln0_ag ln0_rs ln0 uT_ps carry uT qkv sq vev ssum "
                "rn rope kn qkT_ps qz kT s_ps sm exp rz pn pT_ps pT o_ps oT kvprev "
                "wo_ps u1 sh_ps sh ub ln_ag ln_rs hl hl_ps hlT g_ps gelu act w2_ps u2 "
                "oo out").split()})
        X, Y = S

        def half(l, it, do, prev=True):
            before = (1 - l, it - 1 if l == 0 else it)
            for step in ("Xw2 Ys2 XuT Ys3 Xq01 Yp Xq2a Ywoa Ywob Xt Ysh Xq2b Xs0 Xs1 Xs2 Yh Xs3 Yw1a Yw1b "
                         "Xp | Yw2 Xwoa YuT Xwob Yq0a Xsh Yq0b Yq2a Xh Yq2b Xw1a Yt Xw1b Ys0 Ys1").split():
                if step == "|":
                    prev, before = True, (l, it)
                elif step[0] == "X":
                    do(step[1:], X, l, it)
                elif prev:
                    do(step[1:], Y, *before)

        def windows(eng, step):
            def pair(i, more):
                with eng.Fori(1, NT - 1) as t:
                    step(i, t, i * NT + t)
                step(i, NT - 1, i * NT + (NT - 1))
                if more:
                    step(i + 1, 0, i * NT + NT)
            with eng.Fori(0, PAIRS - 1) as i:
                pair(i, True)
            pair(PAIRS - 1, False)

        def is_window(t, n):
            return isinstance(t, int) and t == n

        def interleave(score, tile, rows):
            steps = [*range(DC), "add"]
            for t in range(2):
                tile(t, steps)
            later = [(t, step) for t in range(2, NT) for step in steps]
            for q in range(AHEAD):
                if q == MU + 4:
                    rows()
                score(q)
                if 5 <= q < 5 + 2 * len(later) and q % 2:
                    t, step = later[(q - 5) // 2]
                    tile(t, [step])

        block = ctx.enter_context(nc.Block())

        loads = [0, 0]

        @block.sync
        def _(sp):
            def load(dst, src):
                loads[0] += 1
                sp.dma_start(dst, src).then_inc(s_wts, 16)

            def load_f(dst, src):
                loads[1] += 1
                sp.dma_start(dst, src).then_inc(s_wf, 16)

            def x_load(dst, b):
                return sp.dma_start(dst[:].unsqueeze(1), x.rearrange("b (t p) d -> p b t d", p=P)[:, bass.ds(b, 1)])

            x_load(hn, 0).then_inc(s_x_in, 16)
            with nc.allow_non_contiguous_dma("small set-up vectors"):
                for k in range(DC):
                    load(cT[:, k, :], c.rearrange("b (k p) -> k p b", p=P)[k])
                load(wmod_sb[:], wmod.rearrange("(k p) n -> p k n", p=P))
                load(hv[:], head_vec)
                load(sgnc[:], sgn)
                load(wout_sb[:, 0], Wout.rearrange("(k p) n -> p k n", p=P))
                load(wout_sb[:, 1], Wout_sw.rearrange("(k p) n -> p k n", p=P))
                load(rope_sb[:], rope)
                for l in range(LAYERS):
                    for n, v in ((0, q_scale), (1, k_scale)):
                        load(scl[:, l, n, :], v[l].partition_broadcast(P))
                        load(scl[:, l, 2 + n, 0:LD // 2], v[l, LD // 2:LD].partition_broadcast(P))
                        load(scl[:, l, 2 + n, LD // 2:LD], v[l, 0:LD // 2].partition_broadcast(P))
                load(wi_sb[:, 0], Wi.rearrange("(k p) n -> p k n", p=P))
                load(wi_sb[:, 1], Wo.rearrange("(k p) n -> p k n", p=P))
                load(wvea[:, :, 0:D], Wv.rearrange("(k p) n -> p k n", p=P))
                load(wvea[:, :, D:D + H], We.rearrange("(k p) n -> p k n", p=P))
                load(wvea[:, :, D + H:D + NEA], Wa.rearrange("(k p) n -> p k n", p=P))
                load(bias_ea[:, 0:H], be.partition_broadcast(P))
                load(bias_ea[:, H:NEA], ba.partition_broadcast(P))
            md = mod_d.rearrange("b n -> (b n)")

            def modulation(b):
                sp.dma_start(modA[:].rearrange("p a d -> p (a d)"),
                             md[bass.ds(b * (6 * D), 3 * D)].partition_broadcast(P)).then_inc(s_mod_in, 16)

            sp.wait_ge(s_set_dve, SET_MOD)
            sp.nop(nofuse=True)
            sp.dma_start(mod_d, modsb[:]).then_inc(s_set_out, 16)
            sp.wait_ge(s_set_out, 16)
            sp.nop(nofuse=True)
            modulation(0)
            sp.wait_ge(s_set_dve, SET_ALL)
            sp.nop(nofuse=True)
            for l in range(LAYERS):
                sp.dma_start(tab_d.rearrange("t p (l n) -> l p t n", l=LAYERS)[l],
                             tabs[:, :, l].rearrange("p t a d -> p t (a d)")).then_inc(s_set_out, 16)
            sp.wait_ge(s_set_out, 16 * (1 + LAYERS))
            sp.nop(nofuse=True)

            def next_x(b):
                sp.wait_ge(s_wga, b)
                sp.nop(nofuse=True)
                modulation(b)
                sp.wait_ge(s_vg, b * (2 * NG))
                sp.nop(nofuse=True)
                x_load(hn, b).then_inc(s_x_in, 16)

            def split_out(b):
                for n in range(BLOCKS):
                    sp.wait_ge(s_part, b * (4 * BLOCKS) + (4 * n + 4))
                    sp.nop(nofuse=True)
                    qk, m, h = n // 4, (n // 2) % 2, n % 2
                    sp.dma_start(parts_d[qk, :, m * P:(m + 1) * P, h * HALF:(h + 1) * HALF]
                                 .rearrange("a p t -> p a t"), parts[:, n % 4]).then_inc(s_parts_out[n % 4], 16)
                for k in range(4):
                    sp.wait_ge(s_parts_out[k], FREE + b * 32 + 32)
                    sp.nop(nofuse=True)

            def stacks(b, g, prev=True):
                if g > 1:
                    sp.wait_ge(s_st_ps, b * (NU * 16) + 32 * (g - 1))
                    sp.nop(nofuse=True)
                elif prev:
                    sp.wait_ge(s_st_ps, b * (NU * 16) + 32 * (g - 1))
                    sp.nop(nofuse=True)
                for qk, order in ((0, PAIRS_Q), (1, PAIRS_K)):
                    for s, part in enumerate(order):
                        sp.dma_start(
                            stack[s * DH:(s + 1) * DH, g % 2, qk],
                            parts_d[qk, part, g * G * DH:(g + 1) * G * DH, :].rearrange("(h i) (a t) -> i a h t", i=DH, a=NH)
                        ).then_inc(s_stack_in[g % 2], 16)

            def maxima_in(b, u):
                sp.wait_ge(s_mrow, b * NU + u + 1)
                sp.nop(nofuse=True)
                for s in range(PART):
                    sp.dma_start(
                        stack[KS + s:KS + s + 1, (u // 2) % 2, 0, u % 2].rearrange("o h (a q) -> o (h a) q", q=P),
                        mrow[s * TU:(s + 1) * TU, u % 2, :]
                    ).then_inc(s_m_in[u % 2], 16)

            def x_in(b, prev=True):
                if prev:
                    sp.wait_ge(s_x1_out, b * 16)
                    sp.nop(nofuse=True)
                x_load(xr, b).then_inc(s_xr_in, 16)

            def x1_out(b):
                sp.wait_ge(s_x1, FREE + b * NT + NT)
                sp.nop(nofuse=True)
                sp.dma_start(x1_d.rearrange("b (t p) d -> p b t d", p=P)[:, bass.ds(b, 1)], xr[:].unsqueeze(1)).then_inc(s_x1_out, 16)

            def batch(b, more):
                for u in range(1, NU):
                    maxima_in(b, u)
                    if u % 2 == 0 and u < NU - 2:
                        stacks(b, u // 2 + 1)
                    if u == NU - 4 and more:
                        next_x(b + 1)
                if more:
                    split_out(b + 1)
                    stacks(b + 1, 0)
                    stacks(b + 1, 1)
                    maxima_in(b + 1, 0)
                x1_out(b)
                if more:
                    x_in(b + 1)
            x_in(0, prev=False)
            split_out(0)
            for g in range(2):
                stacks(0, g, prev=False)
            maxima_in(0, 0)
            with nc.allow_non_contiguous_dma("small set-up vectors"):
                for l in range(LAYERS):
                    load_f(wqkv_sb[:, l], wqkv[l].rearrange("(k p) n -> p k n", p=P))
                    load_f(wo_sb[:, l], wo[l].rearrange("(k p) n -> p k n", p=P))
                    load_f(w1_sb[:, l], w1[l].rearrange("(k p) n -> p k n", p=P))
                    load_f(w2_sb[:, l, 0:FC - 1], w2[l, 0:(FC - 1) * P].rearrange("(k p) n -> p k n", p=P))
                    load_f(w2_sb[0:FR, l, FC - 1], w2[l, (FC - 1) * P:HID])
                    for n in range(2):
                        o = n * HID
                        load_f(b1_sb[:, l, n, 0:FC - 1], b1[l, o:o + (FC - 1) * P].rearrange("(k p) -> p k", p=P))
                        load_f(b1_sb[0:FR, l, n, FC - 1:FC], b1[l, o + (FC - 1) * P:o + HID].unsqueeze(1))
                    load_f(b2_sb[:, l], b2[l].partition_broadcast(P))
                    load_f(lnv[:, l, 0], ln_g[l].rearrange("(k p) -> p k", p=P))
                    load_f(lnv[:, l, 1], ln_b[l].rearrange("(k p) -> p k", p=P))
            with sp.Fori(0, B - 1) as b:
                batch(b, True)
            batch(B - 1, False)
            sp.wait_ge(s_x1_out, B * 16)
            sp.nop(nofuse=True)

            def pair_in(i, last):
                done, lo, hi = (s_xs_in, NT - 1, NT) if last else (s_xs0_in, 0, NT - 1)
                for s in range(2):
                    if last:
                        sp.dma_start(gateF[:, s], md[bass.ds(i * (12 * D) + (6 * s + 5) * D, D)].partition_broadcast(P)) \
                            .then_inc(done, 16)
                    else:
                        sp.dma_start(modF[:, s].rearrange("p a d -> p (a d)"),
                                     md[bass.ds(i * (12 * D) + (6 * s + 3) * D, 2 * D)].partition_broadcast(P)).then_inc(done, 16)
                    sp.dma_start(xs[:, s, lo:hi].unsqueeze(1),
                                 x1_d.rearrange("b (t p) d -> p b t d", p=P)[:, bass.ds(i * 2 + s, 1), lo:hi]).then_inc(done, 16)

            def tables(t, it, wait):
                if wait:
                    for w in S:
                        sp.wait_ge(w["s_kn"], it * 2)
                        sp.nop(nofuse=True)
                sp.dma_start(tab[:].rearrange("p l a d -> p (l a d)"),
                             tab_d[bass.ds(t, 1)].rearrange("o p n -> p (o n)")).then_inc(s_tab_in, 16)

            def masks(w, t, it, wait):
                if wait:
                    sp.wait_ge(w["s_sm"], it * 8)
                    sp.nop(nofuse=True)
                sp.dma_start(w["mask"][:], mask[bass.ds(t, 1)].rearrange("o p n -> p (o n)")).then_inc(w["s_mask_in"], 16)

            def store(w, s, i, t, it):
                sp.wait_ge(w["s_oo"], it * 2 + 2)
                sp.nop(nofuse=True)
                sp.dma_start(out.rearrange("(i j) (t p) d -> i j t p d", j=2, p=P)[bass.ds(i, 1), s, bass.ds(t, 1)]
                             .rearrange("o q p d -> p (o q d)"), w["o"][:]).then_inc(w["s_out"], 16)

            def window(i, t, it, prev=True):
                before = (i - 1, NT - 1) if is_window(t, 0) else (i, t - 1)
                tables(t, it, prev)
                for s, w in enumerate(S):
                    masks(w, t, it, prev)
                    if prev:
                        store(w, s, *before, it - 1)
                if is_window(t, NT - 1) and not isinstance(i, int):
                    for w in S:
                        sp.wait_ge(w["s_ln0"], it * 3 + 3)
                        sp.nop(nofuse=True)
                    pair_in(i + 1, False)
                if is_window(t, 0) and prev:
                    pair_in(i, True)
            pair_in(0, False)
            pair_in(0, True)
            window(0, 0, 0, prev=False)
            windows(sp, window)
            for s, w in enumerate(S):
                store(w, s, PAIRS - 1, NT - 1, PAIRS * NT - 1)
            for w in S:
                sp.wait_ge(w["s_out"], FREE + 16 * PAIRS * NT)
                sp.nop(nofuse=True)

        @block.tensor
        def _(pe):
            pe.wait_ge(s_wts, 16 * loads[0])
            pe.wait_ge(s_id, ID_ALL)
            pe.wait_ge(s_set_dve, SET_SILU)
            for n in range(3):
                for k in range(DC):
                    mm = pe.matmul(psum[0:B, n, :], cT[:, k, :], wmod_sb[:, k, n * HALF:(n + 1) * HALF],
                                   start=(k == 0), stop=(k == DC - 1))
            mm.then_inc(s_set_pe, 1)
            pe.wait_ge(s_set_dve, SET_ALL)

            pe.wait_ge(s_ones, 3)

            def hT_group(b, c, prev):
                k, hf = c // 2, c % 2
                if c == 0:
                    pe.wait_ge(s_hn, b * 2 + 2)
                if c >= 2:
                    pe.wait_ge(s_hT, b * 4 + c - 1)
                elif prev:
                    pe.wait_ge(s_max, b * (NU * MU) + (c - 1))
                for t in range(4):
                    mm = pe.transpose(psum[:, 6 + c % 2, t * P:(t + 1) * P], hn[:, 4 * hf + t, k * P:(k + 1) * P], ident[:])
                mm.then_inc(s_hT_ps, 1)

            def project(b, n, k):
                qk, m, h = n // 4, (n // 2) % 2, n % 2
                if n == 0 and k == 0:
                    pe.wait_ge(s_hT, b * 4 + 4)
                if n >= 2 and k == 0:
                    pe.wait_ge(s_part, b * (4 * BLOCKS) + (4 * (n - 2) + 2))
                mm = pe.matmul(psum[:, 6 + n % 2, :], wi_sb[:, qk, k, m * P:(m + 1) * P],
                               hT[:, k, h * HALF:(h + 1) * HALF], start=(k == 0), stop=(k == DC - 1))
                if k == DC - 1:
                    mm.then_inc(s_proj, 1)

            def v_tile(b, t, prev):
                if t == 0 and prev:
                    pe.wait_ge(s_exp, b * (NU * 16))
                if t >= 4:
                    pe.wait_ge(s_v, b * NT + t - 3)
                    pe.wait_ge(s_z, b * NT + t - 3)
                for k in range(DC):
                    mm = pe.matmul(psum[:, t % 4, 0:D + NEA], hT[:, k, t * P:(t + 1) * P], wvea[:, k, :],
                                   start=(k == 0), stop=(k == DC - 1))
                mm.then_inc(s_v_ps, 1)

            def v_done(b):
                pe.wait_ge(s_v, b * NT + NT)
                pe.wait_ge(s_z, b * NT + NT)

            def score_job(b, q):
                u, m, kh = q // MU, (q % MU) // NH, q % NH
                g, h, a = u // 2, m // (NT // NH), m % (NT // NH)
                if q % (2 * MU) == 0:
                    pe.wait_ge(s_stack_in[g % 2], b * (STACK_IN * 2) + STACK_IN * (g // 2 + 1))
                if q >= 2:
                    pe.wait_ge(s_max, b * (NU * MU) + (q - 1))
                else:
                    pe.wait_ge(s_part, b * (4 * BLOCKS) + (4 * (6 + q) + 2))
                pe.matmul(psum[:, 6 + kh, :], stack[0:KS, g % 2, 0, u % 2, h, a * P:(a + 1) * P],
                          stack[0:KS, g % 2, 1, kh, h, :], start=True, stop=True).then_inc(s_s_ps, 1)

            def maxima(b, u):
                pe.wait_ge(s_msplit, b * (NU * 5) + (u * 5 + 5))
                if u > 1:
                    pe.wait_ge(s_conv, b * NU + u - 1)
                pe.nop(nofuse=True)
                pe.transpose(bank_bf16(4 + u % 2)[0:PART * TU, 0:P], m3[:].rearrange("p a m -> p (a m)"), identb[:]) \
                    .then_inc(s_mT_ps, 1)

            def st(b, e, pair):
                u, kc = e // NT, e % NT
                if kc == 0 and pair == 0:
                    pe.wait_ge(s_m_in[u % 2], FREE + b * (48 * NG) + 48 * (u // 2 + 1))
                if 2 * e + pair >= 2:
                    pe.wait_ge(s_exp, b * (NU * 16) + (2 * e + pair - 1))
                for h in (2 * pair, 2 * pair + 1):
                    mm = pe.matmul(psum[:, h, :], stack[0:KS + PART, (u // 2) % 2, 1, kc // 4, h, (kc % 4) * P:(kc % 4 + 1) * P],
                                   stack[0:KS + PART, (u // 2) % 2, 0, u % 2, h, :], start=True, stop=True)
                mm.then_inc(s_st_ps, 1)

            def pv(b, e, pair):
                u, kc = e // NT, e % NT
                if pair == 0:
                    pe.wait_ge(s_exp, b * (NU * 16) + (2 * e + 2))
                    if kc == 0:
                        pe.wait_ge(s_vg, b * (NG * 2) + (u // 2 * 2 + 2))
                for h in (2 * pair, 2 * pair + 1):
                    mm = pe.matmul(psum[h * VW:(h + 1) * VW, 4 + u % 2, :], vg[:, (u // 2) % 2, kc, h, :],
                                   pr[:, e % 2, h, :], start=(kc == 0), stop=(kc == NT - 1))
                if pair == 1:
                    mm.then_inc(s_pv, 1)

            def result(b, u):
                pe.wait_ge(s_osb, b * NU + u + 1)
                for t in range(NT // NH):
                    mm = pe.transpose(psum[:, 4 + u % 2, t * P:(t + 1) * P], o_sb[:, t * P:(t + 1) * P], ident[:])
                mm.then_inc(s_oT_ps, 1)

            def cv_group(b, c):
                hf, k = c // 2, c % 2
                if c == 0:
                    pe.wait_ge(s_conv, b * NU + NU)
                for t in range(4):
                    mm = pe.transpose(psum[:, CV_BANKS[c], t * P:(t + 1) * P], cv[:, 4 * hf + t, k * P:(k + 1) * P], ident[:])
                mm.then_inc(s_cvT_ps, 1)

            def out_tile(b, t, steps=range(DC)):
                if t == 0 and 0 in steps:
                    for e in range(2):
                        pe.wait_ge(s_cvT[e], b * 2 + 2)
                    pe.wait_ge(s_wga, b + 1)
                if t >= 2 and 0 in steps:
                    pe.wait_ge(s_x1, FREE + b * NT + t - 1)
                for k in (k for k in steps if k != "add"):
                    mm = pe.matmul(psum[:, 2 + t % 2, 0:D], cvT[:, k, t * P:(t + 1) * P], wga[:, k, :],
                                   start=(k == 0), stop=(k == DC - 1))
                    if k == DC - 1:
                        mm.then_inc(s_att_ps, 1)

            def start(b, last=None):
                interleave(lambda q: score_job(b, q), lambda t, steps: last is not None and out_tile(last, t, steps),
                           lambda: maxima(b, 0))
                if last is not None:
                    pe.wait_ge(s_x1, FREE + last * NT + NT)
                st(b, 0, 0)
                st(b, 0, 1)

            def batch(b, more):
                for e in range(NU * NT):
                    u, kc = e // NT, e % NT
                    jobs = range(min(AHEAD + 4 * e, NU * MU), min(AHEAD + 4 * e + 4, NU * MU))
                    ahead = e - NEXT
                    for k in range(4):
                        if k < 2:
                            if e + 1 < NU * NT:
                                st(b, e + 1, k)
                        else:
                            pv(b, e, k - 2)
                        if k < len(jobs):
                            score_job(b, jobs[k])
                        if k < 2 and more and 0 <= ahead < 2:
                            hT_group(b + 1, 2 * ahead + k, True)
                        if k < 2 and more and 2 <= ahead < 2 + BLOCKS:
                            project(b + 1, ahead - 2, k)
                        if k == 1 and kc == 2 and u > 0:
                            result(b, u - 1)
                        if k == 1 and kc == 5 and u + 1 < NU:
                            maxima(b, u + 1)
                if more:
                    for t in range(2):
                        v_tile(b + 1, t, True)
                result(b, NU - 1)
                if more:
                    for t in range(2, NT):
                        v_tile(b + 1, t, True)
                for c in range(2):
                    cv_group(b, c)
                if more:
                    v_done(b + 1)
                else:
                    pe.wait_ge(s_exp, b * (NU * 16) + NU * 16)
                for c in range(2, 4):
                    cv_group(b, c)
                if more:
                    start(b + 1, last=b)
                else:
                    for t in range(NT):
                        out_tile(b, t)

            for c in range(4):
                hT_group(0, c, False)
            for n in range(BLOCKS):
                for k in range(DC):
                    project(0, n, k)
            for t in range(NT):
                v_tile(0, t, False)
            v_done(0)
            start(0)
            with pe.Fori(0, B - 1) as b:
                batch(b, True)
            batch(B - 1, False)

            def w2_block(w, l, n):
                bk = w["bk"]
                hid = w["pT"][:].rearrange("p h k n -> p (h k) n")
                pe.wait_ge(w["s_act"], n * FC + FC)
                for cc in range(FC):
                    rows = P if cc < FC - 1 else FR
                    mm = pe.matmul(psum[:, bk, 0:D], hid[0:rows, cc, :], w2_sb[0:rows, l, cc, :],
                                   start=(cc == 0), stop=(cc == FC - 1))
                mm.then_inc(w["s_w2_ps"], 1)

            def blk(name, w, l, it, prev=True):
                n, bk = it * 2 + l, w["bk"]
                if name == "w2":
                    if prev:
                        w2_block(w, 1 - l, n - 1)
                elif name == "uT":
                    src = w["u0"] if l == 0 else w["u"]
                    if l == 0:
                        pe.wait_ge(w["s_ln0"], it * 3 + 3)
                    if l == 1 or prev:
                        pe.wait_ge(w["s_u2"], n)
                    for k in range(DC):
                        mm = pe.transpose(psum[:, bk, k * P:(k + 1) * P], src[:, k * P:(k + 1) * P], ident[:])
                    mm.then_inc(w["s_uT_ps"], 1)
                elif name in ("q01", "q0a", "q0b", "q2a", "q2b"):
                    if name in ("q01", "q0a"):
                        pe.wait_ge(w["s_uT"], n + 1)
                    steps = [(m, k) for m in range(3) for k in range(DC)]
                    steps = {"q01": steps[:2 * DC], "q0a": steps[:1], "q0b": steps[1:2 * DC],
                             "q2a": steps[2 * DC:-1], "q2b": steps[-1:]}[name]
                    for m, k in steps:
                        mm = pe.matmul(psum[:, bk + m, :], w["uT"][:, l, k * (P + 1):k * (P + 1) + P],
                                       wqkv_sb[:, l, k, m * INNER:(m + 1) * INNER],
                                       start=(k == 0), stop=(k == DC - 1))
                    if name not in ("q0a", "q2a"):
                        mm.then_inc(w["s_qkv"], 1)
                elif name == "t":
                    qk = w["big"][:].rearrange("p h n -> p (h n)")
                    for m in range(2 * INNER // P):
                        if m == 0:
                            pe.wait_ge(w["s_rope"], n * 4 + 3)
                        elif m == 4:
                            pe.wait_ge(w["s_kn"], n + 1)
                        mm = pe.transpose(psum[:, bk + m // 4, (m % 4) * P:(m % 4 + 1) * P],
                                          qk[:, m * P:(m + 1) * P], ident[:])
                        if m % 4 == 3:
                            mm.then_inc(w["s_qkT_ps"], 1)
                elif name in ("s0", "s1", "s2", "s3"):
                    if name == "s0":
                        pe.wait_ge(w["s_qz"], n + 1)
                        pe.wait_ge(w["s_kT"], n + 1)
                    if name == "s2":
                        pe.wait_ge(w["s_vev"], n + 1)
                    for h in (2 * int(name[1]), 2 * int(name[1]) + 1):
                        mm = pe.matmul(psum[:, bk + h // 2, (h % 2) * 2 * P:(h % 2 + 1) * 2 * P], w["qz"][:, h, :],
                                       w["kT"][:, l, h // 2, :], start=True, stop=True)
                    mm.then_inc(w["s_s_ps"], 1)
                elif name == "p":
                    for h in range(LH):
                        if h % 2 == 0:
                            pe.wait_ge(w["s_pn"], n * 4 + (h // 2 + 1))
                        for kb in range(2):
                            mm = pe.transpose(psum[:, bk + h // 2, (2 * (h % 2) + kb) * P:(2 * (h % 2) + kb + 1) * P],
                                              w["big"][:, h, kb * P:(kb + 1) * P], ident[:])
                        if h % 2:
                            mm.then_inc(w["s_pT_ps"], 1)
                    for m in range(LH // 2):
                        pe.wait_ge(w["s_pT"], n * 4 + (m + 1))
                        for kb in range(2):
                            for h in (2 * m, 2 * m + 1):
                                mm = pe.matmul(psum[(h % 2) * LD:(h % 2 + 1) * LD, bk, m * P:(m + 1) * P],
                                               w["v"][:, l, kb, h * LD:(h + 1) * LD], w["pT"][:, h, kb, :],
                                               start=(kb == 0), stop=(kb == 1))
                    mm.then_inc(w["s_o_ps"], 1)
                elif name in ("woa", "wob"):
                    if name == "woa":
                        pe.wait_ge(w["s_oT"], n + 1)
                    half_k = INNER // P // 2
                    for k in range(half_k) if name == "woa" else range(half_k, 2 * half_k):
                        mm = pe.matmul(psum[:, bk + 1, 0:D], w["oT"][:, k, :], wo_sb[:, l, k, :],
                                       start=(k == 0), stop=(k == INNER // P - 1))
                    if name == "wob":
                        mm.then_inc(w["s_wo_ps"], 1)
                elif name == "sh":
                    pe.wait_ge(w["s_u1"], n + 1)
                    pe.matmul(psum[:, bk + 2, 0:P], turned[:], w["u"][:, P:D], start=True, stop=True) \
                        .then_inc(w["s_sh_ps"], 1)
                elif name == "h":
                    pe.wait_ge(w["s_hl"], n * 2 + 2)
                    for k in range(DC):
                        mm = pe.transpose(psum[:, bk, k * P:(k + 1) * P], w["hl"][:, k * P:(k + 1) * P], ident[:])
                    mm.then_inc(w["s_hl_ps"], 1)
                elif name in ("w1a", "w1b"):
                    if name == "w1a":
                        pe.wait_ge(w["s_hlT"], n * 2 + 2)
                    for m in range(2 * FC - 2) if name == "w1a" else range(2 * FC - 2, 2 * FC):
                        cc, rows = m % FC, P if m % FC < FC - 1 else FR
                        col = (HID if m < FC else 0) + cc * P
                        for k in range(DC):
                            mm = pe.matmul(psum[0:rows, bk + 1 + m // 4, (m % 4) * P:(m % 4 + 1) * P],
                                           w1_sb[:, l, k, col:col + rows], w["hlT"][:, k, :],
                                           start=(k == 0), stop=(k == DC - 1))
                        if m % 4 == 3:
                            mm.then_inc(w["s_g_ps"], 1)
                else:
                    raise ValueError(name)

            pe.wait_ge(s_wf, 16 * loads[1])
            half(0, 0, lambda name, w, l, it: blk(name, w, l, it, prev=l == 1), prev=False)
            half(1, 0, blk)

            def window(i, t, it):
                for l in range(LAYERS):
                    half(l, it, blk)
            windows(pe, window)
            last = PAIRS * NT - 1
            w2_block(X, 1, last * 2 + 1)
            for name in ("s2", "s3", "p", "woa", "wob", "sh", "h", "w1a", "w1b"):
                blk(name, Y, 1, last)
            w2_block(Y, 1, last * 2 + 1)

        @block.scalar
        def _(act):
            act.wait_ge(s_wts, 16 * loads[0])
            act.activation(ce[:], cT[:], ACT.Exp, scale=-1.0).then_inc(s_set_act, 1)
            act.activation(he[:, 0:3], hv[:, 0:3], ACT.Exp, scale=-1.0).then_inc(s_set_act, 1)
            act.activation(he[:, 3], hv[:, 3], ACT.Tanh).then_inc(s_set_act, 1)
            act.wait_ge(s_set_dve, SET_ANGLE)
            act.activation(hc[:, 4], hc[:, 2], ACT.Sin).then_inc(s_set_act, 1)
            act.activation(hc[:, 5], hc[:, 3], ACT.Sin).then_inc(s_set_act, 1)

            def values(b):
                for t in range(NT):
                    act.wait_ge(s_v_ps, b * NT + t + 1)
                    act.activation(vt[:, t, :], psum[:, t % 4, 0:D], ACT.Copy).then_inc(s_v, 1)

            def gates(b):
                act.wait_ge(s_z, b * NT + NT)
                act.activation(zt[:], zt[:], ACT.Exp, scale=-1.0).then_inc(s_z_exp, 1)

            def take_result(b, u):
                act.wait_ge(s_pv, b * (NU * NT) + (u * NT + NT))
                if u > 0:
                    act.wait_ge(s_oT_ps, b * NU + u)
                act.activation(o_sb[:], psum[:, 4 + u % 2, :], ACT.Copy).then_inc(s_osb, 1)

            def batch(b, more):
                for e in range(NU * NT):
                    for pair in range(2):
                        act.wait_ge(s_st_ps, b * (NU * 16) + (2 * e + pair + 1))
                        if e >= 2:
                            act.wait_ge(s_pv, b * (NU * NT) + (e - 1))
                        act.activation(pr[:, e % 2, 2 * pair:2 * pair + 2, :], psum[:, 2 * pair:2 * pair + 2, :],
                                       ACT.Exp, scale=DH ** -0.5).then_inc(s_exp, 1)
                    if e % NT == 1 and e > NT:
                        take_result(b, e // NT - 1)
                take_result(b, NU - 1)
                if more:
                    values(b + 1)
                for n, c in enumerate((0, 2)):
                    act.wait_ge(s_cvT_ps, b * 4 + c + 1)
                    act.activation(cvT[:, c % 2, (c // 2) * HALF:(c // 2 + 1) * HALF], psum[:, CV_BANKS[c], :], ACT.Copy) \
                        .then_inc(s_cvT[0], 1)
                if more:
                    gates(b + 1)
            values(0)
            gates(0)
            with act.Fori(0, B - 1) as b:
                batch(b, True)
            batch(B - 1, False)

            def blk(name, w, l, it):
                n, bk = it * 2 + l, w["bk"]
                if name == "A":
                    act.wait_ge(w["s_qkv"], n * 2 + 1)
                    act.activation(w["pT"][:].rearrange("p h k n -> p (h k n)")[:, 0:2 * INNER]
                                   .rearrange("p (a n) -> p a n", a=2), psum[:, bk:bk + 2, :], ACT.Square) \
                        .then_inc(w["s_sq"], 1)
                elif name == "V":
                    act.wait_ge(w["s_qkv"], n * 2 + 2)
                    act.wait_ge(w["s_kvprev"], FREE + it * 4)
                    act.activation(w["v"][:, l, 1, :], psum[:, bk + 2, :], ACT.Copy).then_inc(w["s_vev"], 1)
                elif name == "B":
                    act.wait_ge(w["s_qkT_ps"], n * 2 + 1)
                    for hh in range(2):
                        ins = act.activation(w["qz"][hh * LD:(hh + 1) * LD, hh:LH:2, :],
                                             psum[hh * LD:(hh + 1) * LD, bk, :].rearrange("p (m q) -> p m q", q=P),
                                             ACT.Copy)
                    ins.then_inc(w["s_qz"], 1)
                elif name == "E":
                    for h in range(LH):
                        if h % 4 == 0:
                            act.wait_ge(w["s_sm"], n * 4 + (h // 4 * 2 + 2))
                        ins = act.activation(w["big"][:, h, :], w["big"][:, h, :], ACT.Exp, bias=w["mx"][:, h:h + 1],
                                             accum_out=w["z"][:, h:h + 1])
                        if h % 2:
                            ins.then_inc(w["s_exp"], 1)
                elif name == "C":
                    for m in range(4):
                        act.wait_ge(w["s_pT_ps"], n * 4 + m + 1)
                        act.activation(w["pT"][:, 2 * m:2 * m + 2], psum[:, bk + m, :]
                                       .rearrange("p (h k n) -> p h k n", h=2, k=2), ACT.Copy).then_inc(w["s_pT"], 1)
                    act.wait_ge(w["s_o_ps"], n + 1)
                    act.activation(w["oT"][:].rearrange("p a n -> p (a n)"), psum[:, bk, :], ACT.Copy) \
                        .then_inc(w["s_oT"], 1)
                elif name == "H":
                    act.wait_ge(w["s_hl_ps"], n + 1)
                    for k in range(DC):
                        act.activation(w["hlT"][:, k, :], psum[:, bk, k * P:(k + 1) * P], ACT.Identity,
                                       scale=lnv[:, l, 0, k:k + 1], bias=lnv[:, l, 1, k:k + 1]).then_inc(w["s_hlT"], 1)
                elif name == "D":
                    gl = w["pT"][:].rearrange("p h k n -> p (h k) n")
                    for cc in range(FC):
                        rows = P if cc < FC - 1 else FR
                        if cc % 4 == 0:
                            act.wait_ge(w["s_g_ps"], n * 3 + (cc // 4 + 1))
                        act.activation(gl[0:rows, cc, :], psum[0:rows, bk + 1 + cc // 4, (cc % 4) * P:(cc % 4 + 1) * P],
                                       ACT.Gelu, bias=b1_sb[0:rows, l, 1, cc:cc + 1]).then_inc(w["s_gelu"], 1)

            def turn(l, it, prev=True):
                before = (1 - l, it - 1 if l == 0 else it)
                if prev:
                    blk("E", Y, *before)
                blk("A", X, l, it)
                if prev:
                    blk("C", Y, *before)
                blk("B", X, l, it)
                blk("V", X, l, it)
                blk("E", X, l, it)
                if prev:
                    blk("D", Y, *before)
                blk("C", X, l, it)
                blk("A", Y, l, it)
                blk("H", X, l, it)
                blk("V", Y, l, it)
                blk("D", X, l, it)
                blk("B", Y, l, it)

            act.wait_ge(s_wf, 16 * loads[1])
            act.wait_ge(s_zero, 9)
            turn(0, 0, prev=False)
            turn(1, 0)

            def window(i, t, it):
                for l in range(LAYERS):
                    turn(l, it)
            windows(act, window)
            for name in "ECD":
                blk(name, Y, 1, PAIRS * NT - 1)

        @block.vector
        def _(dve):
            chain = [0]

            def link(ins):
                chain[0] += 1
                ins.then_inc(s_set_dve, 1)
                dve.wait_ge(s_set_dve, chain[0])

            def statistics(b, t):
                if t == 0:
                    dve.wait_ge(s_x_in, b * 16 + 16)
                dve.bn_stats(st1[:, t, :], hn[:, t, :]).then_inc(s_stats1, 1)

            def moments(b):
                dve.wait_ge(s_stats1, b * (2 * NT) + NT)
                dve.nop(nofuse=True)
                for t in range(NT):
                    dve.bn_aggr(mv1[:, t, :], st1[:, t, :]).then_inc(s_stats1, 1)

            for t in range(NT):
                statistics(0, t)
            moments(0)
            dve.wait_ge(s_wts, 16 * loads[0])
            dve.wait_ge(s_set_act, 1)
            link(dve.tensor_scalar(ce[:], ce[:], 1.0, None, ALU.add))
            link(dve.reciprocal(ce[:], ce[:]))
            link(dve.tensor_tensor(cT[:], cT[:], ce[:], ALU.mult))
            assert chain[0] == SET_SILU
            dve.wait_ge(s_set_act, 3)
            link(dve.tensor_scalar(he[:, 0:3], he[:, 0:3], 1.0, None, ALU.add))
            link(dve.reciprocal(he[:, 0:3], he[:, 0:3]))
            link(dve.tensor_scalar(hc[:, 2], he[:, 0], float(np.pi), None, ALU.mult))
            link(dve.tensor_scalar(hc[:, 3], hc[:, 2], -1.0, float(np.pi / 2), ALU.mult, ALU.add))
            assert chain[0] == SET_ANGLE
            link(dve.tensor_tensor(hc[:, 0], he[:, 1], he[:, 2], ALU.mult))
            link(dve.tensor_tensor(hc[:, 0], hc[:, 0], he[:, 3], ALU.mult))
            link(dve.tensor_tensor(sgnc[:], sgnc[:], hc[:, 0], ALU.mult))
            dve.wait_ge(s_set_pe, 1)
            link(dve.tensor_copy(modsb[:].rearrange("p (a n) -> p a n", a=3), psum[0:B, 0:3, :]))
            for n in (1, 4):
                link(dve.tensor_scalar(modsb[:, n * D:(n + 1) * D], modsb[:, n * D:(n + 1) * D], 1.0, None, ALU.add))
            for k, n in enumerate((2, 5)):
                g = modsb[:, n * D:(n + 1) * D]
                link(dve.tensor_scalar(sg[:, k], g, 0.0, 2.0, ALU.is_ge, ALU.mult))
                link(dve.tensor_scalar(sg[:, k], sg[:, k], -1.0, None, ALU.add))
                link(dve.tensor_tensor(g, g, sg[:, k], ALU.mult))
                link(dve.tensor_scalar(g, g, 0.25, None, ALU.max))
                link(dve.tensor_tensor(g, g, sg[:, k], ALU.mult))
            assert chain[0] == SET_MOD
            dve.wait_ge(s_set_act, 5)
            link(dve.tensor_tensor(hc[:, 4], hc[:, 4], sgnc[:], ALU.mult))
            link(dve.tensor_tensor(hc[:, 5], hc[:, 5], hc[:, 0], ALU.mult))
            for k in range(DC):
                link(dve.tensor_scalar(wout_sb[:, 0, k], wout_sb[:, 0, k], hc[:, 5, k:k + 1], None, ALU.mult))
                link(dve.scalar_tensor_tensor(out=wfold[:, k], in0=wout_sb[:, 1, k], scalar=hc[:, 4, k:k + 1],
                                              in1=wout_sb[:, 0, k], op0=ALU.mult, op1=ALU.add))
            for l in range(LAYERS):
                for a in range(4):
                    link(dve.tensor_tensor(tabs[:, :, l, a], rope_sb[:, :, a],
                                           scl[:, l, a].unsqueeze(1).broadcast_to([P, NT, LD]), ALU.mult))
            assert chain[0] == SET_ALL, chain[0]

            def take_hT(b, c):
                k, hf = c // 2, c % 2
                dve.wait_ge(s_hT_ps, b * 4 + c + 1)
                dve.tensor_copy(hT[:, k, hf * HALF:(hf + 1) * HALF], psum[:, 6 + c % 2, :]).then_inc(s_hT, 1)

            def split_block(b, n):
                c0, ps = b * (4 * BLOCKS), psum[:, 6 + n % 2, :]
                dve.wait_ge(s_proj, b * BLOCKS + n + 1)
                dve.wait_ge(s_parts_out[n % 4], FREE + b * 32 + 16 * (n // 4))
                dve.tensor_copy(parts[:, n % 4, 0], ps).then_inc(s_part, 1)
                dve.wait_ge(s_part, c0 + (4 * n + 1))
                dve.tensor_tensor(rest[:, n % 2], ps, parts[:, n % 4, 0], ALU.subtract).then_inc(s_part, 1)
                dve.wait_ge(s_part, c0 + (4 * n + 2))
                dve.tensor_copy(parts[:, n % 4, 1], rest[:, n % 2]).then_inc(s_part, 1)
                dve.wait_ge(s_part, c0 + (4 * n + 3))
                dve.tensor_tensor(parts[:, n % 4, 2], rest[:, n % 2], parts[:, n % 4, 1], ALU.subtract).then_inc(s_part, 1)

            def logits(b, prev):
                if prev:
                    dve.wait_ge(s_conv, b * NU)
                    dve.wait_ge(s_vg, b * (2 * NG))
                for t in range(NT):
                    dve.wait_ge(s_v_ps, b * NT + t + 1)
                    dve.wait_ge(s_v, b * NT + t + 1)
                    dve.tensor_tensor(zt[:, t, :], psum[:, t % 4, D:D + NEA], bias_ea[:], ALU.add).then_inc(s_z, 1)

            def gates(b):
                dve.wait_ge(s_z_exp, b + 1)
                dve.tensor_scalar(zt[:], zt[:], 1.0, None, ALU.add).then_inc(s_gate, 1)
                dve.wait_ge(s_gate, b * 3 + 1)
                dve.reciprocal(zt[:, :, 0:H], zt[:, :, 0:H]).then_inc(s_gate, 1)
                dve.tensor_scalar(zt[:, :, H:NEA], zt[:, :, H:NEA], 1e-8, None, ALU.mult).then_inc(s_gate, 1)

            def maximum(b, q):
                u, m, kh = q // MU, (q % MU) // NH, q % NH
                dve.wait_ge(s_s_ps, b * (NU * MU) + (q + 1))
                dve.tensor_reduce(mx[:, u % 2, m, kh:kh + 1], psum[:, 6 + kh, :], AX.X, ALU.max).then_inc(s_max, 1)

            def split(b, u):
                c0 = b * (NU * 5)
                dve.wait_ge(s_max, b * (NU * MU) + (u * MU + MU))
                if u > 0:
                    dve.wait_ge(s_mT_ps, b * NU + u)
                dve.tensor_tensor(m2[:], mx[:, u % 2, :, 0], mx[:, u % 2, :, 1], ALU.max).then_inc(s_msplit, 1)
                dve.wait_ge(s_msplit, c0 + (u * 5 + 1))
                dve.tensor_copy(m3[:, 0], m2[:]).then_inc(s_msplit, 1)
                dve.wait_ge(s_msplit, c0 + (u * 5 + 2))
                dve.tensor_tensor(mr[:], m2[:], m3[:, 0], ALU.subtract).then_inc(s_msplit, 1)
                dve.wait_ge(s_msplit, c0 + (u * 5 + 3))
                dve.tensor_copy(m3[:, 1], mr[:]).then_inc(s_msplit, 1)
                dve.wait_ge(s_msplit, c0 + (u * 5 + 4))
                dve.tensor_tensor(m3[:, 2], mr[:], m3[:, 1], ALU.subtract).then_inc(s_msplit, 1)

            def rows(b, u):
                dve.wait_ge(s_mT_ps, b * NU + u + 1)
                dve.wait_ge(s_m_in[u % 2], FREE + b * (48 * NG) + 48 * (u // 2))
                dve.tensor_copy(mrow[:, u % 2, :], bank_bf16(4 + u % 2)[0:PART * TU, 0:P]).then_inc(s_mrow, 1)

            def normalise(b, u):
                g, t0, nt = u // 2, (u % 2) * (NT // NH), NT // NH
                dve.wait_ge(s_oT_ps, b * NU + u + 1)
                ov = psum[:, 4 + u % 2, :].rearrange("p (t h w) -> p t h w", h=G, w=VW)
                c0 = b * (NU * 3)
                if u > 0:
                    dve.wait_ge(s_conv, b * NU + u)
                dve.tensor_tensor(den[:], ov[:, :, :, DH + 1], zt[:, t0:t0 + nt, H + G * g:H + G * (g + 1)], ALU.mult).then_inc(s_den, 1)
                dve.wait_ge(s_den, c0 + (u * 3 + 1))
                dve.tensor_tensor(den[:], ov[:, :, :, DH], den[:], ALU.add).then_inc(s_den, 1)
                dve.wait_ge(s_den, c0 + (u * 3 + 2))
                dve.reciprocal(den[:], den[:]).then_inc(s_den, 1)
                dve.wait_ge(s_den, c0 + (u * 3 + 3))
                dve.tensor_tensor(cv[:, t0:t0 + nt, G * DH * g:G * DH * (g + 1)].rearrange("p t (h i) -> p t h i", i=DH),
                                  ov[:, :, :, 0:DH], den[:].unsqueeze(3).broadcast_to([P, nt, G, DH]), ALU.mult) \
                    .then_inc(s_conv, 1)

            def residual(b, t):
                if t == 0:
                    dve.wait_ge(s_xr_in, b * 16 + 16)
                dve.wait_ge(s_att_ps, b * NT + t + 1)
                dve.tensor_tensor(xr[:, t, :], psum[:, 2 + t % 2, 0:D], xr[:, t, :], ALU.add).then_inc(s_x1, 1)

            def start(b, last=None):
                def take(q):
                    maximum(b, q)
                    if q == MU - 1:
                        split(b, 0)
                interleave(take, lambda t, steps: last is not None and "add" in steps and residual(last, t),
                           lambda: rows(b, 0))

            def batch(b, more):
                for e in range(NU * NT):
                    u, kc = e // NT, e % NT
                    for k in range(4):
                        q = AHEAD + 4 * e + k
                        if q < NU * MU:
                            maximum(b, q)
                            if q % MU == MU - 1:
                                split(b, q // MU)
                        if k == 1 and kc == 3 and u > 0:
                            normalise(b, u - 1)
                        if k == 1 and kc == 5 and u + 1 < NU:
                            rows(b, u + 1)
                    if more:
                        if 0 <= e - STATS < NT // 2:
                            for t in range(2):
                                statistics(b + 1, 2 * (e - STATS) + t)
                        if e == STATS + NT // 2:
                            moments(b + 1)
                        if 0 <= e - NEXT < 2:
                            for c in range(2):
                                take_hT(b + 1, 2 * (e - NEXT) + c)
                        if 2 <= e - NEXT < 2 + BLOCKS:
                            split_block(b + 1, e - NEXT - 2)
                normalise(b, NU - 1)
                if more:
                    logits(b + 1, True)
                for c in (1, 3):
                    dve.wait_ge(s_cvT_ps, b * 4 + c + 1)
                    dve.tensor_copy(cvT[:, c % 2, (c // 2) * HALF:(c // 2 + 1) * HALF], psum[:, CV_BANKS[c], :]) \
                        .then_inc(s_cvT[1], 1)
                if more:
                    gates(b + 1)
                    start(b + 1, last=b)
                else:
                    for t in range(NT):
                        residual(b, t)

            dve.wait_ge(s_mod_in, 16)
            dve.wait_ge(s_ln1, LN1_ALL)
            dve.tensor_tensor(hn[:], hn[:], modA[:, 1].unsqueeze(1).broadcast_to([P, NT, D]), ALU.mult).then_inc(s_hn, 1)
            dve.wait_ge(s_hn, 1)
            dve.tensor_tensor(hn[:], hn[:], modA[:, 0].unsqueeze(1).broadcast_to([P, NT, D]), ALU.add).then_inc(s_hn, 1)
            for c in range(4):
                take_hT(0, c)
            dve.wait_ge(s_set_out, 16 * (1 + LAYERS))
            for n in range(BLOCKS):
                split_block(0, n)
            logits(0, False)
            gates(0)
            start(0)
            with dve.Fori(0, B - 1) as b:
                batch(b, True)
            batch(B - 1, False)

            def ln0(w, s, t, it):
                x1 = xs[:, s, bass.ds(t, 1), :].rearrange("p o d -> p (o d)")
                dve.bn_stats(w["x1n"][:], x1).then_inc(w["s_ln0_ag"], 1)
                dve.wait_ge(w["s_ln0_ag"], it * 2 + 1)
                dve.nop(nofuse=True)
                dve.bn_aggr(w["mv0"][:], w["x1n"][:]).then_inc(w["s_ln0_ag"], 1)

            def ln0_end(w, s, t, it):
                x1 = xs[:, s, bass.ds(t, 1), :].rearrange("p o d -> p (o d)")
                dve.wait_ge(w["s_ln0_rs"], it * 2 + 2)
                dve.tensor_scalar(w["u0"][:], x1, w["mv0"][:, 0:1], w["rs0"][:], ALU.subtract, ALU.mult).then_inc(w["s_ln0"], 1)
                dve.wait_ge(w["s_ln0"], it * 3 + 1)
                dve.tensor_tensor(w["u0"][:], w["u0"][:], modF[:, s, 1], ALU.mult).then_inc(w["s_ln0"], 1)
                dve.wait_ge(w["s_ln0"], it * 3 + 2)
                dve.tensor_tensor(w["u0"][:], w["u0"][:], modF[:, s, 0], ALU.add).then_inc(w["s_ln0"], 1)

            def finish_layer(w, l, n):
                dve.wait_ge(w["s_w2_ps"], n + 1)
                dve.wait_ge(w["s_ub"], n + 1)
                dve.tensor_tensor(w["u"][:], psum[:, w["bk"], 0:D], w["u"][:], ALU.add).then_inc(w["s_u2"], 1)

            def finish(w, s, t, it):
                x1 = xs[:, s, bass.ds(t, 1), :].rearrange("p o d -> p (o d)")
                dve.wait_ge(w["s_u2"], it * 2 + 2)
                dve.wait_ge(w["s_out"], FREE + it * 16)
                dve.tensor_tensor(w["o"][:], w["u"][:], gateF[:, s], ALU.mult).then_inc(w["s_oo"], 1)
                dve.wait_ge(w["s_oo"], it * 2 + 1)
                dve.tensor_tensor(w["o"][:], w["o"][:], x1, ALU.add).then_inc(w["s_oo"], 1)

            def blk(name, w, l, t, it, prev=True):
                n, bk = it * 2 + l, w["bk"]
                flat = w["big"][:].rearrange("p h n -> p (h n)")
                if name == "F":
                    if prev:
                        finish_layer(w, 1 - l, n - 1)
                elif name == "U":
                    uT = w["uT"][:, l]
                    dve.wait_ge(w["s_uT_ps"], n + 1)
                    dve.tensor_copy(uT[:, P + 1:P + 2], zero[:, 0:1] if is_window(t, 0) else uT[:, 2 * P + 1:2 * P + 2]) \
                        .then_inc(w["s_carry"], 1)
                    dve.wait_ge(w["s_carry"], n + 1)
                    dve.tensor_copy(uT[:, 0:2 * (P + 2)].rearrange("p (a n) -> p a n", a=2)[:, :, 0:P],
                                    psum[:, bk, 0:D].rearrange("p (a n) -> p a n", a=2)).then_inc(w["s_uT"], 1)
                elif name == "A2":
                    sq = w["pT"][:].rearrange("p h k n -> p (h k n)")[:, 0:2 * INNER].rearrange("p (h d) -> p h d", d=LD)
                    qk = psum[:, bk:bk + 2, :].rearrange("p a (h d) -> p a h d", d=LD)
                    rot = flat[:, 0:2 * INNER].rearrange("p (a h d) -> p a h d", a=2, d=LD)
                    rs = flat[:, 2 * INNER:4 * INNER].rearrange("p (a h d) -> p a h d", a=2, d=LD)
                    dve.wait_ge(s_tab_in, it * 16 + 16)
                    dve.wait_ge(w["s_sq"], n + 1)
                    dve.tensor_reduce(w["ss"][:], sq, AX.X, ALU.add).then_inc(w["s_ssum"], 1)
                    dve.tensor_tensor(rot, qk, tab[:, l, 0:2].unsqueeze(2).broadcast_to([P, 2, LH, LD]), ALU.mult) \
                        .then_inc(w["s_rope"], 1)
                    hd = LD // 2
                    for lo, hi in ((0, hd), (hd, 0)):
                        ins = dve.tensor_tensor(rs[:, :, :, lo:lo + hd], qk[:, :, :, hi:hi + hd],
                                                tab[:, l, 2:4, lo:lo + hd].unsqueeze(2).broadcast_to([P, 2, LH, hd]), ALU.mult)
                    ins.then_inc(w["s_rope"], 1)
                    dve.wait_ge(w["s_rope"], n * 4 + 2)
                    for a in range(2):
                        dve.tensor_tensor(flat[:, a * INNER:(a + 1) * INNER], flat[:, a * INNER:(a + 1) * INNER],
                                          flat[:, (2 + a) * INNER:(3 + a) * INNER], ALU.add).then_inc(w["s_rope"], 1)
                    dve.wait_ge(w["s_rope"], n * 4 + 4)
                    dve.wait_ge(w["s_rn"], n * 4 + 2)
                    dve.tensor_tensor(rot[:, 1], rot[:, 1], w["rn"][:, LH:2 * LH].unsqueeze(2).broadcast_to([P, LH, LD]), ALU.mult) \
                        .then_inc(w["s_kn"], 1)
                elif name == "B1":
                    dve.wait_ge(w["s_qkT_ps"], n * 2 + 2)
                    dve.wait_ge(w["s_kvprev"], FREE + it * 4)
                    dve.tensor_copy(w["kT"][:, l, :, P:2 * P], psum[:, bk + 1, :].rearrange("p (m q) -> p m q", q=P)) \
                        .then_inc(w["s_kT"], 1)
                elif name in ("B2", "B2a", "B2b", "B2c"):
                    if name == "B2":
                        dve.wait_ge(w["s_mask_in"], it * 16 + 16)
                        dve.wait_ge(w["s_rn"], n * 4 + 4)
                    for h in {"B2": range(0, 2), "B2a": range(2, 4), "B2b": range(4, 6), "B2c": range(6, 8)}[name]:
                        if h % 2 == 0:
                            dve.wait_ge(w["s_s_ps"], n * (LH // 2) + h // 2 + 1)
                            dve.nop(nofuse=True)
                        ins = dve.tensor_tensor_reduce(out=w["big"][:, h, :],
                                                       in0=psum[:, bk + h // 2, (h % 2) * 2 * P:(h % 2 + 1) * 2 * P],
                                                       in1=w["mask"][:], scale=w["rn"][:, h:h + 1], scalar=-3.4e38,
                                                       op0=ALU.add, op1=ALU.max, accum_out=w["mx"][:, h:h + 1])
                    if name in ("B2a", "B2c"):
                        a = 0 if name == "B2a" else 4
                        ins.then_inc(w["s_sm"], 1)
                        dve.wait_ge(w["s_sm"], n * 4 + (a // 2 + 1))
                        dve.tensor_scalar(w["mx"][:, a:a + 4], w["mx"][:, a:a + 4], -1.0, None, ALU.mult).then_inc(w["s_sm"], 1)
                elif name == "B3":
                    for m in range(4):
                        dve.wait_ge(w["s_exp"], n * 4 + m + 1)
                        dve.reciprocal(w["rz"][:, 2 * m:2 * m + 2], w["z"][:, 2 * m:2 * m + 2]).then_inc(w["s_rz"], 1)
                        dve.wait_ge(w["s_rz"], n * 4 + m + 1)
                        for h in (2 * m, 2 * m + 1):
                            ins = dve.tensor_scalar(w["big"][:, h, :], w["big"][:, h, :], w["rz"][:, h:h + 1], None, ALU.mult)
                        ins.then_inc(w["s_pn"], 1)
                elif name == "C1":
                    dve.wait_ge(w["s_wo_ps"], n + 1)
                    dve.tensor_tensor(w["u"][:], psum[:, bk + 1, 0:D], (w["u0"] if l == 0 else w["u"])[:], ALU.add) \
                        .then_inc(w["s_u1"], 1)
                elif name == "C2":
                    dve.wait_ge(w["s_u1"], n + 1)
                    dve.bn_stats(w["st"][:, 0, :], w["u"][:, 0:P]).then_inc(w["s_ln_ag"], 1)
                    dve.wait_ge(w["s_sh_ps"], n + 1)
                    dve.tensor_copy(w["ush"][:], psum[:, bk + 2, 0:P]).then_inc(w["s_sh"], 1)
                    dve.wait_ge(w["s_sh"], n * 3 + 1)
                    dve.tensor_copy(w["ush"][0:1, :], w["crow"][:, l]).then_inc(w["s_sh"], 1)
                    dve.wait_ge(w["s_sh"], n * 3 + 2)
                    dve.tensor_copy(w["crow"][:, l], zero[0:1, :] if is_window(t, NT - 1) else psum[0:1, bk + 2, 0:P]) \
                        .then_inc(w["s_sh"], 1)
                    dve.bn_stats(w["st"][:, 1, :], w["ush"][:]).then_inc(w["s_ln_ag"], 1)
                    dve.wait_ge(w["s_ln_ag"], n * 3 + 2)
                    dve.nop(nofuse=True)
                    dve.bn_aggr(w["mv"][:], w["st"][:].rearrange("p a n -> p (a n)")).then_inc(w["s_ln_ag"], 1)
                elif name == "C3":
                    dve.wait_ge(w["s_ln_rs"], n * 2 + 2)
                    for k, src in ((0, w["u"][:, 0:P]), (1, w["ush"][:])):
                        dve.tensor_scalar(w["hl"][:, k * P:(k + 1) * P], src, w["mv"][:, 0:1], w["rs"][:], ALU.subtract, ALU.mult) \
                            .then_inc(w["s_hl"], 1)
                elif name == "D1":
                    dve.wait_ge(w["s_hl_ps"], n + 1)
                    for k in range(DC):
                        dve.tensor_scalar(w["hlT"][:, k, :], psum[:, bk, k * P:(k + 1) * P], lnv[:, l, 0, k:k + 1],
                                          lnv[:, l, 1, k:k + 1], ALU.mult, ALU.add).then_inc(w["s_hlT"], 1)
                elif name == "D2":
                    dve.wait_ge(w["s_hl"], n * 2 + 2)
                    dve.tensor_tensor(w["u"][:], w["u"][:], b2_sb[:, l], ALU.add).then_inc(w["s_ub"], 1)
                    gl = w["pT"][:].rearrange("p h k n -> p (h k) n")
                    dve.wait_ge(w["s_gelu"], n * FC + FC)
                    dve.wait_ge(w["s_g_ps"], n * 3 + 3)
                    for cc in range(FC):
                        rows, m = (P if cc < FC - 1 else FR), FC + cc
                        dve.scalar_tensor_tensor(out=gl[0:rows, cc, :],
                                                 in0=psum[0:rows, bk + 1 + m // 4, (m % 4) * P:(m % 4 + 1) * P],
                                                 scalar=b1_sb[0:rows, l, 0, cc:cc + 1], in1=gl[0:rows, cc, :],
                                                 op0=ALU.add, op1=ALU.mult).then_inc(w["s_act"], 1)

            def turn(l, t, it, prev=True, ahead=True):
                t_before = NT - 1 if is_window(t, 0) else t - 1
                before = (0, t, it) if l == 1 else (1, t_before, it - 1)
                t_next = 0 if is_window(t, NT - 1) else t + 1
                blk("F", X, l, t, it, prev)
                blk("U", X, l, t, it)
                if prev:
                    blk("B2b", Y, *before)
                    blk("B2c", Y, *before)
                    if l == 0:
                        finish(X, 0, t_before, it - 1)
                    blk("B3", Y, *before)
                blk("A2", X, l, t, it)
                if prev:
                    blk("C1", Y, *before)
                blk("B1", X, l, t, it)
                if prev:
                    blk("C2", Y, *before)
                blk("B2", X, l, t, it)
                if prev:
                    blk("C3", Y, *before)
                blk("B2a", X, l, t, it)
                if prev:
                    blk("D1", Y, *before)
                blk("B2b", X, l, t, it)
                blk("B2c", X, l, t, it)
                blk("B3", X, l, t, it)
                if prev:
                    blk("D2", Y, *before)
                if l == 1 and ahead:
                    for s in range(2):
                        ln0(S[s], s, t_next, it + 1)
                    ln0_end(X, 0, t_next, it + 1)
                blk("F", Y, l, t, it, prev)
                blk("U", Y, l, t, it)
                blk("C1", X, l, t, it)
                blk("C2", X, l, t, it)
                blk("C3", X, l, t, it)
                if l == 1 and ahead:
                    ln0_end(Y, 1, t_next, it + 1)
                blk("A2", Y, l, t, it)
                if prev and l == 0:
                    finish(Y, 1, t_before, it - 1)
                blk("B1", Y, l, t, it)
                blk("D2", X, l, t, it)
                blk("B2", Y, l, t, it)
                blk("B2a", Y, l, t, it)

            dve.wait_ge(s_wf, 16 * loads[1])
            dve.wait_ge(s_zero, 9)
            dve.wait_ge(s_xs0_in, 64)
            for s in range(2):
                ln0(S[s], s, 0, 0)
            for s in range(2):
                ln0_end(S[s], s, 0, 0)
            turn(0, 0, 0, prev=False)
            turn(1, 0, 0)
            dve.wait_ge(s_xs_in, 64)

            def window(i, t, it):
                ahead = not (is_window(t, NT - 1) and isinstance(i, int))
                turn(0, t, it)
                if is_window(t, NT - 1) and ahead:
                    dve.wait_ge(s_xs0_in, i * 64 + 128)
                turn(1, t, it, ahead=ahead)
                if is_window(t, 0):
                    dve.wait_ge(s_xs_in, i * 64 + 64)
            windows(dve, window)
            t, last = NT - 1, PAIRS * NT - 1
            finish_layer(X, 1, last * 2 + 1)
            for name in ("B2b", "B2c"):
                blk(name, Y, 1, t, last)
            finish(X, 0, t, last)
            for name in ("B3", "C1", "C2", "C3", "D1", "D2"):
                blk(name, Y, 1, t, last)
            finish_layer(Y, 1, last * 2 + 1)
            finish(Y, 1, t, last)

        @block.gpsimd
        def _(gp):
            for s in (s_x1, *s_parts_out, *s_m_in, *(w[n] for w in S for n in ("s_out", "s_kvprev"))):
                gp.sem_inc(s, FREE)
            gp.memset(ident[:], 0.0).then_inc(s_id, 1)
            gp.wait_ge(s_id, 1)
            gp.nop(nofuse=True)
            gp.affine_select(out=ident[:], in_=ident[:], compare_op=ALU.not_equal, fill=1.0, base=0,
                             pattern=[[-1, P]], channel_multiplier=1).then_inc(s_id, 1)
            gp.wait_ge(s_id, 2)
            gp.nop(nofuse=True)
            gp.tensor_copy(identb[:], ident[:]).then_inc(s_id, 1)
            gp.memset(turned[:], 0.0).then_inc(s_id, 1)
            for n, base in enumerate((1, 1 - P)):
                gp.wait_ge(s_id, 4 + n)
                gp.nop(nofuse=True)
                gp.affine_select(out=turned[:], in_=turned[:], compare_op=ALU.not_equal, fill=1.0, base=base,
                                 pattern=[[-1, P]], channel_multiplier=1).then_inc(s_id, 1)
            gp.memset(neghalf[:], -0.5).then_inc(s_id, 1)
            gp.wait_ge(s_id, ID_ALL)
            gp.nop(nofuse=True)
            def norm(b):
                c0 = b * LN1_ALL
                gp.wait_ge(s_stats1, b * (2 * NT) + 2 * NT)
                gp.nop(nofuse=True)
                gp.tensor_scalar(rs1[:], mv1[:, :, 1], LN_EPS, 1.0, ALU.add, ALU.mult).then_inc(s_ln1, 1)
                gp.wait_ge(s_ln1, c0 + 1)
                gp.nop(nofuse=True)
                gp.tensor_tensor(rs1[:], rs1[:], neghalf[:, 0:NT], ALU.pow).then_inc(s_ln1, 1)
                gp.wait_ge(s_ln1, c0 + 2)
                gp.nop(nofuse=True)
                for t in range(NT):
                    gp.tensor_scalar(hn[:, t, :], hn[:, t, :], mv1[:, t, 0:1], rs1[:, t:t + 1], ALU.subtract, ALU.mult) \
                        .then_inc(s_ln1, 1)

            norm(0)
            gp.wait_ge(s_set_dve, SET_ALL)
            gp.wait_ge(s_set_out, 16 * (1 + LAYERS))

            gp.wait_ge(s_ln1, LN1_ALL)
            gp.nop(nofuse=True)
            gp.memset(stack[KS:KS + PART, :, 1], -1.0).then_inc(s_ones, 1)
            gp.wait_ge(s_ones, 1)
            gp.nop(nofuse=True)
            gp.memset(vg[:, :, :, :, DH:VW], 0.0).then_inc(s_ones, 1)
            gp.wait_ge(s_ones, 2)
            gp.nop(nofuse=True)
            gp.memset(vg[:, :, :, :, DH + 1:DH + 2], 1.0).then_inc(s_ones, 1)
            gp.wait_ge(s_ones, 3)
            gp.nop(nofuse=True)

            def modulate(b):
                gp.wait_ge(s_mod_in, b * 16 + 16)
                gp.wait_ge(s_ln1, b * LN1_ALL + LN1_ALL)
                gp.nop(nofuse=True)
                gp.tensor_tensor(hn[:], hn[:], modA[:, 1].unsqueeze(1).broadcast_to([P, NT, D]), ALU.mult).then_inc(s_hn, 1)
                gp.wait_ge(s_hn, b * 2 + 1)
                gp.nop(nofuse=True)
                gp.tensor_tensor(hn[:], hn[:], modA[:, 0].unsqueeze(1).broadcast_to([P, NT, D]), ALU.add).then_inc(s_hn, 1)

            def values(b, g):
                if g == 0:
                    gp.wait_ge(s_gate, b * 3 + 3)
                    gp.wait_ge(s_v, b * NT + NT)
                    gp.nop(nofuse=True)
                if g > 1:
                    gp.wait_ge(s_pv, b * (NU * NT) + (g - 1) * 16)
                    gp.nop(nofuse=True)
                e = zt[:, :, G * g:G * (g + 1)]
                gp.tensor_tensor(vg[:, g % 2, :, :, 0:DH], vt[:, :, G * DH * g:G * DH * (g + 1)].rearrange("p t (h i) -> p t h i", i=DH),
                                 e.unsqueeze(3).broadcast_to([P, NT, G, DH]), ALU.mult).then_inc(s_vg, 1)
                gp.tensor_copy(vg[:, g % 2, :, :, DH], e).then_inc(s_vg, 1)

            def batch(b, more):
                values(b, 0)
                values(b, 1)
                gp.wait_ge(s_x1, FREE + b * NT)
                gp.nop(nofuse=True)
                gp.tensor_tensor(wga[:], wfold[:], modA[:, 2].unsqueeze(1).broadcast_to([P, DC, D]), ALU.mult).then_inc(s_wga, 1)
                values(b, 2)
                values(b, 3)
                if more:
                    norm(b + 1)
                    modulate(b + 1)
            with gp.Fori(0, B - 1) as b:
                batch(b, True)
            batch(B - 1, False)

            def ln0(w, it):
                gp.wait_ge(w["s_ln0_ag"], it * 2 + 2)
                gp.nop(nofuse=True)
                gp.tensor_scalar(w["rs0"][:], w["mv0"][:, 1:2], LN_EPS, 1.0, ALU.add, ALU.mult).then_inc(w["s_ln0_rs"], 1)
                gp.wait_ge(w["s_ln0_rs"], it * 2 + 1)
                gp.nop(nofuse=True)
                gp.tensor_tensor(w["rs0"][:], w["rs0"][:], neghalf[:, 0:1], ALU.pow).then_inc(w["s_ln0_rs"], 1)

            def blk(name, w, l, t, it):
                n = it * 2 + l
                if name == "A":
                    gp.wait_ge(w["s_ssum"], n + 1)
                    gp.nop(nofuse=True)
                    gp.tensor_scalar(w["ss"][:], w["ss"][:], 1e-24, None, ALU.max).then_inc(w["s_rn"], 1)
                    for half_h in (slice(LH, 2 * LH), slice(0, LH)):
                        gp.wait_ge(w["s_rn"], n * 4 + 1)
                        gp.nop(nofuse=True)
                        gp.tensor_tensor(w["rn"][:, half_h], w["ss"][:, half_h], neghalf[:, 0:LH], ALU.pow).then_inc(w["s_rn"], 1)
                    gp.wait_ge(w["s_rn"], n * 4 + 3)
                    gp.nop(nofuse=True)
                    gp.tensor_scalar(w["rn"][:, 0:LH], w["rn"][:, 0:LH], 8.0, 1.0, ALU.mult, ALU.mult).then_inc(w["s_rn"], 1)
                elif name == "C":
                    gp.wait_ge(w["s_o_ps"], n + 1)
                    gp.nop(nofuse=True)
                    if is_window(t, NT - 1):
                        gp.memset(w["v"][:, l, 0, :], 0.0).then_inc(w["s_kvprev"], 1)
                        gp.memset(w["kT"][:, l, :, 0:P], 0.0).then_inc(w["s_kvprev"], 1)
                        return
                    gp.tensor_copy(w["v"][:, l, 0, :], w["v"][:, l, 1, :]).then_inc(w["s_kvprev"], 1)
                    gp.tensor_copy(w["kT"][:, l, :, 0:P], w["kT"][:, l, :, P:2 * P]).then_inc(w["s_kvprev"], 1)
                elif name == "D":
                    gp.wait_ge(w["s_ln_ag"], n * 3 + 3)
                    gp.nop(nofuse=True)
                    gp.tensor_scalar(w["rs"][:], w["mv"][:, 1:2], LN_EPS, 1.0, ALU.add, ALU.mult).then_inc(w["s_ln_rs"], 1)
                    gp.wait_ge(w["s_ln_rs"], n * 2 + 1)
                    gp.nop(nofuse=True)
                    gp.tensor_tensor(w["rs"][:], w["rs"][:], neghalf[:, 0:1], ALU.pow).then_inc(w["s_ln_rs"], 1)

            def turn(l, t, it, prev=True, ahead=True):
                before = (0, t, it) if l == 1 else (1, NT - 1 if is_window(t, 0) else t - 1, it - 1)
                blk("A", X, l, t, it)
                if prev:
                    blk("D", Y, *before)
                    blk("C", Y, *before)
                if l == 1 and ahead:
                    for w in S:
                        ln0(w, it + 1)
                blk("D", X, l, t, it)
                blk("A", Y, l, t, it)
                blk("C", X, l, t, it)

            gp.wait_ge(s_x1_out, B * 16)
            gp.nop(nofuse=True)
            zeros = [w["qz"][:] for w in S] + [zero[:]] + [z for w in S for z in (w["kT"][:, :, :, 0:P], w["v"][:, :, 0, :], w["crow"][:])]
            for n, buf in enumerate(zeros):
                gp.memset(buf, 0.0).then_inc(s_zero, 1)
                gp.wait_ge(s_zero, n + 1)
                gp.nop(nofuse=True)
            for w in S:
                ln0(w, 0)
            turn(0, 0, 0, prev=False)
            turn(1, 0, 0)

            def window(i, t, it):
                turn(0, t, it)
                turn(1, t, it, ahead=not (is_window(t, NT - 1) and isinstance(i, int)))
            windows(gp, window)
            for name in "DC":
                blk(name, Y, 1, NT - 1, PAIRS * NT - 1)


def _constants():
    n = np.float32
    half = np.arange(0, LD, 2, dtype=n)
    inv = (n(1.0) / n(10000.0) ** (half / n(LD))).astype(n)
    t = np.arange(T, dtype=n)
    fr = t[:, None] * inv[None, :]
    fr = np.concatenate([fr, fr], -1)
    base = (half + n(0.4 * LD)) / n(1.4 * LD)
    scale = base[None, :] ** ((t - T // 2) / n(P // 2))[:, None]
    scale = np.concatenate([scale, scale], -1).astype(n)
    cos, sin = np.cos(fr.astype(np.float64)), np.sin(fr.astype(np.float64))
    sign = np.concatenate([-np.ones(LD // 2), np.ones(LD // 2)])
    rope = np.stack([cos * scale, cos / scale, sign * sin * scale, sign * sin / scale], 1).astype(n)
    rope = np.ascontiguousarray(rope.reshape(NT, P, 4, LD).transpose(1, 0, 2, 3))
    q, k = np.arange(P)[:, None], np.arange(2 * P)[None, :] - P
    keep = (k <= q) & (k >= q - P)
    mask = np.stack([keep & ((k >= 0) | (w > 0)) for w in range(NT)])
    return rope, np.where(mask, 0.0, MASKED).astype(n)


def kernel(**inputs):
    import concourse.bacc as _bacc
    from concourse.bass_utils import run_bass_kernel_spmd as _run

    a = {k: np.ascontiguousarray(v) for k, v in inputs.items()}
    rope, mask = _constants()
    wout = a["L0_attn_Wout"]
    heads = np.stack([a["L0_attn_" + k] for k in ("beta_p", "iv_p", "ov_p", "chi")])
    heads = np.repeat(heads, DH, axis=1).reshape(4, DC, P).transpose(2, 0, 1)
    sgn = np.where(np.arange(D) % DH < DH // 2, 1.0, -1.0).astype(np.float32).reshape(DC, P).T
    swapped = wout.reshape(H, 2, DH // 2, D)[:, ::-1].reshape(D, D)
    arrays = {
        "x": a["L0_attn_x"], "Wa": a["L0_attn_Wa"], "ba": a["L0_attn_ba"], "We": a["L0_attn_We"], "be": a["L0_attn_be"],
        "Wi": a["L0_attn_Wi"], "Wo": a["L0_attn_Wo"], "Wv": a["L0_attn_Wv"], "Wout": wout, "Wout_sw": swapped,
        "head_vec": heads, "sgn": sgn, "wqkv": a["L0_ffn_wqkv"], "q_scale": a["L0_ffn_q_scale"],
        "k_scale": a["L0_ffn_k_scale"], "wo": a["L0_ffn_wo"], "ln_g": a["L0_ffn_ln_g"], "ln_b": a["L0_ffn_ln_b"],
        "w1": a["L0_ffn_w1"], "b1": a["L0_ffn_b1"], "w2": a["L0_ffn_w2"], "b2": a["L0_ffn_b2"], "c": a["L0_c"],
        "wmod": a["L0_wmod"], "rope": rope, "mask": mask,
    }
    arrays = {k: np.ascontiguousarray(v) for k, v in arrays.items()}
    nc = _bacc.Bacc("TRN2", target_bir_lowering=False, num_devices=1)
    aps = {k: nc.dram_tensor("in_" + k, v.shape, mybir.dt.from_np(v.dtype), kind="ExternalInput").ap()
           for k, v in arrays.items()}
    aps["out"] = nc.dram_tensor("out_x", (B, T, D), F32, kind="ExternalOutput").ap()
    build(nc, **aps)
    r = _run(nc, [{"in_" + k: v for k, v in arrays.items()}], core_ids=[0])
    return r.results[0]["out_x"]
```
